# Optimizing a Trainium2 kernel written in Bass

```python
import numpy as np
import jax
import jax.numpy as jnp

def _softmax(x, axis=-1):
    return jax.nn.softmax(x, axis=axis)
def _gelu(x):
    return jax.nn.gelu(x, approximate=True)
def _silu(x):
    return jax.nn.silu(x)
def _sigmoid(x):
    return jax.nn.sigmoid(x)
def _layernorm(x, axis=-1, eps=1e-5):
    m = jnp.mean(x, axis=axis, keepdims=True)
    v = jnp.var(x, axis=axis, keepdims=True)
    return (x - m) / jnp.sqrt(v + eps)
def _scatter_add(tgt, idx, src, axis=0):
    return tgt.at[idx].add(src)
def _segment_sum(src, seg, n):
    return jax.ops.segment_sum(src, seg, n)

kernel_name = 'mk_metaformer_d2_conv_nhwc384_955a3a'

def setup_inputs(seed: int = 0):
    np.random.seed(seed)
    _w = jnp.asarray
    def _rec_inputs():
        import jax
        import jax.numpy as jnp
        _gk = jax.random.key(seed)
        x = -0.001003 + 1 * jax.random.normal(jax.random.fold_in(_gk, 1), (4, 32, 32, 384), jnp.float32)
        return x
    x = _rec_inputs()
    def _L0_conv_setup():
        import jax, jax.numpy as jnp
        import numpy as np
        NUM_HEADS = 12
        HEAD_DIM = 32
        GP_NUM = 20
        key = jax.random.key(seed)
        k1, k2, k3, k4 = jax.random.split(key, 4)
        B, H, W, C = (4, 32, 32, 384)
        att = NUM_HEADS * HEAD_DIM
        x = jax.random.normal(k1, (B, H, W, C), dtype=jnp.float32)
        W_qkv = jax.random.normal(k2, (3 * att, C), dtype=jnp.float32) * C ** (-0.5)
        W_proj = jax.random.normal(k3, (C, att), dtype=jnp.float32) * att ** (-0.5)
        W_gp = jax.random.normal(k4, (GP_NUM, C), dtype=jnp.float32) * C ** (-0.5)
        return {'x': x, 'W_qkv': W_qkv, 'W_proj': W_proj, 'W_gp': W_gp}
    _L0_conv_all = _L0_conv_setup()
    _L0_conv_in = {k: v for k, v in _L0_conv_all.items() if k in ('W_qkv', 'W_proj', 'W_gp', )}
    del _L0_conv_all

    def _L0_ffn_setup():
        import jax, jax.numpy as jnp
        import numpy as np
        D_MODEL = 384
        D_FF = 1536
        key = jax.random.key(seed)
        k_x, k1, k2, k3, k4 = jax.random.split(key, 5)
        std = 0.02
        return {'x': jax.random.normal(k_x, (16, 2048, D_MODEL), dtype=jnp.float32), 'c_fc_1': std * jax.random.normal(k1, (1536, 32), dtype=jnp.float32), 'c_fc_2': std * jax.random.normal(k2, (1, 12), dtype=jnp.float32), 'c_proj_1': std * jax.random.normal(k3, (32, 1536), dtype=jnp.float32), 'c_proj_2': std * jax.random.normal(k4, (12, 1), dtype=jnp.float32)}
    _L0_ffn_all = _L0_ffn_setup()
    _L0_ffn_in = {k: v for k, v in _L0_ffn_all.items() if k in ('c_fc_1', 'c_fc_2', 'c_proj_1', 'c_proj_2', )}
    del _L0_ffn_all

    def _L1_conv_setup():
        import jax, jax.numpy as jnp
        import numpy as np
        WINDOW = (1, 5, 20)
        FILL = 1.0

        def box_sum(x, axis, w):
            if w == 1:
                return x
            lo = w // 2
            hi = w - lo - 1
            xm = jnp.moveaxis(x, axis, -1)
            shp = xm.shape
            xr = xm.reshape(-1, 1, shp[-1])
            k = jnp.ones((1, 1, w), x.dtype)
            y = jax.lax.conv_general_dilated(xr, k, window_strides=(1,), padding=[(lo, hi)])
            return jnp.moveaxis(y.reshape(shp), -1, axis)
        key = jax.random.key(seed)
        x = jax.random.normal(key, (2, 256, 256, 384), dtype=jnp.float32)
        return {'x': x}
    _L1_conv_all = _L1_conv_setup()
    _L1_conv_in = {k: v for k, v in _L1_conv_all.items() if k in ()}
    del _L1_conv_all

    def _L1_ffn_setup():
        import jax, jax.numpy as jnp
        import numpy as np
        NUM_EXPERTS = 4
        TOP_K = 2
        DIM = 384
        HID = 4 * DIM
        key = jax.random.key(seed)
        ks = jax.random.split(key, 5)
        B, S = (16, 2048)
        scale_in = 1.0 / np.sqrt(DIM)
        scale_hid = 1.0 / np.sqrt(HID)
        return {'x': jax.random.normal(ks[0], (B, S, DIM), dtype=jnp.float32), 'gate_w': jax.random.normal(ks[1], (DIM, NUM_EXPERTS), dtype=jnp.float32) * scale_in, 'gate_b': jnp.zeros((NUM_EXPERTS,), dtype=jnp.float32), 'w1': jax.random.normal(ks[2], (NUM_EXPERTS, DIM, HID), dtype=jnp.float32) * scale_in, 'b1': jnp.zeros((NUM_EXPERTS, HID), dtype=jnp.float32), 'w2': jax.random.normal(ks[3], (NUM_EXPERTS, HID, DIM), dtype=jnp.float32) * scale_hid, 'b2': jnp.zeros((NUM_EXPERTS, DIM), dtype=jnp.float32)}
    _L1_ffn_all = _L1_ffn_setup()
    _L1_ffn_in = {k: v for k, v in _L1_ffn_all.items() if k in ('gate_w', 'gate_b', 'w1', 'b1', 'w2', 'b2', )}
    del _L1_ffn_all

    return {
        "x": x,
        "L0_conv_W_qkv": _L0_conv_in["W_qkv"],
        "L0_conv_W_proj": _L0_conv_in["W_proj"],
        "L0_conv_W_gp": _L0_conv_in["W_gp"],
        "L0_ffn_c_fc_1": _L0_ffn_in["c_fc_1"],
        "L0_ffn_c_fc_2": _L0_ffn_in["c_fc_2"],
        "L0_ffn_c_proj_1": _L0_ffn_in["c_proj_1"],
        "L0_ffn_c_proj_2": _L0_ffn_in["c_proj_2"],
        "L1_ffn_gate_w": _L1_ffn_in["gate_w"],
        "L1_ffn_gate_b": _L1_ffn_in["gate_b"],
        "L1_ffn_w1": _L1_ffn_in["w1"],
        "L1_ffn_b1": _L1_ffn_in["b1"],
        "L1_ffn_w2": _L1_ffn_in["w2"],
        "L1_ffn_b2": _L1_ffn_in["b2"],
    }

def reference(x, L0_conv_W_qkv, L0_conv_W_proj, L0_conv_W_gp, L0_ffn_c_fc_1, L0_ffn_c_fc_2, L0_ffn_c_proj_1, L0_ffn_c_proj_2, L1_ffn_gate_w, L1_ffn_gate_b, L1_ffn_w1, L1_ffn_b1, L1_ffn_w2, L1_ffn_b2):
    import jax
    import jax.numpy as jnp
    def _L0_conv_ref(x, W_qkv, W_proj, W_gp):
        import jax, jax.numpy as jnp
        import numpy as np
        NUM_HEADS = 12
        HEAD_DIM = 32
        GP_NUM = 20
        B, H, W_, C = x.shape
        N = H * W_
        h, d = (NUM_HEADS, HEAD_DIM)
        scale = d ** (-0.5)
        qkv = x.reshape(B, N, C) @ W_qkv.T
        q, k, v = jnp.split(qkv, 3, axis=-1)
        q = q.reshape(B, N, h, d).transpose(0, 2, 1, 3)
        k = k.reshape(B, N, h, d).transpose(0, 2, 1, 3)
        v = v.reshape(B, N, h, d).transpose(0, 2, 1, 3)
        attn = jax.nn.softmax(jnp.einsum('bhnd,bhmd->bhnm', q, k) * scale, axis=-1)
        q_all = q.transpose(0, 2, 1, 3).reshape(B, N, h * d)
        gw = q_all @ W_gp.T
        oh = jax.nn.one_hot(jnp.argmax(gw, axis=-1), GP_NUM, dtype=attn.dtype)
        G = jnp.einsum('bng,bmg->bnm', oh, oh)
        Gh = jnp.concatenate([jnp.broadcast_to(G[:, None], (B, h // 2, N, N)), jnp.broadcast_to(1.0 - G[:, None], (B, h // 2, N, N))], axis=1)
        attn = attn * Gh
        attn = attn / (attn.sum(axis=2, keepdims=True) + 1e-08)
        out = jnp.einsum('bhnm,bhmd->bhnd', attn, v)
        out = out.transpose(0, 2, 1, 3).reshape(B, H, W_, h * d)
        return out @ W_proj.T

    def _L0_ffn_ref(x, c_fc_1, c_fc_2, c_proj_1, c_proj_2):
        import jax, jax.numpy as jnp
        import numpy as np
        D_MODEL = 384
        D_FF = 1536
        w_fc = jnp.kron(c_fc_1, c_fc_2)
        w_proj = jnp.kron(c_proj_1, c_proj_2)
        h = x @ w_fc.T
        h = jax.nn.gelu(h, approximate=False)
        out = h @ w_proj.T
        return out

    def _L1_conv_ref(x):
        import jax, jax.numpy as jnp
        import numpy as np
        WINDOW = (1, 5, 20)
        FILL = 1.0

        def box_sum(x, axis, w):
            if w == 1:
                return x
            lo = w // 2
            hi = w - lo - 1
            xm = jnp.moveaxis(x, axis, -1)
            shp = xm.shape
            xr = xm.reshape(-1, 1, shp[-1])
            k = jnp.ones((1, 1, w), x.dtype)
            y = jax.lax.conv_general_dilated(xr, k, window_strides=(1,), padding=[(lo, hi)])
            return jnp.moveaxis(y.reshape(shp), -1, axis)
        w0, w1, w2 = WINDOW
        s = box_sum(box_sum(x, 1, w0), 2, w1)
        num = box_sum(s * s, 3, w2)
        d = box_sum(box_sum(box_sum(x * x, 1, w0), 2, w1), 3, w2)
        c0 = box_sum(jnp.ones((x.shape[1],), x.dtype), 0, w0)
        c1 = box_sum(jnp.ones((x.shape[2],), x.dtype), 0, w1)
        norm = c0[:, None] * c1[None, :]
        denum = d * norm[None, :, :, None]
        return jnp.nan_to_num(num / denum, nan=FILL)

    def _L1_ffn_ref(x, gate_w, gate_b, w1, b1, w2, b2):
        import jax, jax.numpy as jnp
        import numpy as np
        NUM_EXPERTS = 4
        TOP_K = 2
        DIM = 384
        HID = 4 * DIM
        scores = jnp.einsum('bsd,de->bse', x, gate_w) + gate_b
        probs = jax.nn.softmax(scores, axis=-1)
        topk_vals, topk_idx = jax.lax.top_k(probs, TOP_K)
        mask = jnp.sum(jax.nn.one_hot(topk_idx, NUM_EXPERTS, dtype=probs.dtype), axis=-2)
        masked = probs * mask
        masked = masked / (jnp.sum(masked, axis=-1, keepdims=True) + 1e-09)
        h = jax.nn.gelu(jnp.einsum('bsd,edh->ebsh', x, w1) + b1[:, None, None, :], approximate=False)
        y = jnp.einsum('ebsh,ehd->ebsd', h, w2) + b2[:, None, None, :]
        out = jnp.einsum('bse,ebsd->bsd', masked, y)
        return out

    def _gn(v, G=32, eps=1e-5):
        B_, H_, W_, C_ = v.shape
        g = v.reshape(B_, H_, W_, G, C_ // G)
        m = jnp.mean(g, axis=(1, 2, 4), keepdims=True)
        s = jnp.var(g, axis=(1, 2, 4), keepdims=True)
        return ((g - m) / jnp.sqrt(s + eps)).reshape(v.shape)

    def _ln_c(v, eps=1e-6):
        m = jnp.mean(v, axis=-1, keepdims=True)
        s = jnp.var(v, axis=-1, keepdims=True)
        return (v - m) / jnp.sqrt(s + eps)

    def _ln_t(v, eps=1e-5):
        m = jnp.mean(v, axis=-1, keepdims=True)
        s = jnp.var(v, axis=-1, keepdims=True)
        return (v - m) / jnp.sqrt(s + eps)

    def _to_tokens(v):
        B_, H_, W_, C_ = v.shape
        return v.reshape(B_, H_ * W_, C_)
    def _from_tokens(t, like):
        return t.reshape(like.shape)

    x = x + _L0_conv_ref(_ln_c(x), L0_conv_W_qkv, L0_conv_W_proj, L0_conv_W_gp)
    t = _to_tokens(x)
    t = t + _L0_ffn_ref(_ln_t(t), L0_ffn_c_fc_1, L0_ffn_c_fc_2, L0_ffn_c_proj_1, L0_ffn_c_proj_2)
    x = _from_tokens(t, x)
    x = x + _L1_conv_ref(_ln_c(x))
    t = _to_tokens(x)
    t = t + _L1_ffn_ref(_ln_t(t), L1_ffn_gate_w, L1_ffn_gate_b, L1_ffn_w1, L1_ffn_b1, L1_ffn_w2, L1_ffn_b2)
    x = _from_tokens(t, x)
    return x


_drawn_inputs = setup_inputs


def setup_inputs(seed=0):
    import zlib

    import numpy as np

    out = dict(_drawn_inputs(seed))
    spreads = {'L1_ffn_gate_b': (0.0, 0.1), 'L1_ffn_b1': (0.0, 0.1), 'L1_ffn_b2': (0.0, 0.1)}
    factors = {'L0_ffn_c_fc_1': 8.0, 'L0_ffn_c_fc_2': 8.0, 'L0_ffn_c_proj_1': 8.0, 'L0_ffn_c_proj_2': 8.0}
    for name, (base, spread) in spreads.items():
        noise = np.random.default_rng([zlib.crc32(name.encode()), seed]).standard_normal(out[name].shape)
        drawn = base * np.exp(spread * noise) if base else spread * noise
        out[name] = jnp.asarray(drawn.astype(out[name].dtype))
    for name, factor in factors.items():
        out[name] = (out[name] * factor).astype(out[name].dtype)
    return out
```

```python
from contextlib import ExitStack

import concourse.bass as bass
from concourse import mybir

F32 = mybir.dt.float32
F16 = mybir.dt.float16
I32 = mybir.dt.int32
U32 = mybir.dt.uint32
ACT = mybir.ActivationFunctionType
ALU = mybir.AluOpType
AX = mybir.AxisListType

P = 128
B, HT, WD, C = 4, 32, 32, 384
N = HT * WD
TOK = B * N
NT = N // P
CC = C // P
NH, HD = 12, 32
NG = 20
OHW = 68
FFN = 1536
FO = FFN // P
KI, KJ = 32, 12
NE = 4
W1, W2 = 5, 20
PADL = W2 // 2
CP = C + W2
BIG = 30000.0
ACT_SET_EXP_LN = 6

SX = 2.0 ** 11
SW = 2.0 ** 10
SATT = 2.0
SZ = 2.0 ** 8
SC1 = 2.0 ** 8
QSCALE = -(HD ** -0.5)

RING = 6
N_T, N_QK, N_V = 2 * CC, 12, NT
OFF_QK = N_T
OFF_V = OFF_QK + N_QK
OFF_G = OFF_V + N_V
OFF_O = OFF_G + 1
SEC1 = OFF_O + 1
OFF_PJ = SEC1
OFF_Z = OFF_PJ + NT
OFF_T3 = OFF_Z + 1
OFF_SC = OFF_T3 + N_T
NRING = OFF_SC + 1
LAG = 2
FLT_MAX = 3.4028234663852886e38

NCST = 12
NW_LOADS = 10
NHI = 2 * N_T + N_QK
NA = 4
NVA = 24
NV = 291
SH = 2.0 ** 8
TT = 256
ET = TOK // TT
WCH = CC
CHW = C * FFN // P // WCH
NPW = 2


def hi_count(n):
    if n < OFF_V:
        return n + 1
    return OFF_V + n - OFF_T3 + 1



class Chain:

    def __init__(self, eng, sem):
        self.eng, self.sem, self.base, self.n = eng, sem, 0, 0

    def mark(self, ins):
        ins.then_inc(self.sem, 1)
        self.n += 1
        return self.base + self.n

    def wait(self, value):
        self.eng.wait_ge(self.sem, value)

    def step(self, ins):
        self.wait(self.mark(ins))

    def enter(self, i, each):
        saved = (self.base, self.n, each)
        self.base, self.n = self.base + self.n + i * each, 0
        return saved

    def leave(self, saved, rounds):
        base, n, each = saved
        assert self.n == each, (self.n, each)
        self.base, self.n = base, n + rounds * each


def build(nc, x, W_qkv, W_proj, W_gp, c_fc_1, c_fc_2, c_proj_1, c_proj_2,
          gate_w, gate_b, w1, b1, w2, b2, out):
    x_tok = x.rearrange("b h w c -> (b h w) c")
    x_v = x_tok.rearrange("(b t p) c -> b p t c", p=P, t=NT)
    out_tok = out.rearrange("b h w c -> (b h w) c")

    with ExitStack() as ctx:
        layers = ExitStack()

        def sb(name, shape, dt, stack=None):
            return (stack or layers).enter_context(nc.sbuf_tensor(name, shape, dt))

        def sem(name):
            return ctx.enter_context(nc.semaphore(name))

        def dram(name, shape, dt):
            return nc.dram_tensor(name, shape, dt, kind="Internal").ap()

        qk_d = dram("qk_d", (2, NH, 3, HD, N), F16)
        oh_d = dram("oh_d", (3 * NG, N), F16)
        x3_d = dram("x3_d", (TOK + P, C), F32)
        att_d = dram("att_d", (NH, HD, N), F32)
        t16_d = dram("t16_d", (TOK, 2 * C), F16)
        w16_d = dram("w16_d", (2, 2, NE, WCH, P, CHW), F16)

        ident16 = sb("ident16", [P, P], F16, ctx)
        desc = sb("desc", [P, NG], F32, ctx)
        b1T = sb("b1T", [P, NE * FO], F32, ctx)
        scores = sb("scores", [P, B * NT, NE], F32, ctx)
        gates = sb("gates", [P, B * NT, NE], F32, ctx)
        oh1 = sb("oh1", [P, B * NT, NE], F32, ctx)
        oh2 = sb("oh2", [P, B * NT, NE], F32, ctx)
        pr2 = sb("pr2", [P, B * NT, NE], F32, ctx)
        red = sb("red", [P, B * NT], F32, ctx)
        ident = sb("ident", [P, P], F32)
        band = sb("band", [P, P], F32)
        cnt = sb("cnt", [P, 1], F32)
        wqT = [sb(f"wqT{i}", [P, CC, 3 * C], F16) for i in range(2)]
        wpT = [sb(f"wpT{i}", [P, CC, C], F16) for i in range(2)]
        gpT = [sb(f"gpT{i}", [P, CC, NG], F16) for i in range(2)]
        gw16 = [sb(f"gw16_{i}", [P, CC, NE], F16) for i in range(2)]
        c1s = sb("c1s", [3 * KI, FFN], F16)
        cp1T = sb("cp1T", [P, FO, KI], F32)
        c2b = sb("c2b", [P, KJ], F32)
        cp2b = sb("cp2b", [P, KJ], F32)
        gbb = sb("gbb", [P, NE], F32)
        gwn = sb("gwn", [P, CC, NE], F32)
        xb = sb("xb", [P, NT, C], F32)
        xn = sb("xn", [P, NT, C], F32)
        at = sb("at", [P, NT, C], F32)
        xT = [sb(f"xT{i}", [P, CC, N], F16) for i in range(2)]
        stg = [sb(f"stg{i}", [P, 6, N], F16) for i in range(2)]
        va = sb("va", [P, NT, C], F32)
        qs = [sb(f"qs{i}", [P, N], F16) for i in range(2)]
        ks = [sb(f"ks{i}", [P, N], F16) for i in range(2)]
        E = sb("E", [P, NT, N], F32)
        oT = [sb(f"oT{i}", [P, N // 4], F32) for i in range(2)]
        vp = sb("vp", [P, NT, HD], F32)
        t16 = sb("t16", [P, NT, 2 * C], F16)
        ohn = sb("ohn", [P, NT, OHW], F16)
        ohT = sb("ohT", [OHW, N], F16)
        znat = sb("znat", [P, NT, 3 * KI], F16)
        zT = sb("zT", [3 * KI, N], F16)
        st6 = sb("st6", [P, NT, 6], F32)
        mv = sb("mv", [P, NT, 2], F32)
        ve = sb("ve", [P, NT], F32)
        lnv = sb("lnv", [P, NT], F32)
        y0 = sb("y0", [P, NT], F32)
        nt1 = sb("nt1", [P, NT], F32)
        rs = sb("rs", [P, NT], F32)
        gws = sb("gws", [P, NT, NG], F32)
        gwe = sb("gwe", [P, NT, NG], F32)
        gm = sb("gm", [P, NT], F32)
        zz = sb("zz", [P, NT, KI], F32)
        zs = sb("zs", [P, NT, KI], F32)
        mn = [sb(f"mn{i}", [P, NT], F32) for i in range(2)]
        rsum = [sb(f"rsum{i}", [P, NT], F32) for i in range(2)]
        lnr = [sb(f"lnr{i}", [P, NT], F32) for i in range(2)]
        Lf = sb("Lf", [P, NT], F32)
        Ld = sb("Ld", [P, NT], F32)
        Lsp = sb("Lsp", [P, NT, 3], F16)
        csum = sb("csum", [P, NT], F32)
        cr = sb("cr", [P, NT], F32)
        wc = sb("wc", [P, CHW], F32)
        wch = [sb(f"wch{i}", [P, CHW], F16) for i in range(2)]

        layers.close()
        w1s = [[sb(f"w1s{i}{j}", [P, WCH, CHW], F16, ctx) for j in range(2)] for i in range(2)]
        w2s = [[sb(f"w2s{i}{j}", [P, WCH, CHW], F16, ctx) for j in range(2)] for i in range(2)]
        b1s = [sb(f"b1s{i}", [P, FO], F32, ctx) for i in range(2)]
        b2s = [sb(f"b2s{i}", [P, C], F32, ctx) for i in range(2)]
        xin = sb("xin", [P, 2, 2 * C], F16, ctx)
        tT = sb("tT", [P, 2, CC, TT], F16, ctx)
        h32 = sb("h32", [P, FO, TT], F32, ctx)
        h16 = [sb(f"h16_{i}", [P, FO, TT], F16, ctx) for i in range(2)]
        yo = sb("yo", [P, 2, C], F32, ctx)

        ps = [ctx.enter_context(nc.psum_tensor(f"ps{i}", [P, 2, 512], F32)) for i in range(4)]

        def bank(i):
            return ps[i // 2][:, i % 2, :]

        def bank16(i):
            return bank(i).bitcast(F16)

        attT = at[:, :, :].rearrange("p t c -> p (t c)").rearrange("p (c n) -> p c n", c=CC)
        uT = oT[0]
        Ef = E[:, :, :].rearrange("p t n -> p (t n)")
        wnat = Ef[:, 0:9 * C].rearrange("p (o c) -> p o c", o=9)
        pnat = Ef[:, 9 * C:12 * C].rearrange("p (o c) -> p o c", o=3)
        gnat = Ef[0:NG, 12 * C:13 * C]
        fnat = Ef[:, 13 * C:14 * C].rearrange("p (o i) -> p o i", o=FO)
        f16n = Ef[:, 14 * C:14 * C + FO * 48].bitcast(F16).rearrange("p (o i) -> p o i", o=FO)
        cpn = Ef[0:KI, 16 * C:20 * C]
        bnat = Ef[0:NE * FO, 20 * C:20 * C + P]
        CB = 2 * 2 * CP
        boxA = [Ef[:, i * CB:(i + 1) * CB].rearrange("p (q t c) -> p q t c", q=2, t=2) for i in range(2)]
        boxX = Ef[:, 2 * CB:3 * CB].rearrange("p (q t c) -> p q t c", q=2, t=2)
        boxY = Ef[:, 3 * CB:4 * CB].rearrange("p (q t c) -> p q t c", q=2, t=2)
        hT = E

        prep_items = []
        for c in range(CC):
            for o0, o1 in ((0, 4), (4, 8), (8, 9)):
                prep_items.append(([w[:, c, o0 * P:o1 * P] for w in wqT], bank(len(prep_items) % RING)[:, 0:(o1 - o0) * P]))
        for c in range(CC):
            prep_items.append(([w[:, c, :] for w in wpT], bank(len(prep_items) % RING)[:, 0:C]))
        prep_items.append(([w[:, :, :].rearrange("p c g -> p (c g)") for w in gpT],
                           bank(len(prep_items) % RING)[:, 0:CC * NG]))

        s_wld = sem("s_wld")
        s_cst = sem("s_cst")
        s_pt = sem("s_pt")
        s_ph = sem("s_ph")
        s_pf = sem("s_pf")
        s_f16 = sem("s_f16")
        s_xb = sem("s_xb")
        s_xn = sem("s_xn")
        s_ve = sem("s_ve")
        s_y0 = sem("s_y0")
        s_pe = sem("s_pe")
        s_hi = sem("s_hi")
        s_fr = sem("s_fr")
        s_stg = sem("s_stg")
        s_oh = sem("s_oh")
        s_qk = [sem("s_qk0"), sem("s_qk1")]
        s_s1 = sem("s_s1")
        s_mx = sem("s_mx")
        s_e1 = sem("s_e1")
        s_ln = sem("s_ln")
        s_lf = sem("s_lf")
        s_lt = sem("s_lt")
        s_lr = sem("s_lr")
        s_s2 = sem("s_s2")
        s_e2 = sem("s_e2")
        s_vp = sem("s_vp")
        s_pv = sem("s_pv")
        s_ev = sem("s_ev")
        s_od = [sem("s_od0"), sem("s_od1")]
        s_at = sem("s_at")
        s_ah = sem("s_ah")
        s_al = sem("s_al")
        s_ut = sem("s_ut")
        s_un = sem("s_un")
        s_z = sem("s_z")
        s_h = sem("s_h")
        s_gl = sem("s_gl")
        s_u = sem("s_u")
        s_y2 = sem("s_y2")
        s_cv = sem("s_cv")
        s_sq = sem("s_sq")
        s_pad = sem("s_pad")
        s_bx = sem("s_bx")
        s_th = sem("s_th")
        s_tl = sem("s_tl")
        s_st = sem("s_st")
        s_d5 = sem("s_d5")
        s_pv0 = sem("s_pv0")
        s_v = sem("s_v")
        s_a = sem("s_a")
        s_wc = sem("s_wc")
        s_wp = sem("s_wp")
        s_wl = sem("s_wl")
        s_pw = sem("s_pw")
        s_sw = sem("s_sw")
        s_ws = sem("s_ws")
        s_ge = sem("s_ge")
        s_gs = sem("s_gs")
        s_gc = sem("s_gc")
        s_ew = [sem("s_ew0"), sem("s_ew1")]
        s_b1 = sem("s_b1")
        s_xi = sem("s_xi")
        s_xt = sem("s_xt")
        s_xe = sem("s_xe")
        s_h1 = sem("s_h1")
        s_hg = sem("s_hg")
        s_ha = sem("s_ha")
        s_h2 = sem("s_h2")
        s_ys = sem("s_ys")
        s_yc = sem("s_yc")
        s_yo = sem("s_yo")
        s_yd = sem("s_yd")
        s_ya = sem("s_ya")

        NSTG = 19
        NXN = NT + 2

        block = ctx.enter_context(nc.Block())

        @block.sync
        def _(sp):
            sp.dma_start(wnat, W_qkv.rearrange("(o p) c -> p o c", p=P)).then_inc(s_wld, 16)
            sp.dma_start(pnat, W_proj.rearrange("(o p) c -> p o c", p=P)).then_inc(s_wld, 16)
            sp.dma_start(gnat, W_gp).then_inc(s_wld, 16)
            sp.dma_start(fnat, c_fc_1.rearrange("(o p) i -> p o i", p=P)).then_inc(s_wld, 16)
            sp.dma_start(cpn, c_proj_1).then_inc(s_wld, 16)
            sp.dma_start(gwn[:, :, :], gate_w.rearrange("(c p) e -> p c e", p=P)).then_inc(s_wld, 16)
            sp.dma_start(c2b[:, :], c_fc_2.to_broadcast([P, KJ])).then_inc(s_wld, 16)
            sp.dma_start(cp2b[:, :], c_proj_2.rearrange("j a -> a j").to_broadcast([P, KJ])).then_inc(s_wld, 16)
            sp.dma_start(gbb[:, :], gate_b.rearrange("(a e) -> a e", a=1).to_broadcast([P, NE])).then_inc(s_wld, 16)

            sp.dma_start(bnat, b1.rearrange("e (o p) -> (e o) p", p=P)).then_inc(s_wld, 16)

            def load_x(b):
                sp.dma_start(xb[:, :, :], x_v[b]).then_inc(s_xb, 16)

            def load_head(b, h, par, mask):
                for dst, src in ((qs[par][0:3 * HD, :], qk_d[0, h]), (ks[par][0:3 * HD, :], qk_d[1, h])):
                    sp.dma_start(dst, src.rearrange("r d n -> (r d) n")).then_inc(s_qk[par], 16)
                sp.dma_start(qs[par][3 * HD + 3:3 * HD + 3 + NG, :], oh_d[0:NG, :]).then_inc(s_qk[par], 16)
                sp.dma_start(ks[par][3 * HD + 3:3 * HD + 3 + NG, :], oh_d[(1 + mask) * NG:(2 + mask) * NG, :]
                             ).then_inc(s_qk[par], 16)

            for par in range(2):
                sp.sem_inc(s_od[par], 16)
            with sp.Fori(0, B) as b:
                load_x(b)
                for j in range(6):
                    sp.wait_ge(s_fr, b * NRING + (1 + OFF_QK + 2 * j + 2))
                    qk, h0 = j // 3, 4 * (j % 3)
                    for r, part in enumerate((0, 0, 1) if qk == 0 else (0, 1, 0)):
                        sp.dma_start(qk_d[qk, h0:h0 + 4, r], stg[part][:, j, :]).then_inc(s_stg, 16)
                sp.wait_ge(s_fr, b * NRING + (1 + OFF_O + 1))
                sp.dma_start(oh_d, ohT[0:3 * NG, :]).then_inc(s_stg, 16)
                sp.wait_ge(s_stg, b * (16 * NSTG) + 16 * NSTG)
                def store_head(h, par):
                    sp.wait_ge(s_ev, b * NH + h + 1)
                    sp.dma_start(att_d[h].rearrange("d (j n) -> j d n", j=4), oT[par][:, :]).then_inc(s_od[par], 16)

                load_head(b, 0, 0, 0)
                load_head(b, 1, 1, 0)
                for mask in range(2):
                    with sp.Fori(0, 2 if mask == 0 else 3) as i:
                        for par in range(2):
                            h = i * 2 + (par + (2 if mask == 0 else 6))
                            sp.wait_ge(s_s2, b * (NH * NT) + (h - 1) * NT)
                            sp.sem_inc(s_sw, 1)
                            load_head(b, h, par, mask)
                            store_head(h - 2, par)
                store_head(NH - 2, 0)
                store_head(NH - 1, 1)
                for par in range(2):
                    sp.wait_ge(s_od[par], 16 + b * (16 * NH // 2) + 16 * NH // 2)
                sp.dma_start(attT, att_d.rearrange("(c h) d n -> (h d) c n", c=CC)).then_inc(s_at, 16)
                sp.wait_ge(s_bx, (b + 1) * 4)
                sp.dma_start(x3_d[0:TOK].rearrange("(b t p) c -> b p t c", p=P, t=NT)[b], xb[:, :, :]).then_inc(s_st, 16)
                sp.wait_ge(s_tl, b + 1)
                sp.dma_start(t16_d.rearrange("(b t p) c -> b p t c", p=P, t=NT)[b], t16[:, :, :]).then_inc(s_st, 16)
                sp.wait_ge(s_st, b * 32 + 32)
                sp.sem_inc(s_sw, 1)
            sp.wait_ge(s_fr, 1 + B * NRING)
            sp.wait_ge(s_ws, 2 * NE * WCH * 32)
            def load_expert(e):
                for k, ws in enumerate((w1s[e % 2], w2s[e % 2])):
                    for j in range(2):
                        sp.dma_start(ws[j][:, :, :], w16_d[k, j, e].rearrange("g p w -> p g w")).then_inc(s_ew[e % 2], 16)
                sp.dma_start(b2s[e % 2][:, :], b2[e].rearrange("(a c) -> a c", a=1).to_broadcast([P, C])).then_inc(s_ew[e % 2], 16)

            def load_tile(j):
                sp.dma_start(xin[:, :, :], t16_d.rearrange("(i s p) c -> i p s c", s=2, p=P)[j]).then_inc(s_xi, 16)

            load_tile(0)
            load_expert(0)
            for e in range(NE):
                if e >= 1:
                    sp.wait_ge(s_yo, e * 2 * ET)
                if e + 1 < NE:
                    load_expert(e + 1)
                with sp.Fori(0, ET - 1) as j:
                    sp.wait_ge(s_xt, j + (e * ET + 1))
                    load_tile(j + 1)
                if e + 1 < NE:
                    sp.wait_ge(s_xt, (e + 1) * ET)
                    load_tile(0)
            sp.wait_ge(s_ya, NE * ET * 32)
            sp.dma_start(out_tok, x3_d[0:TOK]).then_inc(s_st, 16)
            sp.wait_ge(s_st, B * 32 + 16)

        @block.gpsimd
        def _(pool):
            ch = Chain(pool, s_cst)
            ch.mark(pool.memset(ident[:, :], 0.0))
            ch.mark(pool.memset(ident16[:, :], 0.0))
            ch.step(pool.memset(band[:, :], 1.0))
            for m in (ident, ident16):
                ch.step(pool.affine_select(out=m[:, :], in_=m[:, :], compare_op=ALU.not_equal, fill=1.0, base=0,
                                           pattern=[[-1, P]], channel_multiplier=1))
            for base, step, cm in ((W1 // 2, -1, 1), (W1 // 2, 1, -1)):
                ch.step(pool.affine_select(out=band[:, :], in_=band[:, :], compare_op=ALU.is_ge, fill=0.0, base=base,
                                           pattern=[[step, P]], channel_multiplier=cm))
            bv = band[:, :].rearrange("p (a w) -> p a w", w=WD)
            for base, step, cm in ((0, -WD, 1), (WD - 1, WD, -1)):
                ch.step(pool.affine_select(out=bv, in_=bv, compare_op=ALU.is_ge, fill=0.0, base=base,
                                           pattern=[[step, P // WD], [0, WD]], channel_multiplier=cm))
            ch.step(pool.iota(desc[:, :], pattern=[[-1, NG]], base=KI, channel_multiplier=0,
                              allow_small_or_imprecise_dtypes=True))
            for i in range(2):
                ch.step(pool.memset(ks[i][3 * HD:3 * HD + 3, :], 1.0))
            assert ch.n == NCST

            def wait_alone(semaphore, value, carrier=s_pw):
                pool.wait_ge(semaphore, value)
                pool.sem_inc(carrier, 1)

            pool.sem_inc(s_yd, 2)
            ch = Chain(pool, s_wp)
            for k, src in enumerate((w1.rearrange("e (c p) f -> (e c) p f", p=P),
                                     w2.rearrange("e (g o p) d -> (e g) p o d", p=P, o=FO // WCH))):
                with pool.Fori(0, NE * WCH) as m:
                    done = m + k * NE * WCH
                    saved = ch.enter(m, NPW)
                    pool.dma_start(wc[:, :] if k == 0 else wc[:, :].rearrange("p (o d) -> p o d", o=FO // WCH),
                                   src[m]).then_inc(s_wc, 16)
                    wait_alone(s_wc, done * 16 + 16)
                    wait_alone(s_wp, ch.mark(pool.tensor_scalar(wc[:, :], wc[:, :], SW, None, ALU.mult)))
                    wait_alone(s_wp, ch.mark(pool.tensor_copy(wch[0][:, :], wc[:, :])))
                    pool.tensor_tensor(wch[1][:, :], wc[:, :], wch[0][:, :], ALU.subtract).then_inc(s_wl, 1)
                    wait_alone(s_wl, done + 1)
                    for j in range(2):
                        pool.dma_start(w16_d[k, j].rearrange("e g p w -> (e g) p w")[m], wch[j][:, :]).then_inc(s_ws, 16)
                    wait_alone(s_ws, done * 32 + 32)
                ch.leave(saved, NE * WCH)

            pool.wait_ge(s_st, B * 32)
            with pool.Fori(0, NE) as e:
                with pool.Fori(0, ET) as j:
                    for s in range(2):
                        n = e * (2 * ET) + j * 2 + s
                        wait_alone(s_yo, n + 1)
                        pool.dma_start(x3_d[0:TOK].rearrange("(j s p) c -> j s p c", s=2, p=P)[j, s], yo[:, s, :],
                                       accum_op=ALU.add).then_inc(s_ya, 16)
                        wait_alone(s_ya, n * 16 + 16, s_yd)

        @block.scalar
        def _(act):
            def table():
                act.add_instruction(mybir.InstLoadActFuncSet(
                    name=nc.get_next_instruction_name(), act_func_set_id=ACT_SET_EXP_LN, ins=[], outs=[]))

            table()
            for n, (dst, src) in enumerate(prep_items):
                act.wait_ge(s_pt, n + 1)
                nc.scalar.activation(dst[0], src, ACT.Copy, scale=SW).then_inc(s_ph, 1)
            act.wait_ge(s_wld, 16 * NW_LOADS)
            nc.scalar.activation(gw16[0][:, :, :], gwn[:, :, :], ACT.Copy, scale=SW).then_inc(s_ph, 1)

            chs = [0]
            with act.Fori(0, B) as b:
                ch = Chain(act, s_a)
                ch.base = b * NA

                def rsqrt_start(k):
                    act.wait_ge(s_ve, b * 4 + (k + 1))
                    ch.step(nc.scalar.activation(lnv[:, :], ve[:, :], ACT.Ln))
                    nc.scalar.activation(y0[:, :], lnv[:, :], ACT.Exp, scale=-0.5).then_inc(s_y0, 1)

                def hi_item(n, dst, src, scale):
                    act.wait_ge(s_pe, b * NRING + (n + 1))
                    nc.scalar.activation(dst, src, ACT.Copy, scale=scale).then_inc(s_hi, 1)

                rsqrt_start(0)
                for n in range(N_T):
                    hf, c = n // CC, n % CC
                    hi_item(n, xT[0][:, c, hf * 512:(hf + 1) * 512], bank(n % RING), 1.0)
                for n in range(N_QK):
                    j, hf = n // 2, n % 2
                    k = OFF_QK + n
                    hi_item(k, stg[0][:, j, hf * 512:(hf + 1) * 512], bank(k % RING),
                            (QSCALE if j < 3 else 1.0) / (SX * SW))

                def e1(h, par, k):
                    g = b * (NH * NT) + h * NT + k
                    act.wait_ge(s_mx, g + 1)
                    scratch = ps[k % 2][:, :, :].rearrange("p a n -> p (a n)")
                    nc.scalar.activation(scratch, scratch, ACT.Exp,
                                         bias=mn[par][:, k:k + 1], scale=-1.0,
                                         accum_out=rsum[par][:, k:k + 1]).then_inc(s_e1, 1)

                def e2(h, t, first):
                    g = b * (NH * NT) + h * NT + t
                    act.wait_ge(s_s2, g + 1)
                    if not first:
                        act.wait_ge(s_pv, b * (NH * 4) + (h - 1) * 4 + (t // 2 + 1))
                    nc.scalar.activation(E[:, t, :], ps[2][:, :, :].rearrange("p a n -> p (a n)"), ACT.Exp, scale=-1.0,
                                         accum_out=csum[:, t:t + 1]).then_inc(s_e2, 1)

                def ln_rows(h, par):
                    act.wait_ge(s_e1, b * (NH * NT) + (h + 1) * NT)
                    nc.scalar.activation(lnr[par][:, :], rsum[par][:, :], ACT.Ln).then_inc(s_ln, 1)

                def attn(hn, pn, hc, first=False):
                    for k in range(NT + LAG if hc is not None else NT):
                        if k < NT and hn is not None:
                            e1(hn, pn, k)
                        if k == NT and hn is not None:
                            ln_rows(hn, pn)
                        if k >= LAG and hc is not None:
                            e2(hc, k - LAG, first)
                    if hc is None:
                        ln_rows(hn, pn)

                attn(0, 0, None)
                attn(1, 1, 0, first=True)
                with act.Fori(0, 5) as i:
                    attn(i * 2 + 2, 0, i * 2 + 1)
                    attn(i * 2 + 3, 1, i * 2 + 2)
                attn(None, None, NH - 1)

                act.wait_ge(s_at, b * 16 + 16)
                for c in range(CC):
                    nc.scalar.activation(xT[0][:, c, :], attT[:, c, :], ACT.Copy, scale=SATT).then_inc(s_ah, 1)
                rsqrt_start(1)
                for o in range(FO):
                    act.wait_ge(s_h, b * FO + (o + 1))
                    if o >= 4:
                        act.wait_ge(s_u, b * FO + (o - 3))
                    nc.scalar.activation(hT[:, o % 4, :], ps[o % 2][:, :, :].rearrange("p a n -> p (a n)"), ACT.Gelu,
                                         scale=1.0 / (SZ * SC1)).then_inc(s_gl, 1)
                table()
                rsqrt_start(2)
                act.wait_ge(s_xn, b * NXN + (NT + 1))
                for g in range(4):
                    nc.scalar.activation(at[:, 2 * g:2 * g + 2, :], xn[:, 2 * g:2 * g + 2, :], ACT.Square).then_inc(s_y2, 1)
                for t in range(NT):
                    act.wait_ge(s_cv, b * NT + (t + 1))
                    g = t // 2
                    if t % 2 == 0:
                        act.wait_ge(s_pad, b + 1)
                        if g >= 2:
                            act.wait_ge(s_bx, b * 4 + (g - 1))
                    nc.scalar.activation(boxA[g % 2][:, 0, t % 2, PADL:PADL + C], bank(2 * (t % 3))[:, 0:C],
                                         ACT.Square).then_inc(s_sq, 1)
                rsqrt_start(3)
                act.wait_ge(s_xn, b * NXN + NXN)
                nc.scalar.activation(t16[:, :, 0:C], xn[:, :, :], ACT.Copy).then_inc(s_th, 1)
                for n in range(N_T):
                    hf, c = n // CC, n % CC
                    hi_item(OFF_T3 + n, xT[0][:, c, hf * 512:(hf + 1) * 512], bank(n % RING), 1.0)
                assert ch.n == NA

            act.wait_ge(s_gs, 1)
            nc.scalar.activation(gates[:, :, :], gates[:, :, :], ACT.Exp).then_inc(s_ge, 1)
            with act.Fori(0, NE // 2) as pair:
                for par in range(2):
                    act.wait_ge(s_b1, pair * 2 + (par + 1))
                    with act.Fori(0, ET) as j:
                        i = pair * (2 * ET) + (j + par * ET)
                        for q in range(FO // 2):
                            act.wait_ge(s_h1, i * (FO // 2) + (q + 1))
                            for o in (2 * q, 2 * q + 1):
                                last = nc.scalar.activation(h32[:, o, :], bank(q % 3)[:, (o % 2) * TT:(o % 2 + 1) * TT],
                                                            ACT.Gelu, bias=b1s[par][:, o:o + 1], scale=1.0 / (SX * SW))
                            last.then_inc(s_hg, 1)

        @block.tensor
        def _(pe):
            pe.wait_ge(s_cst, NCST)
            pe.wait_ge(s_wld, 16 * NW_LOADS)
            n = 0
            for c in range(CC):
                for o0, o1 in ((0, 4), (4, 8), (8, 9)):
                    if n >= RING:
                        pe.wait_ge(s_pf, n - RING + 1)
                    for o in range(o0, o1):
                        last = nc.tensor.transpose(bank(n % RING)[:, (o - o0) * P:(o - o0 + 1) * P],
                                                   wnat[:, o, c * P:(c + 1) * P], ident[:, :])
                    last.then_inc(s_pt, 1)
                    n += 1
            for c in range(CC):
                pe.wait_ge(s_pf, n - RING + 1)
                for o in range(CC):
                    last = nc.tensor.transpose(bank(n % RING)[:, o * P:(o + 1) * P], pnat[:, o, c * P:(c + 1) * P],
                                               ident[:, :])
                last.then_inc(s_pt, 1)
                n += 1
            pe.wait_ge(s_pf, n - RING + 1)
            for c in range(CC):
                last = nc.tensor.transpose(bank(n % RING)[:, c * NG:(c + 1) * NG], gnat[:, c * P:(c + 1) * P],
                                           ident[0:NG, 0:NG])
            last.then_inc(s_pt, 1)
            n += 1
            assert n == len(prep_items)
            pe.wait_ge(s_pf, n - RING + 1)
            for o in range(FO):
                last = nc.tensor.transpose(bank(6)[:, o * KI:(o + 1) * KI], cpn[:, o * P:(o + 1) * P],
                                           ident[0:KI, 0:KI])
            nc.tensor.transpose(bank(7)[:, 0:NE * FO], bnat, ident[0:NE * FO, 0:NE * FO]).then_inc(s_pt, 1)
            pe.wait_ge(s_f16, 1)
            pe.wait_ge(s_pf, n)
            for o in range(FO):
                last = nc.tensor.transpose(bank16(o // 8)[0:3 * KI, (o % 8) * P:(o % 8 + 1) * P], f16n[:, o, :],
                                           ident16[:, :])
            last.then_inc(s_pt, 1)
            pe.wait_ge(s_pf, n + 3)

            with pe.Fori(0, B) as b:
                def ring(k, s0):
                    pe.wait_ge(s_fr, b * NRING + (1 + max(s0, k - RING + 1)))
                    return (k - s0) % RING

                def products(dst, pairs):
                    todo = [(lh[i], rh[j]) for lh, rh in pairs for i, j in ((0, 0), (0, 1), (1, 0))]
                    for m, (lhsT, rhs) in enumerate(todo):
                        last = nc.tensor.matmul(dst, lhsT, rhs, start=(m == 0), stop=(m == len(todo) - 1))
                    return last

                def transposes(s0, k0, src, ready):
                    for n in range(N_T):
                        hf, c = n // CC, n % CC
                        if c == 0:
                            ready(hf)
                        at_bank = bank(ring(k0 + n, s0))
                        for tt in range(4):
                            last = nc.tensor.transpose(at_bank[:, tt * P:(tt + 1) * P],
                                                       src[:, 4 * hf + tt, c * P:(c + 1) * P], ident[:, :])
                        last.then_inc(s_pe, 1)

                transposes(0, 0, xn, lambda hf: pe.wait_ge(s_xn, b * NXN + 4 * (hf + 1)))
                for n in range(N_QK):
                    j, hf = n // 2, n % 2
                    k = OFF_QK + n
                    pe.wait_ge(s_fr, b * NRING + (1 + (hf + 1) * CC))
                    i = ring(k, 0)
                    products(bank(i), [([wqT[a][:, c, j * P:(j + 1) * P] for a in range(2)],
                                        [xT[a][:, c, hf * 512:(hf + 1) * 512] for a in range(2)])
                                       for c in range(CC)]).then_inc(s_pe, 1)
                for t in range(NT):
                    i = ring(OFF_V + t, 0)
                    products(bank(i)[:, 0:C], [([xT[a][:, c, t * P:(t + 1) * P] for a in range(2)],
                                                [wqT[a][:, c, 2 * C:3 * C] for a in range(2)])
                                               for c in range(CC)]).then_inc(s_pe, 1)
                i = ring(OFF_G, 0)
                pe.wait_ge(s_fr, b * NRING + (1 + OFF_QK + 6))
                for t in range(NT):
                    last = products(bank(i)[:, t * 32:t * 32 + NG],
                                    [([stg[a][:, c, t * P:(t + 1) * P] for a in range(2)],
                                      [gpT[a][:, c, :] for a in range(2)]) for c in range(CC)])
                last.then_inc(s_pe, 1)
                i = ring(OFF_O, 0)
                pe.wait_ge(s_oh, b + 1)
                for t in range(NT):
                    last = nc.tensor.transpose(bank16(i)[0:OHW, t * P:(t + 1) * P], ohn[:, t, :], ident16[:, :])
                last.then_inc(s_pe, 1)
                pe.wait_ge(s_fr, b * NRING + (1 + SEC1))

                pv = bank(6)
                lt = bank16(7)

                def quarters(lhsT, rhs, start, stop):
                    for j in range(4):
                        last = nc.tensor.matmul(pv[32 * j:32 * j + 32, 0:N // 4], lhsT,
                                                rhs[:, j * (N // 4):(j + 1) * (N // 4)], start=start, stop=stop)
                    return last

                def p1(h, par, k, half, head0=False):
                    g = b * (NH * NT) + h * NT + k
                    if k == 0:
                        pe.wait_ge(s_qk[par], b * (64 * 6) + half * 64 + 64)
                    if not (head0 and k < 2):
                        pe.wait_ge(s_e1, g - 1)
                    for hf in range(2):
                        last = nc.tensor.matmul(ps[k % 2][:, hf, :], qs[par][0:3 * HD, k * P:(k + 1) * P],
                                                ks[par][0:3 * HD, hf * 512:(hf + 1) * 512], start=True, stop=True)
                    last.then_inc(s_s1, 1)

                def p2(h, par, t, head0=False):
                    g = b * (NH * NT) + h * NT + t
                    if t == 0:
                        pe.wait_ge(s_lr, b * NH + h + 1)
                    if not (head0 and t == 0):
                        pe.wait_ge(s_e2, g)
                    k2 = 3 * HD + 3 + NG
                    for hf in range(2):
                        last = nc.tensor.matmul(ps[2][:, hf, :], ks[par][0:k2, t * P:(t + 1) * P],
                                                qs[par][0:k2, hf * 512:(hf + 1) * 512], start=True, stop=True)
                    last.then_inc(s_s2, 1)

                def lrows(h):
                    pe.wait_ge(s_lf, b * NH + h + 1)
                    for t in range(NT):
                        last = nc.tensor.transpose(lt[0:3, t * P:(t + 1) * P], Lsp[:, t, :], ident16[:, :])
                    last.then_inc(s_lt, 1)

                def pvs(h, u, head0=False):
                    pe.wait_ge(s_vp, b * (NH * 4) + h * 4 + (u + 1))
                    if u == 0 and not head0:
                        pe.wait_ge(s_ev, b * NH + h)
                    for t in (2 * u, 2 * u + 1):
                        last = quarters(vp[:, t, :], E[:, t, :], t == 0, t == NT - 1)
                    last.then_inc(s_pv, 1)

                def attn(hn, pn, hc, pc, hp, half, head0=False):
                    for k in range(NT + LAG):
                        if k < NT and hn is not None:
                            p1(hn, pn, k, half)
                        if k == 0:
                            lrows(hc)
                        if k >= LAG:
                            p2(hc, pc, k - LAG, head0)
                        if k == 1 and hp is not None:
                            pvs(hp, 2)
                        if k == 2 and hp is not None:
                            pvs(hp, 3)
                        if k - LAG == 3:
                            pvs(hc, 0, head0)
                        if k - LAG == 5:
                            pvs(hc, 1)

                for k in range(NT):
                    p1(0, 0, k, 0, head0=True)
                attn(1, 1, 0, 0, None, 0, head0=True)
                with pe.Fori(0, 5) as i:
                    attn(i * 2 + 2, 0, i * 2 + 1, 1, i * 2, i + 1)
                    attn(i * 2 + 3, 1, i * 2 + 2, 0, i * 2 + 1, i + 1)
                attn(None, None, NH - 1, 1, NH - 2, 0)
                pvs(NH - 1, 2)
                pvs(NH - 1, 3)

                pe.wait_ge(s_ev, b * NH + NH)
                pe.wait_ge(s_al, b * CC + CC)
                for t in range(NT):
                    i = ring(OFF_PJ + t, SEC1)
                    products(bank(i)[:, 0:C], [([xT[a][:, c, t * P:(t + 1) * P] for a in range(2)],
                                                [wpT[a][:, c, :] for a in range(2)])
                                               for c in range(CC)]).then_inc(s_pe, 1)
                i = ring(OFF_Z, SEC1)
                pe.wait_ge(s_z, b + 1)
                for t in range(NT):
                    last = nc.tensor.transpose(bank16(i)[0:3 * KI, t * P:(t + 1) * P], znat[:, t, :], ident16[:, :])
                last.then_inc(s_pe, 1)
                pe.wait_ge(s_fr, b * NRING + (1 + OFF_Z + 1))
                for o in range(FO + 1):
                    if o < FO:
                        if o >= 2:
                            pe.wait_ge(s_gl, b * FO + (o - 1))
                        for hf in range(2):
                            last = nc.tensor.matmul(ps[o % 2][:, hf, :], c1s[:, o * P:(o + 1) * P],
                                                    zT[:, hf * 512:(hf + 1) * 512], start=True, stop=True)
                        last.then_inc(s_h, 1)
                    if o >= 1:
                        pe.wait_ge(s_gl, b * FO + o)
                        quarters(cp1T[:, o - 1, :], hT[:, (o - 1) % 4, :], o == 1, o == FO).then_inc(s_u, 1)
                pe.wait_ge(s_ut, b + 1)
                for s in range(2):
                    last = nc.tensor.transpose(bank(7)[:, s * P:(s + 1) * P], uT[:, s * P:(s + 1) * P], ident[:, :])
                last.then_inc(s_un, 1)
                pe.wait_ge(s_xn, b * NXN + (NT + 1))
                for t in range(NT):
                    pe.wait_ge(s_y2, b * 4 + (t // 2 + 1))
                    if t >= 3:
                        pe.wait_ge(s_sq, b * NT + (t - 2))
                        pe.wait_ge(s_d5, b * NT + (t - 2))
                    nc.tensor.matmul(bank(2 * (t % 3))[:, 0:C], band[:, :], xn[:, t, :], start=True, stop=True)
                    nc.tensor.matmul(bank(2 * (t % 3) + 1)[:, 0:C], band[:, :], at[:, t, :], start=True, stop=True
                                     ).then_inc(s_cv, 1)
                transposes(OFF_T3, OFF_T3, xn, lambda hf: pe.wait_ge(s_xn, b * NXN + NXN))
                i = ring(OFF_SC, OFF_T3)
                pe.wait_ge(s_fr, b * NRING + (1 + OFF_T3 + N_T))
                for t in range(NT):
                    last = products(bank(i)[:, t * NE:(t + 1) * NE],
                                    [([xT[a][:, c, t * P:(t + 1) * P] for a in range(2)],
                                      [gw16[a][:, c, :] for a in range(2)]) for c in range(CC)])
                last.then_inc(s_pe, 1)

            with pe.Fori(0, NE // 2) as pair:
                for par in range(2):
                    pe.wait_ge(s_ew[par], pair * 80 + 80)
                    pe.sem_inc(s_pw, 1)
                    with pe.Fori(0, ET) as j:
                        i = pair * (2 * ET) + (j + par * ET)
                        pe.wait_ge(s_xi, i * 16 + 16)
                        for s in range(2):
                            for c in range(CC):
                                for th in range(2):
                                    last = nc.tensor.transpose(bank16(6 + s)[:, c * TT + th * P:c * TT + (th + 1) * P],
                                                               xin[:, th, s * C + c * P:s * C + (c + 1) * P],
                                                               ident16[:, :])
                        last.then_inc(s_xt, 1)
                        pe.wait_ge(s_xe, i * 2 + 2)
                        for q in range(FO // 2):
                            if q >= 3:
                                pe.wait_ge(s_hg, i * (FO // 2) + (q - 2))
                            for o in (2 * q, 2 * q + 1):
                                todo = [(a, c2, c) for c in range(CC) for a, c2 in ((0, 0), (1, 0), (0, 1))]
                                for m, (a, x_, c) in enumerate(todo):
                                    last = nc.tensor.matmul(bank(q % 3)[:, (o % 2) * TT:(o % 2 + 1) * TT],
                                                            w1s[par][a][:, c, o * P:(o + 1) * P], tT[:, x_, c, :],
                                                            start=(m == 0), stop=(m == len(todo) - 1))
                            last.then_inc(s_h1, 1)
                        for s in range(2):
                            sl = slice(s * P, (s + 1) * P)
                            for o in range(FO):
                                if s == 0 and o % 2 == 0:
                                    pe.wait_ge(s_h2, i * (FO // 2) + (o // 2 + 1))
                                for m, (a, w_) in enumerate(((0, 0), (0, 1), (1, 0))):
                                    g, r = o // (FO // WCH), o % (FO // WCH)
                                    last = nc.tensor.matmul(bank(4 + s)[:, 0:C], h16[a][:, o, sl],
                                                            w2s[par][w_][:, g, r * C:(r + 1) * C],
                                                            start=(o == 0 and m == 0), stop=(o == FO - 1 and m == 2))
                            last.then_inc(s_ys, 1)

        @block.vector
        def _(dve):
            dve.sem_inc(s_fr, 1)
            ch = Chain(dve, s_pv0)
            dve.wait_ge(s_cst, NCST)
            nc.vector.reduce_sum(cnt[:, :], band[:, :], AX.X)
            nc.vector.memset(ohn[:, :, 3 * NG:OHW], 0.0)
            for n, (dst, src) in enumerate(prep_items):
                dve.wait_ge(s_ph, n + 1)
                nc.vector.scalar_tensor_tensor(out=dst[1], in0=src, scalar=SW, in1=dst[0], op0=ALU.mult,
                                               op1=ALU.subtract).then_inc(s_pf, 1)
                if n == 0:
                    ch.mark(nc.vector.tensor_scalar(f16n[:, :, 0:KI], fnat, SC1, None, ALU.mult))
                    ch.step(nc.vector.tensor_scalar(f16n[:, :, 2 * KI:3 * KI], fnat, SC1, None, ALU.mult))
                    nc.vector.scalar_tensor_tensor(out=f16n[:, :, KI:2 * KI], in0=fnat, scalar=SC1,
                                                   in1=f16n[:, :, 0:KI], op0=ALU.mult,
                                                   op1=ALU.subtract).then_inc(s_f16, 1)
            np_ = len(prep_items)
            dve.wait_ge(s_ph, np_ + 1)
            nc.vector.scalar_tensor_tensor(out=gw16[1][:, :, :], in0=gwn[:, :, :], scalar=SW, in1=gw16[0][:, :, :],
                                           op0=ALU.mult, op1=ALU.subtract).then_inc(s_pf, 1)
            dve.wait_ge(s_pt, np_ + 1)
            nc.vector.tensor_copy(cp1T[:, :, :].rearrange("p o i -> p (o i)"), bank(6)[:, 0:C])
            nc.vector.tensor_copy(b1T[:, :], bank(7)[:, 0:NE * FO]).then_inc(s_pf, 1)
            dve.wait_ge(s_pt, np_ + 2)
            nc.vector.tensor_copy(c1s[:, 0:1024], bank16(0)[0:3 * KI, :])
            nc.vector.tensor_copy(c1s[:, 1024:FFN], bank16(1)[0:3 * KI, 0:512]).then_inc(s_pf, 1)

            with dve.Fori(0, B) as b:
                ch = Chain(dve, s_v)
                ch.base = b * NV

                def layer_stats(k, eps, scale):
                    for t in range(NT):
                        m = ch.mark(nc.vector.bn_stats(st6[:, t, :], xb[:, t, :]))
                    ch.wait(m)
                    nc.vector.memset(nt1[:, :], 0.0)
                    for t in range(NT):
                        m = ch.mark(nc.vector.bn_aggr(mv[:, t, :], st6[:, t, :]))
                    ch.wait(m)
                    nc.vector.tensor_scalar(ve[:, :], mv[:, :, 1], eps, None, ALU.add).then_inc(s_ve, 1)
                    dve.wait_ge(s_y0, b * 4 + (k + 1))
                    ch.step(nc.vector.tensor_tensor(nt1[:, :], y0[:, :], y0[:, :], ALU.mult))
                    ch.step(nc.vector.tensor_tensor(nt1[:, :], nt1[:, :], ve[:, :], ALU.mult))
                    ch.step(nc.vector.tensor_scalar(nt1[:, :], nt1[:, :], -0.5 * scale, 1.5 * scale, ALU.mult, ALU.add))
                    ch.step(nc.vector.tensor_tensor(rs[:, :], nt1[:, :], y0[:, :], ALU.mult))

                def normalise(t):
                    return nc.vector.tensor_scalar(xn[:, t, :], xb[:, t, :], mv[:, t, 0:1], rs[:, t:t + 1],
                                                   ALU.subtract, ALU.mult)

                def lo_item(n, dst, src, hi, scale):
                    dve.wait_ge(s_hi, b * NHI + hi_count(n))
                    nc.vector.scalar_tensor_tensor(out=dst, in0=src, scalar=scale, in1=hi, op0=ALU.mult,
                                                   op1=ALU.subtract).then_inc(s_fr, 1)

                def lo_transposed(k0, scale):
                    for n in range(N_T):
                        hf, c = n // CC, n % CC
                        lo_item(k0 + n, xT[1][:, c, hf * 512:(hf + 1) * 512], bank(n % RING),
                                xT[0][:, c, hf * 512:(hf + 1) * 512], scale)

                dve.wait_ge(s_xb, b * 16 + 16)
                layer_stats(0, 1e-6, SX)
                for t in range(NT):
                    normalise(t).then_inc(s_xn, 1)
                lo_transposed(0, 1.0)
                for n in range(N_QK):
                    j, hf = n // 2, n % 2
                    k = OFF_QK + n
                    sl = slice(hf * 512, (hf + 1) * 512)
                    lo_item(k, stg[1][:, j, sl], bank(k % RING), stg[0][:, j, sl], (QSCALE if j < 3 else 1.0) / (SX * SW))
                for t in range(NT):
                    k = OFF_V + t
                    dve.wait_ge(s_pe, b * NRING + (k + 1))
                    nc.vector.tensor_scalar(va[:, t, :], bank(k % RING)[:, 0:C], 1.0 / (SX * SW), None, ALU.mult
                                            ).then_inc(s_fr, 1)
                dve.wait_ge(s_pe, b * NRING + (OFF_G + 1))
                g3 = bank(OFF_G % RING)[:, 0:NT * 32].rearrange("p (t g) -> p t g", g=32)[:, :, 0:NG]
                cp = nc.vector.tensor_copy(gws[:, :, :], g3)
                cp.then_inc(s_fr, 1)
                dve.wait_ge(s_fr, b * NRING + (1 + OFF_G + 1))
                gb = gm[:, :].rearrange("p (t a) -> p t a", a=1).to_broadcast([P, NT, NG])
                db = desc[:, :].rearrange("p (a g) -> p a g", a=1).to_broadcast([P, NT, NG])
                ch.step(nc.vector.tensor_reduce(gm[:, :], gws[:, :, :], axis=AX.X, op=ALU.min))
                ch.step(nc.vector.tensor_tensor(gwe[:, :, :], gws[:, :, :], gb, ALU.is_equal))
                ch.step(nc.vector.tensor_tensor(gwe[:, :, :], gwe[:, :, :], db, ALU.mult))
                ch.step(nc.vector.tensor_reduce(gm[:, :], gwe[:, :, :], axis=AX.X, op=ALU.max))
                ch.step(nc.vector.tensor_tensor(gws[:, :, :], gwe[:, :, :], gb, ALU.is_equal))
                ch.mark(nc.vector.tensor_scalar(ohn[:, :, 0:NG], gws[:, :, :], BIG, None, ALU.mult))
                ch.mark(nc.vector.tensor_scalar(ohn[:, :, NG:2 * NG], gws[:, :, :], -1.0, 1.0, ALU.mult, ALU.add))
                nc.vector.tensor_copy(ohn[:, :, 2 * NG:3 * NG], gws[:, :, :]).then_inc(s_oh, 1)
                dve.wait_ge(s_pe, b * NRING + (OFF_O + 1))
                nc.vector.tensor_copy(ohT[:, :], bank16(OFF_O % RING)[0:OHW, :]).then_inc(s_fr, 1)

                def mx(h, par, k):
                    dve.wait_ge(s_s1, b * (NH * NT) + h * NT + (k + 1))
                    nc.vector.tensor_reduce(mn[par][:, k:k + 1], ps[k % 2][:, :, :].rearrange("p a n -> p (a n)"),
                                            axis=AX.X, op=ALU.min).then_inc(s_mx, 1)

                def values(h, u):
                    sl = slice(2 * u, 2 * u + 2)
                    dve.wait_ge(s_e2, b * (NH * NT) + h * NT + (2 * u + 2))
                    ch.step(nc.vector.tensor_scalar(cr[:, sl], csum[:, sl], 1e-8, None, ALU.add))
                    ch.step(nc.vector.reciprocal(cr[:, sl], cr[:, sl]))
                    nc.vector.tensor_tensor(vp[:, sl, :], va[:, sl, bass.ds(h * HD, HD)],
                                            cr[:, sl].rearrange("p (t a) -> p t a", a=1).to_broadcast([P, 2, HD]),
                                            ALU.mult).then_inc(s_vp, 1)

                def lparts(h, par):
                    dve.wait_ge(s_ln, b * NH + h + 1)
                    ch.step(nc.vector.tensor_tensor(Lf[:, :], lnr[par][:, :], mn[par][:, :], ALU.subtract))
                    ch.step(nc.vector.tensor_copy(Lsp[:, :, 0], Lf[:, :]))
                    ch.step(nc.vector.tensor_tensor(Ld[:, :], Lf[:, :], Lsp[:, :, 0], ALU.subtract))
                    ch.step(nc.vector.tensor_copy(Lsp[:, :, 1], Ld[:, :]))
                    nc.vector.tensor_tensor(Lsp[:, :, 2], Ld[:, :], Lsp[:, :, 1], ALU.subtract).then_inc(s_lf, 1)

                def lcopy(h, par):
                    dve.wait_ge(s_lt, b * NH + h + 1)
                    nc.vector.tensor_copy(qs[par][3 * HD:3 * HD + 3, :], bank16(7)[0:3, :]).then_inc(s_lr, 1)

                def evict(h, par, before):
                    dve.wait_ge(s_pv, b * (NH * 4) + h * 4 + 4)
                    dve.wait_ge(s_od[par], 16 + b * (16 * NH // 2) + before * 16)
                    nc.vector.tensor_copy(oT[par][:, :], bank(6)[:, 0:N // 4]).then_inc(s_ev, 1)

                def attn(hn, pn, hc, pc, hp, before=None):
                    for k in range(NT + LAG):
                        if k < NT and hn is not None:
                            mx(hn, pn, k)
                        if k == 0:
                            lcopy(hc, pc)
                            if hp is not None:
                                values(hp, 3)
                        if k == 3 and hp is not None:
                            evict(hp, 1 - pc, before)
                        if k == NT and hn is not None:
                            lparts(hn, pn)
                        if k - LAG - 1 in (1, 3, 5):
                            values(hc, (k - LAG - 1) // 2)

                for k in range(NT):
                    mx(0, 0, k)
                lparts(0, 0)
                attn(1, 1, 0, 0, None)
                with dve.Fori(0, 5) as i:
                    saved = ch.enter(i, NVA)
                    attn(i * 2 + 2, 0, i * 2 + 1, 1, i * 2, i)
                    attn(i * 2 + 3, 1, i * 2 + 2, 0, i * 2 + 1, i)
                ch.leave(saved, 5)
                attn(None, None, NH - 1, 1, NH - 2, 5)
                values(NH - 1, 3)
                evict(NH - 1, 1, 5)

                for c in range(CC):
                    dve.wait_ge(s_ah, b * CC + (c + 1))
                    nc.vector.scalar_tensor_tensor(out=xT[1][:, c, :], in0=attT[:, c, :], scalar=SATT,
                                                   in1=xT[0][:, c, :], op0=ALU.mult, op1=ALU.subtract).then_inc(s_al, 1)
                for t in range(NT):
                    k = OFF_PJ + t
                    dve.wait_ge(s_pe, b * NRING + (k + 1))
                    nc.vector.scalar_tensor_tensor(out=xb[:, t, :], in0=bank((k - SEC1) % RING)[:, 0:C],
                                                   scalar=1.0 / (SATT * SW), in1=xb[:, t, :], op0=ALU.mult,
                                                   op1=ALU.add).then_inc(s_fr, 1)
                dve.wait_ge(s_fr, b * NRING + (1 + OFF_Z))
                layer_stats(1, 1e-5, SZ)
                for t in range(NT):
                    m = ch.mark(nc.vector.scalar_tensor_tensor(
                        out=xn[:, t, :].rearrange("p (i j) -> p i j", j=KJ),
                        in0=xb[:, t, :].rearrange("p (i j) -> p i j", j=KJ), scalar=mv[:, t, 0:1],
                        in1=c2b[:, :].rearrange("p (a j) -> p a j", a=1).to_broadcast([P, KI, KJ]),
                        op0=ALU.subtract, op1=ALU.mult))
                ch.wait(m)
                ch.step(nc.vector.reduce_sum(zz[:, :, :].rearrange("p t i -> p (t i)"),
                                             xn[:, :, :].rearrange("p t (i j) -> p (t i) j", j=KJ), AX.X))
                ch.step(nc.vector.tensor_tensor(zs[:, :, :], zz[:, :, :],
                                                rs[:, :].rearrange("p (t a) -> p t a", a=1).to_broadcast([P, NT, KI]),
                                                ALU.mult))
                ch.mark(nc.vector.tensor_copy(znat[:, :, KI:2 * KI], zs[:, :, :]))
                ch.step(nc.vector.tensor_copy(znat[:, :, 0:KI], zs[:, :, :]))
                nc.vector.tensor_tensor(znat[:, :, 2 * KI:3 * KI], zs[:, :, :], znat[:, :, 0:KI], ALU.subtract
                                        ).then_inc(s_z, 1)
                dve.wait_ge(s_pe, b * NRING + (OFF_Z + 1))
                nc.vector.tensor_copy(zT[:, :], bank16((OFF_Z - SEC1) % RING)[0:3 * KI, :]).then_inc(s_fr, 1)
                dve.wait_ge(s_u, b * FO + FO)
                nc.vector.tensor_copy(uT[:, :], bank(6)[:, 0:N // 4]).then_inc(s_ut, 1)
                dve.wait_ge(s_un, b + 1)
                for s in range(2):
                    m = ch.mark(nc.vector.tensor_copy(
                        zz[:, :, :].rearrange("p (j s) i -> p s j i", s=2)[:, s],
                        bank(7)[:, s * P:(s + 1) * P].rearrange("p (j i) -> p j i", i=KI)))
                ch.wait(m)
                ch.step(nc.vector.tensor_tensor(
                    at[:, :, :].rearrange("p t (i j) -> p (t i) j", j=KJ),
                    zz[:, :, :].rearrange("p t (i a) -> p (t i) a", a=1).to_broadcast([P, NT * KI, KJ]),
                    cp2b[:, :].rearrange("p (a j) -> p a j", a=1).to_broadcast([P, NT * KI, KJ]), ALU.mult))
                ch.step(nc.vector.tensor_tensor(xb[:, :, :], xb[:, :, :], at[:, :, :], ALU.add))
                for i in range(2):
                    nc.vector.memset(boxA[i][:, :, :, 0:PADL], 0.0)
                    last = nc.vector.memset(boxA[i][:, :, :, PADL + C:CP], 0.0)
                last.then_inc(s_pad, 1)
                layer_stats(2, 1e-6, 1.0)
                for t in range(NT - 1):
                    normalise(t)
                normalise(NT - 1).then_inc(s_xn, 1)
                for g in range(4):
                    A = boxA[g % 2]
                    for t in (2 * g, 2 * g + 1):
                        dve.wait_ge(s_cv, b * NT + (t + 1))
                        nc.vector.tensor_scalar(A[:, 1, t % 2, PADL:PADL + C], bank(2 * (t % 3) + 1)[:, 0:C],
                                                cnt[:, 0:1], None, ALU.mult).then_inc(s_d5, 1)
                    dve.wait_ge(s_sq, b * NT + (2 * g + 2))
                    dve.wait_ge(s_d5, b * NT + (2 * g + 2))
                    dve.wait_ge(s_pad, b + 1)

                    def add(o, a, sa, c, sc, length):
                        ch.step(nc.vector.tensor_tensor(o[:, :, :, 0:length], a[:, :, :, sa:sa + length],
                                                        c[:, :, :, sc:sc + length], ALU.add))

                    add(boxX, A, 0, A, 1, CP - 1)
                    add(boxY, boxX, 0, boxX, 2, CP - 3)
                    add(boxX, boxY, 0, boxY, 4, CP - 7)
                    add(A, boxX, 0, boxX, 8, CP - 15)
                    add(boxX, A, 0, boxY, 16, C)
                    num, den = boxX[:, 0, :, 0:C], boxX[:, 1, :, 0:C]
                    tot, dn, nm = boxY[:, 0, :, 0:C], A[:, 1, :, 0:C], A[:, 0, :, 0:C]
                    xs = xb[:, 2 * g:2 * g + 2, :]
                    ch.step(nc.vector.tensor_tensor(tot, num, den, ALU.add))
                    ch.step(nc.vector.scalar_tensor_tensor(out=dn, in0=tot, scalar=0.0, in1=den, op0=ALU.is_equal,
                                                           op1=ALU.add))
                    ch.step(nc.vector.scalar_tensor_tensor(out=nm, in0=tot, scalar=0.0, in1=num, op0=ALU.is_equal,
                                                           op1=ALU.add))
                    ch.step(nc.vector.reciprocal(dn, dn))
                    ch.step(nc.vector.tensor_tensor(nm, nm, dn, ALU.mult))
                    ch.step(nc.vector.scalar_tensor_tensor(out=xs, in0=nm, scalar=FLT_MAX, in1=xs, op0=ALU.min,
                                                           op1=ALU.add))
                    nc.vector.memset(A[:, :, :, 0:PADL], 0.0).then_inc(s_bx, 1)
                layer_stats(3, 1e-5, SX)
                for t in range(NT - 1):
                    normalise(t)
                normalise(NT - 1).then_inc(s_xn, 1)
                dve.wait_ge(s_th, b + 1)
                nc.vector.tensor_tensor(t16[:, :, C:2 * C], xn[:, :, :], t16[:, :, 0:C], ALU.subtract).then_inc(s_tl, 1)
                lo_transposed(OFF_T3, 1.0)
                dve.wait_ge(s_pe, b * NRING + NRING)
                nc.vector.scalar_tensor_tensor(
                    out=scores[:, bass.ds(b * NT, NT), :],
                    in0=bank((OFF_SC - OFF_T3) % RING)[:, 0:NT * NE].rearrange("p (t e) -> p t e", e=NE),
                    scalar=1.0 / (SX * SW),
                    in1=gbb[:, :].rearrange("p (a e) -> p a e", a=1).to_broadcast([P, NT, NE]),
                    op0=ALU.mult, op1=ALU.add).then_inc(s_fr, 1)
                assert ch.n == NV, ch.n

            ch = Chain(dve, s_gc)

            def rows(v):
                return v[:, :].rearrange("p (t a) -> p t a", a=1).to_broadcast([P, B * NT, NE])

            ranks = desc[:, 0:NE].rearrange("p (a e) -> p a e", a=1).to_broadcast([P, B * NT, NE])
            dve.wait_ge(s_fr, 1 + B * NRING)
            ch.step(nc.vector.tensor_reduce(red[:, :], scores[:, :, :], axis=AX.X, op=ALU.max))
            nc.vector.tensor_tensor(gates[:, :, :], scores[:, :, :], rows(red), ALU.subtract).then_inc(s_gs, 1)
            dve.wait_ge(s_ge, 1)
            ch.step(nc.vector.reduce_sum(red[:, :], gates[:, :, :], AX.X))
            ch.step(nc.vector.reciprocal(red[:, :], red[:, :]))
            ch.step(nc.vector.tensor_tensor(gates[:, :, :], gates[:, :, :], rows(red), ALU.mult))
            ch.step(nc.vector.tensor_copy(pr2[:, :, :], gates[:, :, :]))
            for k, oh in enumerate((oh1, oh2)):
                ch.step(nc.vector.tensor_reduce(red[:, :], pr2[:, :, :], axis=AX.X, op=ALU.max))
                ch.step(nc.vector.tensor_tensor(oh[:, :, :], pr2[:, :, :], rows(red), ALU.is_equal))
                ch.step(nc.vector.tensor_tensor(oh[:, :, :], oh[:, :, :], ranks, ALU.mult))
                ch.step(nc.vector.tensor_reduce(red[:, :], oh[:, :, :], axis=AX.X, op=ALU.max))
                ch.step(nc.vector.tensor_tensor(oh[:, :, :], oh[:, :, :], rows(red), ALU.is_equal))
                if k == 0:
                    ch.step(nc.vector.scalar_tensor_tensor(out=pr2[:, :, :], in0=oh1[:, :, :], scalar=-2.0,
                                                           in1=pr2[:, :, :], op0=ALU.mult, op1=ALU.add))
            ch.step(nc.vector.tensor_tensor(pr2[:, :, :], oh1[:, :, :], oh2[:, :, :], ALU.add))
            ch.step(nc.vector.tensor_tensor(gates[:, :, :], gates[:, :, :], pr2[:, :, :], ALU.mult))
            ch.step(nc.vector.reduce_sum(red[:, :], gates[:, :, :], AX.X))
            ch.step(nc.vector.tensor_scalar(red[:, :], red[:, :], 1e-9, None, ALU.add))
            ch.step(nc.vector.reciprocal(red[:, :], red[:, :]))
            ch.step(nc.vector.tensor_tensor(gates[:, :, :], gates[:, :, :], rows(red), ALU.mult))

            with dve.Fori(0, NE // 2) as pair:
                for par in range(2):
                    nc.vector.tensor_scalar(b1s[par][:, :], b1T[:, bass.ds(pair * (2 * FO) + par * FO, FO)], 1.0, None,
                                            ALU.mult).then_inc(s_b1, 1)
                    with dve.Fori(0, ET) as j:
                        i = pair * (2 * ET) + (j + par * ET)
                        dve.wait_ge(s_xt, i + 1)
                        for s in range(2):
                            nc.vector.tensor_copy(tT[:, s, :, :].rearrange("p c n -> p (c n)"),
                                                  bank16(6 + s)[:, 0:CC * TT]).then_inc(s_xe, 1)
                        for q in range(FO // 2):
                            dve.wait_ge(s_hg, i * (FO // 2) + (q + 1))
                            hs = slice(2 * q, 2 * q + 2)
                            nc.vector.tensor_scalar(h16[0][:, hs, :], h32[:, hs, :], SH, None, ALU.mult).then_inc(s_ha, 1)
                            dve.wait_ge(s_ha, i * (FO // 2) + (q + 1))
                            nc.vector.scalar_tensor_tensor(out=h16[1][:, hs, :], in0=h32[:, hs, :], scalar=SH,
                                                           in1=h16[0][:, hs, :], op0=ALU.mult, op1=ALU.subtract
                                                           ).then_inc(s_h2, 1)
                        for s in range(2):
                            n = i * 2 + s
                            dve.wait_ge(s_ys, n + 1)
                            dve.wait_ge(s_yd, n + 1)
                            nc.vector.scalar_tensor_tensor(out=yo[:, s, :], in0=bank(4 + s)[:, 0:C],
                                                           scalar=1.0 / (SH * SW), in1=b2s[par][:, :],
                                                           op0=ALU.mult, op1=ALU.add).then_inc(s_yc, 1)
                            dve.wait_ge(s_yc, n + 1)
                            nc.vector.tensor_scalar(yo[:, s, :], yo[:, s, :],
                                                    gates[:, bass.ds(j * 2 + s, 1), bass.ds(pair * 2 + par, 1)], None,
                                                    ALU.mult).then_inc(s_yo, 1)


_INS = ['x', 'L0_conv_W_qkv', 'L0_conv_W_proj', 'L0_conv_W_gp', 'L0_ffn_c_fc_1', 'L0_ffn_c_fc_2', 'L0_ffn_c_proj_1',
        'L0_ffn_c_proj_2', 'L1_ffn_gate_w', 'L1_ffn_gate_b', 'L1_ffn_w1', 'L1_ffn_b1', 'L1_ffn_w2', 'L1_ffn_b2']


def kernel(**inputs):
    import numpy as _np
    import concourse.bacc as _bacc
    from concourse import mybir as _mybir
    from concourse.bass_utils import run_bass_kernel_spmd as _run

    nc = _bacc.Bacc("TRN2", target_bir_lowering=False, num_devices=1)
    arrays, args = {}, []
    for name in _INS:
        a = _np.ascontiguousarray(inputs[name])
        arrays[f"in_{name}_dram"] = a
        args.append(nc.dram_tensor(f"in_{name}_dram", a.shape, _mybir.dt.from_np(a.dtype), kind="ExternalInput").ap())
    args.append(nc.dram_tensor("out_0_dram", (B, HT, WD, C), F32, kind="ExternalOutput").ap())
    build(nc, *args)
    r = _run(nc, [arrays], core_ids=[0])
    return r.results[0]["out_0_dram"]
```

```python
from contextlib import ExitStack

import concourse.bass as bass
from concourse import mybir

F32 = mybir.dt.float32
F16 = mybir.dt.float16
I32 = mybir.dt.int32
U32 = mybir.dt.uint32
ACT = mybir.ActivationFunctionType
ALU = mybir.AluOpType
AX = mybir.AxisListType

P = 128
B, HT, WD, C = 4, 32, 32, 384
N = HT * WD
TOK = B * N
NT = N // P
CC = C // P
NH, HD = 12, 32
NG = 20
OHW = 68
FFN = 1536
FO = FFN // P
KI, KJ = 32, 12
NE = 4
W1, W2 = 5, 20
PADL = W2 // 2
CP = C + W2
BIG = 30000.0
ACT_SET_EXP_LN = 6

SX = 2.0 ** 11
SW = 2.0 ** 10
SATT = 2.0
SZ = 2.0 ** 8
SC1 = 2.0 ** 8
QSCALE = -(HD ** -0.5)

RING = 6
N_T, N_QK, N_V = 2 * CC, 12, NT
OFF_QK = N_T
OFF_V = OFF_QK + N_QK
OFF_G = OFF_V + N_V
OFF_O = OFF_G + 1
SEC1 = OFF_O + 1
OFF_PJ = SEC1
OFF_Z = OFF_PJ + NT
OFF_T3 = OFF_Z + 1
OFF_SC = OFF_T3 + N_T
NRING = OFF_SC + 1
LAG = 2
FLT_MAX = 3.4028234663852886e38

NCST = 21
NW_LOADS = 10
NHI = 2 * N_T + N_QK
NA = 4
NVA = 24
NV = 327
SH = 2.0 ** 8
TT = 256
SEG = TOK + TT
MT = TOK // TT
ROW = C + NE + 1
WCH = CC
CHW = C * FFN // P // WCH
NPW = 2


def hi_count(n):
    if n < OFF_V:
        return n + 1
    return OFF_V + n - OFF_T3 + 1



class Chain:

    def __init__(self, eng, sem):
        self.eng, self.sem, self.base, self.n = eng, sem, 0, 0

    def mark(self, ins):
        ins.then_inc(self.sem, 1)
        self.n += 1
        return self.base + self.n

    def wait(self, value):
        self.eng.wait_ge(self.sem, value)

    def step(self, ins):
        self.wait(self.mark(ins))

    def enter(self, i, each):
        saved = (self.base, self.n, each)
        self.base, self.n = self.base + self.n + i * each, 0
        return saved

    def leave(self, saved, rounds):
        base, n, each = saved
        assert self.n == each, (self.n, each)
        self.base, self.n = base, n + rounds * each


def build(nc, x, W_qkv, W_proj, W_gp, c_fc_1, c_fc_2, c_proj_1, c_proj_2,
          gate_w, gate_b, w1, b1, w2, b2, out):
    x_tok = x.rearrange("b h w c -> (b h w) c")
    x_v = x_tok.rearrange("(b t p) c -> b p t c", p=P, t=NT)
    out_tok = out.rearrange("b h w c -> (b h w) c")

    with ExitStack() as ctx:
        layers = ExitStack()

        def sb(name, shape, dt, stack=None):
            return (stack or layers).enter_context(nc.sbuf_tensor(name, shape, dt))

        def sem(name):
            return ctx.enter_context(nc.semaphore(name))

        def dram(name, shape, dt):
            return nc.dram_tensor(name, shape, dt, kind="Internal").ap()

        qk_d = dram("qk_d", (2, NH, 3, HD, N), F16)
        oh_d = dram("oh_d", (3 * NG, N), F16)
        x3_d = dram("x3_d", (TOK + P, C), F32)
        att_d = dram("att_d", (NH, HD, N), F32)
        xg_d = dram("xg_d", (NE * SEG, ROW), F32)
        w16_d = dram("w16_d", (2, 2, NE, WCH, P, CHW), F16)

        ident16 = sb("ident16", [P, P], F16, ctx)
        desc = sb("desc", [P, NG], F32, ctx)
        b1T = sb("b1T", [P, NE * FO], F32, ctx)
        triu = sb("triu", [P, P], F32, ctx)
        ones = sb("ones", [P, P], F32, ctx)
        rout = sb("rout", [P, NT, ROW], F32, ctx)
        sc = sb("sc", [P, NT, NE], F32, ctx)
        prob = sb("prob", [P, NT, NE], F32, ctx)
        oh1 = sb("oh1", [P, NT, NE], F32, ctx)
        oh2 = sb("oh2", [P, NT, NE], F32, ctx)
        mask = sb("mask", [P, NT, NE], F32, ctx)
        pos = sb("pos", [P, NT, NE], F32, ctx)
        cum = [sb(f"cum{i}", [P, NT, NE], F32, ctx) for i in range(2)]
        red = sb("red", [P, NT], F32, ctx)
        slots = sb("slots", [P, NT, 2], I32, ctx)
        tok = sb("tok", [P, NT], F32, ctx)
        seg = sb("seg", [P, NE], F32, ctx)
        run = sb("run", [P, NE], F32, ctx)
        thr = sb("thr", [P, MT], F32, ctx)
        over = sb("over", [P, NE, MT], F32, ctx)
        tiles = sb("tiles", [P, NE], F32, ctx)
        tb = sb("tb", [P, NE + 1], F32, ctx)
        tbi = sb("tbi", [P, NE + 1], I32, ctx)
        cti = sb("cti", [P, NE], I32, ctx)
        pq = sb("pq", [P, TT // P], F32, ctx)
        padf = sb("padf", [P, NE, TT // P], F32, ctx)
        pads = sb("pads", [P, NE, TT // P], I32, ctx)
        padrow = sb("padrow", [P, ROW], F32, ctx)
        ident = sb("ident", [P, P], F32)
        band = sb("band", [P, P], F32)
        cnt = sb("cnt", [P, 1], F32)
        wqT = [sb(f"wqT{i}", [P, CC, 3 * C], F16) for i in range(2)]
        wpT = [sb(f"wpT{i}", [P, CC, C], F16) for i in range(2)]
        gpT = [sb(f"gpT{i}", [P, CC, NG], F16) for i in range(2)]
        gw16 = [sb(f"gw16_{i}", [P, CC, NE], F16) for i in range(2)]
        c1s = sb("c1s", [3 * KI, FFN], F16)
        cp1T = sb("cp1T", [P, FO, KI], F32)
        c2b = sb("c2b", [P, KJ], F32)
        cp2b = sb("cp2b", [P, KJ], F32)
        gbb = sb("gbb", [P, NE], F32)
        gwn = sb("gwn", [P, CC, NE], F32)
        xb = sb("xb", [P, NT, C], F32)
        xn = sb("xn", [P, NT, C], F32)
        at = sb("at", [P, NT, C], F32)
        xT = [sb(f"xT{i}", [P, CC, N], F16) for i in range(2)]
        stg = [sb(f"stg{i}", [P, 6, N], F16) for i in range(2)]
        va = sb("va", [P, NT, C], F32)
        qs = [sb(f"qs{i}", [P, N], F16) for i in range(2)]
        ks = [sb(f"ks{i}", [P, N], F16) for i in range(2)]
        E = sb("E", [P, NT, N], F32)
        oT = [sb(f"oT{i}", [P, N // 4], F32) for i in range(2)]
        vp = sb("vp", [P, NT, HD], F32)
        ohn = sb("ohn", [P, NT, OHW], F16)
        ohT = sb("ohT", [OHW, N], F16)
        znat = sb("znat", [P, NT, 3 * KI], F16)
        zT = sb("zT", [3 * KI, N], F16)
        st6 = sb("st6", [P, NT, 6], F32)
        mv = sb("mv", [P, NT, 2], F32)
        ve = sb("ve", [P, NT], F32)
        lnv = sb("lnv", [P, NT], F32)
        y0 = sb("y0", [P, NT], F32)
        nt1 = sb("nt1", [P, NT], F32)
        rs = sb("rs", [P, NT], F32)
        gws = sb("gws", [P, NT, NG], F32)
        gwe = sb("gwe", [P, NT, NG], F32)
        gm = sb("gm", [P, NT], F32)
        zz = sb("zz", [P, NT, KI], F32)
        zs = sb("zs", [P, NT, KI], F32)
        mn = [sb(f"mn{i}", [P, NT], F32) for i in range(2)]
        rsum = [sb(f"rsum{i}", [P, NT], F32) for i in range(2)]
        lnr = [sb(f"lnr{i}", [P, NT], F32) for i in range(2)]
        Lf = sb("Lf", [P, NT], F32)
        Ld = sb("Ld", [P, NT], F32)
        Lsp = sb("Lsp", [P, NT, 3], F16)
        csum = sb("csum", [P, NT], F32)
        cr = sb("cr", [P, NT], F32)
        wc = sb("wc", [P, CHW], F32)
        wch = [sb(f"wch{i}", [P, CHW], F16) for i in range(2)]

        layers.close()
        w1s = [[sb(f"w1s{i}{j}", [P, WCH, CHW], F16, ctx) for j in range(2)] for i in range(2)]
        w2s = [[sb(f"w2s{i}{j}", [P, WCH, CHW], F16, ctx) for j in range(2)] for i in range(2)]
        b2s = [sb(f"b2s{i}", [P, C], F32, ctx) for i in range(2)]
        xin32 = sb("xin", [P, 2, C], F32, ctx)
        meta = sb("meta", [P, 2, NE + 1], F32, ctx)
        xin = xin32[:, :, :].bitcast(F16)
        t16 = rout[:, :, :].bitcast(F16)
        gates = rout[:, :, C:C + NE]
        tT = sb("tT", [P, 2, CC, TT], F16, ctx)
        h32 = sb("h32", [P, FO, TT], F32, ctx)
        h16 = [sb(f"h16_{i}", [P, FO, TT], F16, ctx) for i in range(2)]
        yo = sb("yo", [P, 2, C], F32, ctx)

        ps = [ctx.enter_context(nc.psum_tensor(f"ps{i}", [P, 2, 512], F32)) for i in range(4)]

        def bank(i):
            return ps[i // 2][:, i % 2, :]

        def bank16(i):
            return bank(i).bitcast(F16)

        attT = at[:, :, :].rearrange("p t c -> p (t c)").rearrange("p (c n) -> p c n", c=CC)
        uT = oT[0]
        Ef = E[:, :, :].rearrange("p t n -> p (t n)")
        wnat = Ef[:, 0:9 * C].rearrange("p (o c) -> p o c", o=9)
        pnat = Ef[:, 9 * C:12 * C].rearrange("p (o c) -> p o c", o=3)
        gnat = Ef[0:NG, 12 * C:13 * C]
        fnat = Ef[:, 13 * C:14 * C].rearrange("p (o i) -> p o i", o=FO)
        f16n = Ef[:, 14 * C:14 * C + FO * 48].bitcast(F16).rearrange("p (o i) -> p o i", o=FO)
        cpn = Ef[0:KI, 16 * C:20 * C]
        bnat = Ef[0:NE * FO, 20 * C:20 * C + P]
        CB = 2 * 2 * CP
        boxA = [Ef[:, i * CB:(i + 1) * CB].rearrange("p (q t c) -> p q t c", q=2, t=2) for i in range(2)]
        boxX = Ef[:, 2 * CB:3 * CB].rearrange("p (q t c) -> p q t c", q=2, t=2)
        boxY = Ef[:, 3 * CB:4 * CB].rearrange("p (q t c) -> p q t c", q=2, t=2)
        hT = E

        prep_items = []
        for c in range(CC):
            for o0, o1 in ((0, 4), (4, 8), (8, 9)):
                prep_items.append(([w[:, c, o0 * P:o1 * P] for w in wqT], bank(len(prep_items) % RING)[:, 0:(o1 - o0) * P]))
        for c in range(CC):
            prep_items.append(([w[:, c, :] for w in wpT], bank(len(prep_items) % RING)[:, 0:C]))
        prep_items.append(([w[:, :, :].rearrange("p c g -> p (c g)") for w in gpT],
                           bank(len(prep_items) % RING)[:, 0:CC * NG]))

        s_wld = sem("s_wld")
        s_cst = sem("s_cst")
        s_pt = sem("s_pt")
        s_ph = sem("s_ph")
        s_pf = sem("s_pf")
        s_f16 = sem("s_f16")
        s_xb = sem("s_xb")
        s_xn = sem("s_xn")
        s_ve = sem("s_ve")
        s_y0 = sem("s_y0")
        s_pe = sem("s_pe")
        s_hi = sem("s_hi")
        s_fr = sem("s_fr")
        s_stg = sem("s_stg")
        s_oh = sem("s_oh")
        s_qk = [sem("s_qk0"), sem("s_qk1")]
        s_s1 = sem("s_s1")
        s_mx = sem("s_mx")
        s_e1 = sem("s_e1")
        s_ln = sem("s_ln")
        s_lf = sem("s_lf")
        s_lt = sem("s_lt")
        s_lr = sem("s_lr")
        s_s2 = sem("s_s2")
        s_e2 = sem("s_e2")
        s_vp = sem("s_vp")
        s_pv = sem("s_pv")
        s_ev = sem("s_ev")
        s_od = [sem("s_od0"), sem("s_od1")]
        s_at = sem("s_at")
        s_ah = sem("s_ah")
        s_al = sem("s_al")
        s_ut = sem("s_ut")
        s_un = sem("s_un")
        s_z = sem("s_z")
        s_h = sem("s_h")
        s_gl = sem("s_gl")
        s_u = sem("s_u")
        s_y2 = sem("s_y2")
        s_cv = sem("s_cv")
        s_sq = sem("s_sq")
        s_pad = sem("s_pad")
        s_bx = sem("s_bx")
        s_th = sem("s_th")
        s_tl = sem("s_tl")
        s_st = sem("s_st")
        s_d5 = sem("s_d5")
        s_pv0 = sem("s_pv0")
        s_v = sem("s_v")
        s_a = sem("s_a")
        s_wc = sem("s_wc")
        s_wp = sem("s_wp")
        s_wl = sem("s_wl")
        s_pw = sem("s_pw")
        s_sw = sem("s_sw")
        s_ws = sem("s_ws")
        s_ge = sem("s_ge")
        s_gs = sem("s_gs")
        s_gc = sem("s_gc")
        s_mk = sem("s_mk")
        s_rk = sem("s_rk")
        s_rt = sem("s_rt")
        s_sc = sem("s_sc")
        s_td = sem("s_td")
        s_tb = sem("s_tb")
        s_mt = sem("s_mt")
        s_end = sem("s_end")
        s_ew = [sem("s_ew0"), sem("s_ew1")]
        s_xi = sem("s_xi")
        s_xt = sem("s_xt")
        s_xe = sem("s_xe")
        s_h1 = sem("s_h1")
        s_hg = sem("s_hg")
        s_ha = sem("s_ha")
        s_h2 = sem("s_h2")
        s_ys = sem("s_ys")
        s_yc = sem("s_yc")
        s_yo = sem("s_yo")
        s_yd = sem("s_yd")
        s_ya = sem("s_ya")

        NSTG = 19
        NXN = NT + 2

        block = ctx.enter_context(nc.Block())

        @block.sync
        def _(sp):
            sp.dma_start(wnat, W_qkv.rearrange("(o p) c -> p o c", p=P)).then_inc(s_wld, 16)
            sp.dma_start(pnat, W_proj.rearrange("(o p) c -> p o c", p=P)).then_inc(s_wld, 16)
            sp.dma_start(gnat, W_gp).then_inc(s_wld, 16)
            sp.dma_start(fnat, c_fc_1.rearrange("(o p) i -> p o i", p=P)).then_inc(s_wld, 16)
            sp.dma_start(cpn, c_proj_1).then_inc(s_wld, 16)
            sp.dma_start(gwn[:, :, :], gate_w.rearrange("(c p) e -> p c e", p=P)).then_inc(s_wld, 16)
            sp.dma_start(c2b[:, :], c_fc_2.to_broadcast([P, KJ])).then_inc(s_wld, 16)
            sp.dma_start(cp2b[:, :], c_proj_2.rearrange("j a -> a j").to_broadcast([P, KJ])).then_inc(s_wld, 16)
            sp.dma_start(gbb[:, :], gate_b.rearrange("(a e) -> a e", a=1).to_broadcast([P, NE])).then_inc(s_wld, 16)

            sp.dma_start(bnat, b1.rearrange("e (o p) -> (e o) p", p=P)).then_inc(s_wld, 16)

            def load_x(b):
                sp.dma_start(xb[:, :, :], x_v[b]).then_inc(s_xb, 16)

            def load_head(b, h, par, mask):
                for dst, src in ((qs[par][0:3 * HD, :], qk_d[0, h]), (ks[par][0:3 * HD, :], qk_d[1, h])):
                    sp.dma_start(dst, src.rearrange("r d n -> (r d) n")).then_inc(s_qk[par], 16)
                sp.dma_start(qs[par][3 * HD + 3:3 * HD + 3 + NG, :], oh_d[0:NG, :]).then_inc(s_qk[par], 16)
                sp.dma_start(ks[par][3 * HD + 3:3 * HD + 3 + NG, :], oh_d[(1 + mask) * NG:(2 + mask) * NG, :]
                             ).then_inc(s_qk[par], 16)

            for par in range(2):
                sp.sem_inc(s_od[par], 16)
            with sp.Fori(0, B) as b:
                load_x(b)
                for j in range(6):
                    sp.wait_ge(s_fr, b * NRING + (1 + OFF_QK + 2 * j + 2))
                    qk, h0 = j // 3, 4 * (j % 3)
                    for r, part in enumerate((0, 0, 1) if qk == 0 else (0, 1, 0)):
                        sp.dma_start(qk_d[qk, h0:h0 + 4, r], stg[part][:, j, :]).then_inc(s_stg, 16)
                sp.wait_ge(s_fr, b * NRING + (1 + OFF_O + 1))
                sp.dma_start(oh_d, ohT[0:3 * NG, :]).then_inc(s_stg, 16)
                sp.wait_ge(s_stg, b * (16 * NSTG) + 16 * NSTG)
                def store_head(h, par):
                    sp.wait_ge(s_ev, b * NH + h + 1)
                    sp.dma_start(att_d[h].rearrange("d (j n) -> j d n", j=4), oT[par][:, :]).then_inc(s_od[par], 16)

                load_head(b, 0, 0, 0)
                load_head(b, 1, 1, 0)
                for mask in range(2):
                    with sp.Fori(0, 2 if mask == 0 else 3) as i:
                        for par in range(2):
                            h = i * 2 + (par + (2 if mask == 0 else 6))
                            sp.wait_ge(s_s2, b * (NH * NT) + (h - 1) * NT)
                            sp.sem_inc(s_sw, 1)
                            load_head(b, h, par, mask)
                            store_head(h - 2, par)
                store_head(NH - 2, 0)
                store_head(NH - 1, 1)
                for par in range(2):
                    sp.wait_ge(s_od[par], 16 + b * (16 * NH // 2) + 16 * NH // 2)
                sp.dma_start(attT, att_d.rearrange("(c h) d n -> (h d) c n", c=CC)).then_inc(s_at, 16)
                sp.wait_ge(s_bx, (b + 1) * 4)
                sp.dma_start(x3_d[0:TOK].rearrange("(b t p) c -> b p t c", p=P, t=NT)[b], xb[:, :, :]).then_inc(s_st, 16)
                sp.wait_ge(s_xn, b * NXN + NXN)
                sp.wait_ge(s_st, b * 16 + 16)
                sp.sem_inc(s_sw, 1)
            sp.wait_ge(s_td, B + 2)
            xg_v = xg_d.rearrange("(m s p) c -> m p s c", s=2, p=P)

            def load_tile(m):
                sp.dma_start(xin32[:, :, :], xg_v[m, :, :, 0:C]).then_inc(s_xi, 16)

            with sp.Fori(0, NE) as e:
                first = sp.value_load(tbi[0:1, bass.ds(e, 1)], min_val=0, max_val=NE * MT)
                count = sp.value_load(cti[0:1, bass.ds(e, 1)], min_val=1, max_val=MT)
                with sp.Fori(0, count) as j:
                    i, m = first + j, e * (SEG // TT) + j
                    sp.wait_ge(s_xt, i + 1)
                    load_tile(m)
                    sp.wait_ge(s_yd, i * 2 + 2)
                    sp.dma_start(meta[:, :, :], xg_v[m, :, :, C:ROW]).then_inc(s_mt, 16)
            end = sp.value_load(tbi[0:1, NE:NE + 1], min_val=0, max_val=NE * MT)
            sp.wait_ge(s_xt, end + 1)
            sp.sem_inc(s_sw, 1)
            load_tile(0)
            sp.wait_ge(s_xi, end * 16 + 16)
            sp.sem_inc(s_sw, 1)
            sp.wait_ge(s_end, 1)
            sp.dma_start(out_tok, x3_d[0:TOK]).then_inc(s_st, 16)
            sp.wait_ge(s_st, B * 16 + 16)

        @block.gpsimd
        def _(pool):
            ch = Chain(pool, s_cst)
            ch.mark(pool.memset(ident[:, :], 0.0))
            ch.mark(pool.memset(ident16[:, :], 0.0))
            ch.step(pool.memset(band[:, :], 1.0))
            for m in (ident, ident16):
                ch.step(pool.affine_select(out=m[:, :], in_=m[:, :], compare_op=ALU.not_equal, fill=1.0, base=0,
                                           pattern=[[-1, P]], channel_multiplier=1))
            for base, step, cm in ((W1 // 2, -1, 1), (W1 // 2, 1, -1)):
                ch.step(pool.affine_select(out=band[:, :], in_=band[:, :], compare_op=ALU.is_ge, fill=0.0, base=base,
                                           pattern=[[step, P]], channel_multiplier=cm))
            bv = band[:, :].rearrange("p (a w) -> p a w", w=WD)
            for base, step, cm in ((0, -WD, 1), (WD - 1, WD, -1)):
                ch.step(pool.affine_select(out=bv, in_=bv, compare_op=ALU.is_ge, fill=0.0, base=base,
                                           pattern=[[step, P // WD], [0, WD]], channel_multiplier=cm))
            ch.step(pool.iota(desc[:, :], pattern=[[-1, NG]], base=KI, channel_multiplier=0,
                              allow_small_or_imprecise_dtypes=True))
            for i in range(2):
                ch.step(pool.memset(ks[i][3 * HD:3 * HD + 3, :], 1.0))
            ch.mark(pool.memset(ones[:, :], 1.0))
            ch.step(pool.memset(triu[:, :], 1.0))
            ch.step(pool.affine_select(out=triu[:, :], in_=triu[:, :], compare_op=ALU.is_ge, fill=0.0, base=-1,
                                       pattern=[[1, P]], channel_multiplier=-1))
            for dst, pattern, cm in ((tok, [[P, NT]], 1), (seg, [[SEG, NE]], 0), (thr, [[TT, MT]], 0),
                                     (pq, [[P, TT // P]], 1)):
                ch.mark(pool.iota(dst[:, :], pattern=pattern, base=0, channel_multiplier=cm,
                                  allow_small_or_imprecise_dtypes=True))
            ch.step(pool.memset(padrow[:, :], 0.0))
            ch.step(pool.iota(padrow[:, :].bitcast(I32)[:, ROW - 1:ROW], pattern=[[0, 1]], base=TOK,
                              channel_multiplier=1))
            assert ch.n == NCST
            pool.dma_start(x3_d[TOK:TOK + P], padrow[:, 0:C]).then_inc(s_sc, 16)

            def wait_alone(semaphore, value, carrier=s_pw):
                pool.wait_ge(semaphore, value)
                pool.sem_inc(carrier, 1)

            pool.sem_inc(s_yd, 2)
            pool.sem_inc(s_td, 1)
            ch = Chain(pool, s_wp)
            for k, src in enumerate((w1.rearrange("e (c p) f -> (e c) p f", p=P),
                                     w2.rearrange("e (g o p) d -> (e g) p o d", p=P, o=FO // WCH))):
                with pool.Fori(0, NE * WCH) as m:
                    done = m + k * NE * WCH
                    saved = ch.enter(m, NPW)
                    pool.dma_start(wc[:, :] if k == 0 else wc[:, :].rearrange("p (o d) -> p o d", o=FO // WCH),
                                   src[m]).then_inc(s_wc, 16)
                    wait_alone(s_wc, done * 16 + 16)
                    wait_alone(s_wp, ch.mark(pool.tensor_scalar(wc[:, :], wc[:, :], SW, None, ALU.mult)))
                    wait_alone(s_wp, ch.mark(pool.tensor_copy(wch[0][:, :], wc[:, :])))
                    pool.tensor_tensor(wch[1][:, :], wc[:, :], wch[0][:, :], ALU.subtract).then_inc(s_wl, 1)
                    wait_alone(s_wl, done + 1)
                    for j in range(2):
                        pool.dma_start(w16_d[k, j].rearrange("e g p w -> (e g) p w")[m], wch[j][:, :]).then_inc(s_ws, 16)
                    wait_alone(s_ws, done * 32 + 32)
                ch.leave(saved, NE * WCH)

            def scatter(index, rows):
                pool.indirect_dma_start(out=xg_d, out_offset=bass.IndirectOffsetOnAxis(ap=index, axis=0), in_=rows,
                                        in_offset=None).then_inc(s_sc, 16)

            with pool.Fori(0, B) as b:
                wait_alone(s_rt, b + 1)
                for t in range(NT):
                    for k in range(2):
                        scatter(slots[:, t, k:k + 1], rout[:, t, :])
                wait_alone(s_sc, b * (2 * NT * 16) + 16 + 2 * NT * 16)
                pool.sem_inc(s_td, 1)
            pool.wait_ge(s_tb, 1)
            for e in range(NE):
                for q in range(TT // P):
                    scatter(pads[:, e, q:q + 1], padrow[:, :])
            pool.wait_ge(s_sc, 16 * (1 + B * 2 * NT + NE * (TT // P)))
            pool.wait_ge(s_st, B * 16)
            pool.wait_ge(s_ws, 2 * NE * WCH * 32)
            pool.sem_inc(s_td, 1)

            total = pool.value_load(tbi[0:1, NE:NE + 1], min_val=0, max_val=NE * MT)
            with pool.Fori(0, total) as i:
                for s in range(2):
                    wait_alone(s_yo, i * 2 + (s + 1))
                    pool.indirect_dma_start(
                        out=x3_d, out_offset=bass.IndirectOffsetOnAxis(
                            ap=meta[:, :, :].bitcast(I32)[:, s, NE:NE + 1], axis=0),
                        in_=yo[:, s, :], in_offset=None, compute_op=ALU.add).then_inc(s_ya, 16)
                    wait_alone(s_ya, i * 32 + (s + 1) * 16, s_yd)
            pool.sem_inc(s_end, 1)

        @block.scalar
        def _(act):
            def table():
                act.add_instruction(mybir.InstLoadActFuncSet(
                    name=nc.get_next_instruction_name(), act_func_set_id=ACT_SET_EXP_LN, ins=[], outs=[]))

            table()
            for n, (dst, src) in enumerate(prep_items):
                act.wait_ge(s_pt, n + 1)
                nc.scalar.activation(dst[0], src, ACT.Copy, scale=SW).then_inc(s_ph, 1)
            act.wait_ge(s_wld, 16 * NW_LOADS)
            nc.scalar.activation(gw16[0][:, :, :], gwn[:, :, :], ACT.Copy, scale=SW).then_inc(s_ph, 1)

            chs = [0]
            with act.Fori(0, B) as b:
                ch = Chain(act, s_a)
                ch.base = b * NA

                def rsqrt_start(k):
                    act.wait_ge(s_ve, b * 4 + (k + 1))
                    ch.step(nc.scalar.activation(lnv[:, :], ve[:, :], ACT.Ln))
                    nc.scalar.activation(y0[:, :], lnv[:, :], ACT.Exp, scale=-0.5).then_inc(s_y0, 1)

                def hi_item(n, dst, src, scale):
                    act.wait_ge(s_pe, b * NRING + (n + 1))
                    nc.scalar.activation(dst, src, ACT.Copy, scale=scale).then_inc(s_hi, 1)

                rsqrt_start(0)
                for n in range(N_T):
                    hf, c = n // CC, n % CC
                    hi_item(n, xT[0][:, c, hf * 512:(hf + 1) * 512], bank(n % RING), 1.0)
                for n in range(N_QK):
                    j, hf = n // 2, n % 2
                    k = OFF_QK + n
                    hi_item(k, stg[0][:, j, hf * 512:(hf + 1) * 512], bank(k % RING),
                            (QSCALE if j < 3 else 1.0) / (SX * SW))

                def e1(h, par, k):
                    g = b * (NH * NT) + h * NT + k
                    act.wait_ge(s_mx, g + 1)
                    scratch = ps[k % 2][:, :, :].rearrange("p a n -> p (a n)")
                    nc.scalar.activation(scratch, scratch, ACT.Exp,
                                         bias=mn[par][:, k:k + 1], scale=-1.0,
                                         accum_out=rsum[par][:, k:k + 1]).then_inc(s_e1, 1)

                def e2(h, t, first):
                    g = b * (NH * NT) + h * NT + t
                    act.wait_ge(s_s2, g + 1)
                    if not first:
                        act.wait_ge(s_pv, b * (NH * 4) + (h - 1) * 4 + (t // 2 + 1))
                    nc.scalar.activation(E[:, t, :], ps[2][:, :, :].rearrange("p a n -> p (a n)"), ACT.Exp, scale=-1.0,
                                         accum_out=csum[:, t:t + 1]).then_inc(s_e2, 1)

                def ln_rows(h, par):
                    act.wait_ge(s_e1, b * (NH * NT) + (h + 1) * NT)
                    nc.scalar.activation(lnr[par][:, :], rsum[par][:, :], ACT.Ln).then_inc(s_ln, 1)

                def attn(hn, pn, hc, first=False):
                    for k in range(NT + LAG if hc is not None else NT):
                        if k < NT and hn is not None:
                            e1(hn, pn, k)
                        if k == NT and hn is not None:
                            ln_rows(hn, pn)
                        if k >= LAG and hc is not None:
                            e2(hc, k - LAG, first)
                    if hc is None:
                        ln_rows(hn, pn)

                attn(0, 0, None)
                attn(1, 1, 0, first=True)
                with act.Fori(0, 5) as i:
                    attn(i * 2 + 2, 0, i * 2 + 1)
                    attn(i * 2 + 3, 1, i * 2 + 2)
                attn(None, None, NH - 1)

                act.wait_ge(s_at, b * 16 + 16)
                for c in range(CC):
                    nc.scalar.activation(xT[0][:, c, :], attT[:, c, :], ACT.Copy, scale=SATT).then_inc(s_ah, 1)
                rsqrt_start(1)
                for o in range(FO):
                    act.wait_ge(s_h, b * FO + (o + 1))
                    if o >= 4:
                        act.wait_ge(s_u, b * FO + (o - 3))
                    nc.scalar.activation(hT[:, o % 4, :], ps[o % 2][:, :, :].rearrange("p a n -> p (a n)"), ACT.Gelu,
                                         scale=1.0 / (SZ * SC1)).then_inc(s_gl, 1)
                table()
                rsqrt_start(2)
                act.wait_ge(s_xn, b * NXN + (NT + 1))
                for g in range(4):
                    nc.scalar.activation(at[:, 2 * g:2 * g + 2, :], xn[:, 2 * g:2 * g + 2, :], ACT.Square).then_inc(s_y2, 1)
                for t in range(NT):
                    act.wait_ge(s_cv, b * NT + (t + 1))
                    g = t // 2
                    if t % 2 == 0:
                        act.wait_ge(s_pad, b + 1)
                        if g >= 2:
                            act.wait_ge(s_bx, b * 4 + (g - 1))
                    nc.scalar.activation(boxA[g % 2][:, 0, t % 2, PADL:PADL + C], bank(2 * (t % 3))[:, 0:C],
                                         ACT.Square).then_inc(s_sq, 1)
                rsqrt_start(3)
                act.wait_ge(s_xn, b * NXN + NXN)
                act.wait_ge(s_td, b + 1)
                nc.scalar.activation(t16[:, :, 0:C], xn[:, :, :], ACT.Copy).then_inc(s_th, 1)
                for n in range(N_T):
                    hf, c = n // CC, n % CC
                    hi_item(OFF_T3 + n, xT[0][:, c, hf * 512:(hf + 1) * 512], bank(n % RING), 1.0)
                act.wait_ge(s_gs, b + 1)
                nc.scalar.activation(sc[:, :, :], sc[:, :, :], ACT.Exp).then_inc(s_ge, 1)
                assert ch.n == NA

            def load_expert(e):
                for k, ws in enumerate((w1s[e % 2], w2s[e % 2])):
                    for j in range(2):
                        act.dma_start(ws[j][:, :, :], w16_d[k, j, e].rearrange("g p w -> p g w")
                                      ).then_inc(s_ew[e % 2], 16)
                act.dma_start(b2s[e % 2][:, :], b2[e].rearrange("(a c) -> a c", a=1).to_broadcast([P, C])
                              ).then_inc(s_ew[e % 2], 16)

            act.wait_ge(s_td, B + 2)
            load_expert(0)
            for e in range(NE):
                first = act.value_load(tbi[0:1, e:e + 1], min_val=0, max_val=NE * MT)
                end = act.value_load(tbi[0:1, e + 1:e + 2], min_val=0, max_val=NE * MT)
                if e >= 1:
                    act.wait_ge(s_yo, first * 2)
                    act.sem_inc(s_sw, 1)
                if e + 1 < NE:
                    load_expert(e + 1)
                with act.Fori(first, end) as i:
                    for q in range(FO // 2):
                        act.wait_ge(s_h1, i * (FO // 2) + (q + 1))
                        for o in (2 * q, 2 * q + 1):
                            last = nc.scalar.activation(h32[:, o, :], bank(q % 3)[:, (o % 2) * TT:(o % 2 + 1) * TT],
                                                        ACT.Gelu, bias=b1T[:, e * FO + o:e * FO + o + 1],
                                                        scale=1.0 / (SX * SW))
                        last.then_inc(s_hg, 1)

        @block.tensor
        def _(pe):
            pe.wait_ge(s_cst, NCST)
            pe.wait_ge(s_wld, 16 * NW_LOADS)
            n = 0
            for c in range(CC):
                for o0, o1 in ((0, 4), (4, 8), (8, 9)):
                    if n >= RING:
                        pe.wait_ge(s_pf, n - RING + 1)
                    for o in range(o0, o1):
                        last = nc.tensor.transpose(bank(n % RING)[:, (o - o0) * P:(o - o0 + 1) * P],
                                                   wnat[:, o, c * P:(c + 1) * P], ident[:, :])
                    last.then_inc(s_pt, 1)
                    n += 1
            for c in range(CC):
                pe.wait_ge(s_pf, n - RING + 1)
                for o in range(CC):
                    last = nc.tensor.transpose(bank(n % RING)[:, o * P:(o + 1) * P], pnat[:, o, c * P:(c + 1) * P],
                                               ident[:, :])
                last.then_inc(s_pt, 1)
                n += 1
            pe.wait_ge(s_pf, n - RING + 1)
            for c in range(CC):
                last = nc.tensor.transpose(bank(n % RING)[:, c * NG:(c + 1) * NG], gnat[:, c * P:(c + 1) * P],
                                           ident[0:NG, 0:NG])
            last.then_inc(s_pt, 1)
            n += 1
            assert n == len(prep_items)
            pe.wait_ge(s_pf, n - RING + 1)
            for o in range(FO):
                last = nc.tensor.transpose(bank(6)[:, o * KI:(o + 1) * KI], cpn[:, o * P:(o + 1) * P],
                                           ident[0:KI, 0:KI])
            nc.tensor.transpose(bank(7)[:, 0:NE * FO], bnat, ident[0:NE * FO, 0:NE * FO]).then_inc(s_pt, 1)
            pe.wait_ge(s_f16, 1)
            pe.wait_ge(s_pf, n)
            for o in range(FO):
                last = nc.tensor.transpose(bank16(o // 8)[0:3 * KI, (o % 8) * P:(o % 8 + 1) * P], f16n[:, o, :],
                                           ident16[:, :])
            last.then_inc(s_pt, 1)
            pe.wait_ge(s_pf, n + 3)

            with pe.Fori(0, B) as b:
                def ring(k, s0):
                    pe.wait_ge(s_fr, b * NRING + (1 + max(s0, k - RING + 1)))
                    return (k - s0) % RING

                def products(dst, pairs):
                    todo = [(lh[i], rh[j]) for lh, rh in pairs for i, j in ((0, 0), (0, 1), (1, 0))]
                    for m, (lhsT, rhs) in enumerate(todo):
                        last = nc.tensor.matmul(dst, lhsT, rhs, start=(m == 0), stop=(m == len(todo) - 1))
                    return last

                def transposes(s0, k0, src, ready):
                    for n in range(N_T):
                        hf, c = n // CC, n % CC
                        if c == 0:
                            ready(hf)
                        at_bank = bank(ring(k0 + n, s0))
                        for tt in range(4):
                            last = nc.tensor.transpose(at_bank[:, tt * P:(tt + 1) * P],
                                                       src[:, 4 * hf + tt, c * P:(c + 1) * P], ident[:, :])
                        last.then_inc(s_pe, 1)

                transposes(0, 0, xn, lambda hf: pe.wait_ge(s_xn, b * NXN + 4 * (hf + 1)))
                for n in range(N_QK):
                    j, hf = n // 2, n % 2
                    k = OFF_QK + n
                    pe.wait_ge(s_fr, b * NRING + (1 + (hf + 1) * CC))
                    i = ring(k, 0)
                    products(bank(i), [([wqT[a][:, c, j * P:(j + 1) * P] for a in range(2)],
                                        [xT[a][:, c, hf * 512:(hf + 1) * 512] for a in range(2)])
                                       for c in range(CC)]).then_inc(s_pe, 1)
                for t in range(NT):
                    i = ring(OFF_V + t, 0)
                    products(bank(i)[:, 0:C], [([xT[a][:, c, t * P:(t + 1) * P] for a in range(2)],
                                                [wqT[a][:, c, 2 * C:3 * C] for a in range(2)])
                                               for c in range(CC)]).then_inc(s_pe, 1)
                i = ring(OFF_G, 0)
                pe.wait_ge(s_fr, b * NRING + (1 + OFF_QK + 6))
                for t in range(NT):
                    last = products(bank(i)[:, t * 32:t * 32 + NG],
                                    [([stg[a][:, c, t * P:(t + 1) * P] for a in range(2)],
                                      [gpT[a][:, c, :] for a in range(2)]) for c in range(CC)])
                last.then_inc(s_pe, 1)
                i = ring(OFF_O, 0)
                pe.wait_ge(s_oh, b + 1)
                for t in range(NT):
                    last = nc.tensor.transpose(bank16(i)[0:OHW, t * P:(t + 1) * P], ohn[:, t, :], ident16[:, :])
                last.then_inc(s_pe, 1)
                pe.wait_ge(s_fr, b * NRING + (1 + SEC1))

                pv = bank(6)
                lt = bank16(7)

                def quarters(lhsT, rhs, start, stop):
                    for j in range(4):
                        last = nc.tensor.matmul(pv[32 * j:32 * j + 32, 0:N // 4], lhsT,
                                                rhs[:, j * (N // 4):(j + 1) * (N // 4)], start=start, stop=stop)
                    return last

                def p1(h, par, k, half, head0=False):
                    g = b * (NH * NT) + h * NT + k
                    if k == 0:
                        pe.wait_ge(s_qk[par], b * (64 * 6) + half * 64 + 64)
                    if not (head0 and k < 2):
                        pe.wait_ge(s_e1, g - 1)
                    for hf in range(2):
                        last = nc.tensor.matmul(ps[k % 2][:, hf, :], qs[par][0:3 * HD, k * P:(k + 1) * P],
                                                ks[par][0:3 * HD, hf * 512:(hf + 1) * 512], start=True, stop=True)
                    last.then_inc(s_s1, 1)

                def p2(h, par, t, head0=False):
                    g = b * (NH * NT) + h * NT + t
                    if t == 0:
                        pe.wait_ge(s_lr, b * NH + h + 1)
                    if not (head0 and t == 0):
                        pe.wait_ge(s_e2, g)
                    k2 = 3 * HD + 3 + NG
                    for hf in range(2):
                        last = nc.tensor.matmul(ps[2][:, hf, :], ks[par][0:k2, t * P:(t + 1) * P],
                                                qs[par][0:k2, hf * 512:(hf + 1) * 512], start=True, stop=True)
                    last.then_inc(s_s2, 1)

                def lrows(h):
                    pe.wait_ge(s_lf, b * NH + h + 1)
                    for t in range(NT):
                        last = nc.tensor.transpose(lt[0:3, t * P:(t + 1) * P], Lsp[:, t, :], ident16[:, :])
                    last.then_inc(s_lt, 1)

                def pvs(h, u, head0=False):
                    pe.wait_ge(s_vp, b * (NH * 4) + h * 4 + (u + 1))
                    if u == 0 and not head0:
                        pe.wait_ge(s_ev, b * NH + h)
                    for t in (2 * u, 2 * u + 1):
                        last = quarters(vp[:, t, :], E[:, t, :], t == 0, t == NT - 1)
                    last.then_inc(s_pv, 1)

                def attn(hn, pn, hc, pc, hp, half, head0=False):
                    for k in range(NT + LAG):
                        if k < NT and hn is not None:
                            p1(hn, pn, k, half)
                        if k == 0:
                            lrows(hc)
                        if k >= LAG:
                            p2(hc, pc, k - LAG, head0)
                        if k == 1 and hp is not None:
                            pvs(hp, 2)
                        if k == 2 and hp is not None:
                            pvs(hp, 3)
                        if k - LAG == 3:
                            pvs(hc, 0, head0)
                        if k - LAG == 5:
                            pvs(hc, 1)

                for k in range(NT):
                    p1(0, 0, k, 0, head0=True)
                attn(1, 1, 0, 0, None, 0, head0=True)
                with pe.Fori(0, 5) as i:
                    attn(i * 2 + 2, 0, i * 2 + 1, 1, i * 2, i + 1)
                    attn(i * 2 + 3, 1, i * 2 + 2, 0, i * 2 + 1, i + 1)
                attn(None, None, NH - 1, 1, NH - 2, 0)
                pvs(NH - 1, 2)
                pvs(NH - 1, 3)

                pe.wait_ge(s_ev, b * NH + NH)
                pe.wait_ge(s_al, b * CC + CC)
                for t in range(NT):
                    i = ring(OFF_PJ + t, SEC1)
                    products(bank(i)[:, 0:C], [([xT[a][:, c, t * P:(t + 1) * P] for a in range(2)],
                                                [wpT[a][:, c, :] for a in range(2)])
                                               for c in range(CC)]).then_inc(s_pe, 1)
                i = ring(OFF_Z, SEC1)
                pe.wait_ge(s_z, b + 1)
                for t in range(NT):
                    last = nc.tensor.transpose(bank16(i)[0:3 * KI, t * P:(t + 1) * P], znat[:, t, :], ident16[:, :])
                last.then_inc(s_pe, 1)
                pe.wait_ge(s_fr, b * NRING + (1 + OFF_Z + 1))
                for o in range(FO + 1):
                    if o < FO:
                        if o >= 2:
                            pe.wait_ge(s_gl, b * FO + (o - 1))
                        for hf in range(2):
                            last = nc.tensor.matmul(ps[o % 2][:, hf, :], c1s[:, o * P:(o + 1) * P],
                                                    zT[:, hf * 512:(hf + 1) * 512], start=True, stop=True)
                        last.then_inc(s_h, 1)
                    if o >= 1:
                        pe.wait_ge(s_gl, b * FO + o)
                        quarters(cp1T[:, o - 1, :], hT[:, (o - 1) % 4, :], o == 1, o == FO).then_inc(s_u, 1)
                pe.wait_ge(s_ut, b + 1)
                for s in range(2):
                    last = nc.tensor.transpose(bank(7)[:, s * P:(s + 1) * P], uT[:, s * P:(s + 1) * P], ident[:, :])
                last.then_inc(s_un, 1)
                pe.wait_ge(s_xn, b * NXN + (NT + 1))
                for t in range(NT):
                    pe.wait_ge(s_y2, b * 4 + (t // 2 + 1))
                    if t >= 3:
                        pe.wait_ge(s_sq, b * NT + (t - 2))
                        pe.wait_ge(s_d5, b * NT + (t - 2))
                    nc.tensor.matmul(bank(2 * (t % 3))[:, 0:C], band[:, :], xn[:, t, :], start=True, stop=True)
                    nc.tensor.matmul(bank(2 * (t % 3) + 1)[:, 0:C], band[:, :], at[:, t, :], start=True, stop=True
                                     ).then_inc(s_cv, 1)
                transposes(OFF_T3, OFF_T3, xn, lambda hf: pe.wait_ge(s_xn, b * NXN + NXN))
                i = ring(OFF_SC, OFF_T3)
                pe.wait_ge(s_fr, b * NRING + (1 + OFF_T3 + N_T))
                for t in range(NT):
                    last = products(bank(i)[:, t * NE:(t + 1) * NE],
                                    [([xT[a][:, c, t * P:(t + 1) * P] for a in range(2)],
                                      [gw16[a][:, c, :] for a in range(2)]) for c in range(CC)])
                last.then_inc(s_pe, 1)
                pe.wait_ge(s_mk, b + 1)
                for m, bk in ((triu, 6), (ones, 7)):
                    last = nc.tensor.matmul(bank(bk)[:, 0:NT * NE], m[:, :], mask[:, :, :].rearrange("p t e -> p (t e)"),
                                            start=True, stop=True)
                last.then_inc(s_rk, 1)

            pe.wait_ge(s_tb, 1)

            def transpose_tile(m):
                pe.wait_ge(s_xi, m * 16 + 16)
                for s in range(2):
                    for c in range(CC):
                        for th in range(2):
                            last = nc.tensor.transpose(bank16(6 + s)[:, c * TT + th * P:c * TT + (th + 1) * P],
                                                       xin[:, th, s * C + c * P:s * C + (c + 1) * P], ident16[:, :])
                last.then_inc(s_xt, 1)

            pe.sem_inc(s_xt, 1)
            transpose_tile(0)
            with pe.Fori(0, NE // 2) as pair:
                for par in range(2):
                    pe.wait_ge(s_ew[par], pair * 80 + 80)
                    pe.sem_inc(s_pw, 1)
                    first = pe.value_load(tbi[0:1, bass.ds(pair * 2 + par, 1)], min_val=0, max_val=NE * MT)
                    end = pe.value_load(tbi[0:1, bass.ds(pair * 2 + (par + 1), 1)], min_val=0, max_val=NE * MT)
                    with pe.Fori(first, end) as i:
                        pe.wait_ge(s_xe, i * 2 + 2)
                        for q in range(FO // 2):
                            if q >= 3:
                                pe.wait_ge(s_hg, i * (FO // 2) + (q - 2))
                            for o in (2 * q, 2 * q + 1):
                                todo = [(a, c2, c) for c in range(CC) for a, c2 in ((0, 0), (1, 0), (0, 1))]
                                for m, (a, x_, c) in enumerate(todo):
                                    last = nc.tensor.matmul(bank(q % 3)[:, (o % 2) * TT:(o % 2 + 1) * TT],
                                                            w1s[par][a][:, c, o * P:(o + 1) * P], tT[:, x_, c, :],
                                                            start=(m == 0), stop=(m == len(todo) - 1))
                            last.then_inc(s_h1, 1)
                        transpose_tile(i + 1)
                        for s in range(2):
                            sl = slice(s * P, (s + 1) * P)
                            for o in range(FO):
                                if s == 0 and o % 2 == 0:
                                    pe.wait_ge(s_h2, i * (FO // 2) + (o // 2 + 1))
                                for m, (a, w_) in enumerate(((0, 0), (0, 1), (1, 0))):
                                    g, r = o // (FO // WCH), o % (FO // WCH)
                                    last = nc.tensor.matmul(bank(4 + s)[:, 0:C], h16[a][:, o, sl],
                                                            w2s[par][w_][:, g, r * C:(r + 1) * C],
                                                            start=(o == 0 and m == 0), stop=(o == FO - 1 and m == 2))
                            last.then_inc(s_ys, 1)

        @block.vector
        def _(dve):
            dve.sem_inc(s_fr, 1)
            ch = Chain(dve, s_pv0)
            dve.wait_ge(s_cst, NCST)
            nc.vector.reduce_sum(cnt[:, :], band[:, :], AX.X)
            nc.vector.memset(ohn[:, :, 3 * NG:OHW], 0.0)
            for n, (dst, src) in enumerate(prep_items):
                dve.wait_ge(s_ph, n + 1)
                nc.vector.scalar_tensor_tensor(out=dst[1], in0=src, scalar=SW, in1=dst[0], op0=ALU.mult,
                                               op1=ALU.subtract).then_inc(s_pf, 1)
                if n == 0:
                    ch.mark(nc.vector.tensor_scalar(f16n[:, :, 0:KI], fnat, SC1, None, ALU.mult))
                    ch.step(nc.vector.tensor_scalar(f16n[:, :, 2 * KI:3 * KI], fnat, SC1, None, ALU.mult))
                    nc.vector.scalar_tensor_tensor(out=f16n[:, :, KI:2 * KI], in0=fnat, scalar=SC1,
                                                   in1=f16n[:, :, 0:KI], op0=ALU.mult,
                                                   op1=ALU.subtract).then_inc(s_f16, 1)
            nc.vector.tensor_copy(run[:, :], seg[:, :])
            np_ = len(prep_items)
            dve.wait_ge(s_ph, np_ + 1)
            nc.vector.scalar_tensor_tensor(out=gw16[1][:, :, :], in0=gwn[:, :, :], scalar=SW, in1=gw16[0][:, :, :],
                                           op0=ALU.mult, op1=ALU.subtract).then_inc(s_pf, 1)
            dve.wait_ge(s_pt, np_ + 1)
            nc.vector.tensor_copy(cp1T[:, :, :].rearrange("p o i -> p (o i)"), bank(6)[:, 0:C])
            nc.vector.tensor_copy(b1T[:, :], bank(7)[:, 0:NE * FO]).then_inc(s_pf, 1)
            dve.wait_ge(s_pt, np_ + 2)
            nc.vector.tensor_copy(c1s[:, 0:1024], bank16(0)[0:3 * KI, :])
            nc.vector.tensor_copy(c1s[:, 1024:FFN], bank16(1)[0:3 * KI, 0:512]).then_inc(s_pf, 1)

            with dve.Fori(0, B) as b:
                ch = Chain(dve, s_v)
                ch.base = b * NV

                def layer_stats(k, eps, scale):
                    for t in range(NT):
                        m = ch.mark(nc.vector.bn_stats(st6[:, t, :], xb[:, t, :]))
                    ch.wait(m)
                    nc.vector.memset(nt1[:, :], 0.0)
                    for t in range(NT):
                        m = ch.mark(nc.vector.bn_aggr(mv[:, t, :], st6[:, t, :]))
                    ch.wait(m)
                    nc.vector.tensor_scalar(ve[:, :], mv[:, :, 1], eps, None, ALU.add).then_inc(s_ve, 1)
                    dve.wait_ge(s_y0, b * 4 + (k + 1))
                    ch.step(nc.vector.tensor_tensor(nt1[:, :], y0[:, :], y0[:, :], ALU.mult))
                    ch.step(nc.vector.tensor_tensor(nt1[:, :], nt1[:, :], ve[:, :], ALU.mult))
                    ch.step(nc.vector.tensor_scalar(nt1[:, :], nt1[:, :], -0.5 * scale, 1.5 * scale, ALU.mult, ALU.add))
                    ch.step(nc.vector.tensor_tensor(rs[:, :], nt1[:, :], y0[:, :], ALU.mult))

                def normalise(t):
                    return nc.vector.tensor_scalar(xn[:, t, :], xb[:, t, :], mv[:, t, 0:1], rs[:, t:t + 1],
                                                   ALU.subtract, ALU.mult)

                def lo_item(n, dst, src, hi, scale):
                    dve.wait_ge(s_hi, b * NHI + hi_count(n))
                    nc.vector.scalar_tensor_tensor(out=dst, in0=src, scalar=scale, in1=hi, op0=ALU.mult,
                                                   op1=ALU.subtract).then_inc(s_fr, 1)

                def lo_transposed(k0, scale):
                    for n in range(N_T):
                        hf, c = n // CC, n % CC
                        lo_item(k0 + n, xT[1][:, c, hf * 512:(hf + 1) * 512], bank(n % RING),
                                xT[0][:, c, hf * 512:(hf + 1) * 512], scale)

                dve.wait_ge(s_xb, b * 16 + 16)
                layer_stats(0, 1e-6, SX)
                for t in range(NT):
                    normalise(t).then_inc(s_xn, 1)
                lo_transposed(0, 1.0)
                for n in range(N_QK):
                    j, hf = n // 2, n % 2
                    k = OFF_QK + n
                    sl = slice(hf * 512, (hf + 1) * 512)
                    lo_item(k, stg[1][:, j, sl], bank(k % RING), stg[0][:, j, sl], (QSCALE if j < 3 else 1.0) / (SX * SW))
                for t in range(NT):
                    k = OFF_V + t
                    dve.wait_ge(s_pe, b * NRING + (k + 1))
                    nc.vector.tensor_scalar(va[:, t, :], bank(k % RING)[:, 0:C], 1.0 / (SX * SW), None, ALU.mult
                                            ).then_inc(s_fr, 1)
                dve.wait_ge(s_pe, b * NRING + (OFF_G + 1))
                g3 = bank(OFF_G % RING)[:, 0:NT * 32].rearrange("p (t g) -> p t g", g=32)[:, :, 0:NG]
                cp = nc.vector.tensor_copy(gws[:, :, :], g3)
                cp.then_inc(s_fr, 1)
                dve.wait_ge(s_fr, b * NRING + (1 + OFF_G + 1))
                gb = gm[:, :].rearrange("p (t a) -> p t a", a=1).to_broadcast([P, NT, NG])
                db = desc[:, :].rearrange("p (a g) -> p a g", a=1).to_broadcast([P, NT, NG])
                ch.step(nc.vector.tensor_reduce(gm[:, :], gws[:, :, :], axis=AX.X, op=ALU.min))
                ch.step(nc.vector.tensor_tensor(gwe[:, :, :], gws[:, :, :], gb, ALU.is_equal))
                ch.step(nc.vector.tensor_tensor(gwe[:, :, :], gwe[:, :, :], db, ALU.mult))
                ch.step(nc.vector.tensor_reduce(gm[:, :], gwe[:, :, :], axis=AX.X, op=ALU.max))
                ch.step(nc.vector.tensor_tensor(gws[:, :, :], gwe[:, :, :], gb, ALU.is_equal))
                ch.mark(nc.vector.tensor_scalar(ohn[:, :, 0:NG], gws[:, :, :], BIG, None, ALU.mult))
                ch.mark(nc.vector.tensor_scalar(ohn[:, :, NG:2 * NG], gws[:, :, :], -1.0, 1.0, ALU.mult, ALU.add))
                nc.vector.tensor_copy(ohn[:, :, 2 * NG:3 * NG], gws[:, :, :]).then_inc(s_oh, 1)
                dve.wait_ge(s_pe, b * NRING + (OFF_O + 1))
                nc.vector.tensor_copy(ohT[:, :], bank16(OFF_O % RING)[0:OHW, :]).then_inc(s_fr, 1)

                def mx(h, par, k):
                    dve.wait_ge(s_s1, b * (NH * NT) + h * NT + (k + 1))
                    nc.vector.tensor_reduce(mn[par][:, k:k + 1], ps[k % 2][:, :, :].rearrange("p a n -> p (a n)"),
                                            axis=AX.X, op=ALU.min).then_inc(s_mx, 1)

                def values(h, u):
                    sl = slice(2 * u, 2 * u + 2)
                    dve.wait_ge(s_e2, b * (NH * NT) + h * NT + (2 * u + 2))
                    ch.step(nc.vector.tensor_scalar(cr[:, sl], csum[:, sl], 1e-8, None, ALU.add))
                    ch.step(nc.vector.reciprocal(cr[:, sl], cr[:, sl]))
                    nc.vector.tensor_tensor(vp[:, sl, :], va[:, sl, bass.ds(h * HD, HD)],
                                            cr[:, sl].rearrange("p (t a) -> p t a", a=1).to_broadcast([P, 2, HD]),
                                            ALU.mult).then_inc(s_vp, 1)

                def lparts(h, par):
                    dve.wait_ge(s_ln, b * NH + h + 1)
                    ch.step(nc.vector.tensor_tensor(Lf[:, :], lnr[par][:, :], mn[par][:, :], ALU.subtract))
                    ch.step(nc.vector.tensor_copy(Lsp[:, :, 0], Lf[:, :]))
                    ch.step(nc.vector.tensor_tensor(Ld[:, :], Lf[:, :], Lsp[:, :, 0], ALU.subtract))
                    ch.step(nc.vector.tensor_copy(Lsp[:, :, 1], Ld[:, :]))
                    nc.vector.tensor_tensor(Lsp[:, :, 2], Ld[:, :], Lsp[:, :, 1], ALU.subtract).then_inc(s_lf, 1)

                def lcopy(h, par):
                    dve.wait_ge(s_lt, b * NH + h + 1)
                    nc.vector.tensor_copy(qs[par][3 * HD:3 * HD + 3, :], bank16(7)[0:3, :]).then_inc(s_lr, 1)

                def evict(h, par, before):
                    dve.wait_ge(s_pv, b * (NH * 4) + h * 4 + 4)
                    dve.wait_ge(s_od[par], 16 + b * (16 * NH // 2) + before * 16)
                    nc.vector.tensor_copy(oT[par][:, :], bank(6)[:, 0:N // 4]).then_inc(s_ev, 1)

                def attn(hn, pn, hc, pc, hp, before=None):
                    for k in range(NT + LAG):
                        if k < NT and hn is not None:
                            mx(hn, pn, k)
                        if k == 0:
                            lcopy(hc, pc)
                            if hp is not None:
                                values(hp, 3)
                        if k == 3 and hp is not None:
                            evict(hp, 1 - pc, before)
                        if k == NT and hn is not None:
                            lparts(hn, pn)
                        if k - LAG - 1 in (1, 3, 5):
                            values(hc, (k - LAG - 1) // 2)

                for k in range(NT):
                    mx(0, 0, k)
                lparts(0, 0)
                attn(1, 1, 0, 0, None)
                with dve.Fori(0, 5) as i:
                    saved = ch.enter(i, NVA)
                    attn(i * 2 + 2, 0, i * 2 + 1, 1, i * 2, i)
                    attn(i * 2 + 3, 1, i * 2 + 2, 0, i * 2 + 1, i)
                ch.leave(saved, 5)
                attn(None, None, NH - 1, 1, NH - 2, 5)
                values(NH - 1, 3)
                evict(NH - 1, 1, 5)

                for c in range(CC):
                    dve.wait_ge(s_ah, b * CC + (c + 1))
                    nc.vector.scalar_tensor_tensor(out=xT[1][:, c, :], in0=attT[:, c, :], scalar=SATT,
                                                   in1=xT[0][:, c, :], op0=ALU.mult, op1=ALU.subtract).then_inc(s_al, 1)
                for t in range(NT):
                    k = OFF_PJ + t
                    dve.wait_ge(s_pe, b * NRING + (k + 1))
                    nc.vector.scalar_tensor_tensor(out=xb[:, t, :], in0=bank((k - SEC1) % RING)[:, 0:C],
                                                   scalar=1.0 / (SATT * SW), in1=xb[:, t, :], op0=ALU.mult,
                                                   op1=ALU.add).then_inc(s_fr, 1)
                dve.wait_ge(s_fr, b * NRING + (1 + OFF_Z))
                layer_stats(1, 1e-5, SZ)
                for t in range(NT):
                    m = ch.mark(nc.vector.scalar_tensor_tensor(
                        out=xn[:, t, :].rearrange("p (i j) -> p i j", j=KJ),
                        in0=xb[:, t, :].rearrange("p (i j) -> p i j", j=KJ), scalar=mv[:, t, 0:1],
                        in1=c2b[:, :].rearrange("p (a j) -> p a j", a=1).to_broadcast([P, KI, KJ]),
                        op0=ALU.subtract, op1=ALU.mult))
                ch.wait(m)
                ch.step(nc.vector.reduce_sum(zz[:, :, :].rearrange("p t i -> p (t i)"),
                                             xn[:, :, :].rearrange("p t (i j) -> p (t i) j", j=KJ), AX.X))
                ch.step(nc.vector.tensor_tensor(zs[:, :, :], zz[:, :, :],
                                                rs[:, :].rearrange("p (t a) -> p t a", a=1).to_broadcast([P, NT, KI]),
                                                ALU.mult))
                ch.mark(nc.vector.tensor_copy(znat[:, :, KI:2 * KI], zs[:, :, :]))
                ch.step(nc.vector.tensor_copy(znat[:, :, 0:KI], zs[:, :, :]))
                nc.vector.tensor_tensor(znat[:, :, 2 * KI:3 * KI], zs[:, :, :], znat[:, :, 0:KI], ALU.subtract
                                        ).then_inc(s_z, 1)
                dve.wait_ge(s_pe, b * NRING + (OFF_Z + 1))
                nc.vector.tensor_copy(zT[:, :], bank16((OFF_Z - SEC1) % RING)[0:3 * KI, :]).then_inc(s_fr, 1)
                dve.wait_ge(s_u, b * FO + FO)
                nc.vector.tensor_copy(uT[:, :], bank(6)[:, 0:N // 4]).then_inc(s_ut, 1)
                dve.wait_ge(s_un, b + 1)
                for s in range(2):
                    m = ch.mark(nc.vector.tensor_copy(
                        zz[:, :, :].rearrange("p (j s) i -> p s j i", s=2)[:, s],
                        bank(7)[:, s * P:(s + 1) * P].rearrange("p (j i) -> p j i", i=KI)))
                ch.wait(m)
                ch.step(nc.vector.tensor_tensor(
                    at[:, :, :].rearrange("p t (i j) -> p (t i) j", j=KJ),
                    zz[:, :, :].rearrange("p t (i a) -> p (t i) a", a=1).to_broadcast([P, NT * KI, KJ]),
                    cp2b[:, :].rearrange("p (a j) -> p a j", a=1).to_broadcast([P, NT * KI, KJ]), ALU.mult))
                ch.step(nc.vector.tensor_tensor(xb[:, :, :], xb[:, :, :], at[:, :, :], ALU.add))
                for i in range(2):
                    nc.vector.memset(boxA[i][:, :, :, 0:PADL], 0.0)
                    last = nc.vector.memset(boxA[i][:, :, :, PADL + C:CP], 0.0)
                last.then_inc(s_pad, 1)
                layer_stats(2, 1e-6, 1.0)
                for t in range(NT - 1):
                    normalise(t)
                normalise(NT - 1).then_inc(s_xn, 1)
                for g in range(4):
                    A = boxA[g % 2]
                    for t in (2 * g, 2 * g + 1):
                        dve.wait_ge(s_cv, b * NT + (t + 1))
                        nc.vector.tensor_scalar(A[:, 1, t % 2, PADL:PADL + C], bank(2 * (t % 3) + 1)[:, 0:C],
                                                cnt[:, 0:1], None, ALU.mult).then_inc(s_d5, 1)
                    dve.wait_ge(s_sq, b * NT + (2 * g + 2))
                    dve.wait_ge(s_d5, b * NT + (2 * g + 2))
                    dve.wait_ge(s_pad, b + 1)

                    def add(o, a, sa, c, sc, length):
                        ch.step(nc.vector.tensor_tensor(o[:, :, :, 0:length], a[:, :, :, sa:sa + length],
                                                        c[:, :, :, sc:sc + length], ALU.add))

                    add(boxX, A, 0, A, 1, CP - 1)
                    add(boxY, boxX, 0, boxX, 2, CP - 3)
                    add(boxX, boxY, 0, boxY, 4, CP - 7)
                    add(A, boxX, 0, boxX, 8, CP - 15)
                    add(boxX, A, 0, boxY, 16, C)
                    num, den = boxX[:, 0, :, 0:C], boxX[:, 1, :, 0:C]
                    tot, dn, nm = boxY[:, 0, :, 0:C], A[:, 1, :, 0:C], A[:, 0, :, 0:C]
                    xs = xb[:, 2 * g:2 * g + 2, :]
                    ch.step(nc.vector.tensor_tensor(tot, num, den, ALU.add))
                    ch.step(nc.vector.scalar_tensor_tensor(out=dn, in0=tot, scalar=0.0, in1=den, op0=ALU.is_equal,
                                                           op1=ALU.add))
                    ch.step(nc.vector.scalar_tensor_tensor(out=nm, in0=tot, scalar=0.0, in1=num, op0=ALU.is_equal,
                                                           op1=ALU.add))
                    ch.step(nc.vector.reciprocal(dn, dn))
                    ch.step(nc.vector.tensor_tensor(nm, nm, dn, ALU.mult))
                    ch.step(nc.vector.scalar_tensor_tensor(out=xs, in0=nm, scalar=FLT_MAX, in1=xs, op0=ALU.min,
                                                           op1=ALU.add))
                    nc.vector.memset(A[:, :, :, 0:PADL], 0.0).then_inc(s_bx, 1)
                layer_stats(3, 1e-5, SX)
                for t in range(NT - 1):
                    normalise(t)
                normalise(NT - 1).then_inc(s_xn, 1)
                dve.wait_ge(s_th, b + 1)
                nc.vector.tensor_tensor(t16[:, :, C:2 * C], xn[:, :, :], t16[:, :, 0:C], ALU.subtract).then_inc(s_tl, 1)
                lo_transposed(OFF_T3, 1.0)
                dve.wait_ge(s_pe, b * NRING + NRING)
                nc.vector.scalar_tensor_tensor(
                    out=sc[:, :, :], in0=bank((OFF_SC - OFF_T3) % RING)[:, 0:NT * NE].rearrange("p (t e) -> p t e", e=NE),
                    scalar=1.0 / (SX * SW), in1=gbb[:, :].rearrange("p (a e) -> p a e", a=1).to_broadcast([P, NT, NE]),
                    op0=ALU.mult, op1=ALU.add).then_inc(s_fr, 1)
                dve.wait_ge(s_fr, b * NRING + (1 + NRING))

                def rows(v):
                    return v[:, :].rearrange("p (t a) -> p t a", a=1).to_broadcast([P, NT, NE])

                def all_rows(v):
                    return v.rearrange("p (a e) -> p a e", a=1).to_broadcast([P, NT, NE])

                ch.step(nc.vector.tensor_reduce(red[:, :], sc[:, :, :], axis=AX.X, op=ALU.max))
                nc.vector.tensor_tensor(sc[:, :, :], sc[:, :, :], rows(red), ALU.subtract).then_inc(s_gs, 1)
                dve.wait_ge(s_ge, b + 1)
                ch.step(nc.vector.reduce_sum(red[:, :], sc[:, :, :], AX.X))
                ch.step(nc.vector.reciprocal(red[:, :], red[:, :]))
                ch.step(nc.vector.tensor_tensor(prob[:, :, :], sc[:, :, :], rows(red), ALU.mult))
                src = prob
                for k, oh in enumerate((oh1, oh2)):
                    ch.step(nc.vector.tensor_reduce(red[:, :], src[:, :, :], axis=AX.X, op=ALU.max))
                    ch.step(nc.vector.tensor_tensor(oh[:, :, :], src[:, :, :], rows(red), ALU.is_equal))
                    ch.step(nc.vector.tensor_tensor(oh[:, :, :], oh[:, :, :], all_rows(desc[:, 0:NE]), ALU.mult))
                    ch.step(nc.vector.tensor_reduce(red[:, :], oh[:, :, :], axis=AX.X, op=ALU.max))
                    ch.step(nc.vector.tensor_tensor(oh[:, :, :], oh[:, :, :], rows(red), ALU.is_equal))
                    if k == 0:
                        ch.step(nc.vector.scalar_tensor_tensor(out=sc[:, :, :], in0=oh1[:, :, :], scalar=-2.0,
                                                               in1=prob[:, :, :], op0=ALU.mult, op1=ALU.add))
                        src = sc
                nc.vector.tensor_tensor(mask[:, :, :], oh1[:, :, :], oh2[:, :, :], ALU.add).then_inc(s_mk, 1)
                dve.wait_ge(s_mk, b + 1)
                ch.step(nc.vector.tensor_tensor(prob[:, :, :], prob[:, :, :], mask[:, :, :], ALU.mult))
                ch.step(nc.vector.reduce_sum(red[:, :], prob[:, :, :], AX.X))
                ch.step(nc.vector.tensor_scalar(red[:, :], red[:, :], 1e-9, None, ALU.add))
                ch.step(nc.vector.reciprocal(red[:, :], red[:, :]))
                nc.vector.tensor_tensor(gates, prob[:, :, :], rows(red), ALU.mult)
                nc.vector.tensor_copy(rout[:, :, :].bitcast(I32)[:, :, ROW - 1], tok[:, :])
                dve.wait_ge(s_rk, b + 1)
                ch.mark(nc.vector.tensor_scalar(tok[:, :], tok[:, :], float(N), None, ALU.add))
                before, total = [bank(i)[:, 0:NT * NE].rearrange("p (t e) -> p t e", e=NE) for i in (6, 7)]
                ch.step(nc.vector.tensor_copy(cum[0][:, :, :], total))
                ch.step(nc.vector.tensor_tensor(pos[:, :, :], before, cum[0][:, :, :], ALU.subtract))
                old, new = cum
                for d in (1, 2, 4):
                    ch.mark(nc.vector.tensor_tensor(new[:, d:, :], old[:, d:, :], old[:, 0:NT - d, :], ALU.add))
                    ch.step(nc.vector.tensor_copy(new[:, 0:d, :], old[:, 0:d, :]))
                    old, new = new, old
                ch.step(nc.vector.tensor_tensor(pos[:, :, :], pos[:, :, :], old[:, :, :], ALU.add))
                ch.step(nc.vector.tensor_tensor(pos[:, :, :], pos[:, :, :], all_rows(run[:, :]), ALU.add))
                ch.step(nc.vector.tensor_tensor(run[:, :], run[:, :], old[:, NT - 1, :], ALU.add))
                for oh in (oh1, oh2):
                    ch.step(nc.vector.tensor_tensor(oh[:, :, :], oh[:, :, :], pos[:, :, :], ALU.mult))
                ch.step(nc.vector.reduce_sum(red[:, :], oh1[:, :, :], AX.X))
                ch.step(nc.vector.tensor_copy(slots[:, :, 0], red[:, :]))
                ch.step(nc.vector.reduce_sum(red[:, :], oh2[:, :, :], AX.X))
                nc.vector.tensor_copy(slots[:, :, 1], red[:, :]).then_inc(s_rt, 1)
                assert ch.n == NV, ch.n

            ch = Chain(dve, s_gc)
            ch.step(nc.vector.tensor_tensor(tiles[:, :], run[:, :], seg[:, :], ALU.subtract))
            ch.step(nc.vector.tensor_tensor(
                over[:, :, :], tiles[:, :].rearrange("p (e a) -> p e a", a=1).to_broadcast([P, NE, MT]),
                thr[:, :].rearrange("p (a j) -> p a j", a=1).to_broadcast([P, NE, MT]), ALU.is_gt))
            ch.step(nc.vector.reduce_sum(tiles[:, :], over[:, :, :], AX.X))
            ch.step(nc.vector.tensor_scalar(tiles[:, :], tiles[:, :], 1.0, None, ALU.max))
            ch.step(nc.vector.memset(tb[:, :], 0.0))
            for e in range(NE):
                ch.step(nc.vector.tensor_tensor(tb[:, e + 1:e + 2], tb[:, e:e + 1], tiles[:, e:e + 1], ALU.add))
            ch.step(nc.vector.tensor_tensor(
                padf[:, :, :], run[:, :].rearrange("p (e a) -> p e a", a=1).to_broadcast([P, NE, TT // P]),
                pq[:, :].rearrange("p (a q) -> p a q", a=1).to_broadcast([P, NE, TT // P]), ALU.add))
            nc.vector.tensor_copy(pads[:, :, :], padf[:, :, :])
            nc.vector.tensor_copy(cti[:, :], tiles[:, :])
            nc.vector.tensor_copy(tbi[:, :], tb[:, :]).then_inc(s_tb, 1)

            def read_tile(m):
                dve.wait_ge(s_xt, m + 2)
                for s in range(2):
                    nc.vector.tensor_copy(tT[:, s, :, :].rearrange("p c n -> p (c n)"),
                                          bank16(6 + s)[:, 0:CC * TT]).then_inc(s_xe, 1)

            dve.wait_ge(s_tb, 1)
            read_tile(0)
            with dve.Fori(0, NE // 2) as pair:
                for par in range(2):
                    first = dve.value_load(tbi[0:1, bass.ds(pair * 2 + par, 1)], min_val=0, max_val=NE * MT)
                    end = dve.value_load(tbi[0:1, bass.ds(pair * 2 + (par + 1), 1)], min_val=0, max_val=NE * MT)
                    with dve.Fori(first, end) as i:
                        for q in range(FO // 2):
                            dve.wait_ge(s_hg, i * (FO // 2) + (q + 1))
                            hs = slice(2 * q, 2 * q + 2)
                            nc.vector.tensor_scalar(h16[0][:, hs, :], h32[:, hs, :], SH, None, ALU.mult).then_inc(s_ha, 1)
                            dve.wait_ge(s_ha, i * (FO // 2) + (q + 1))
                            nc.vector.scalar_tensor_tensor(out=h16[1][:, hs, :], in0=h32[:, hs, :], scalar=SH,
                                                           in1=h16[0][:, hs, :], op0=ALU.mult, op1=ALU.subtract
                                                           ).then_inc(s_h2, 1)
                        read_tile(i + 1)
                        dve.wait_ge(s_mt, i * 16 + 16)
                        for s in range(2):
                            n = i * 2 + s
                            dve.wait_ge(s_ys, n + 1)
                            dve.wait_ge(s_yd, n + 1)
                            nc.vector.scalar_tensor_tensor(out=yo[:, s, :], in0=bank(4 + s)[:, 0:C],
                                                           scalar=1.0 / (SH * SW), in1=b2s[par][:, :],
                                                           op0=ALU.mult, op1=ALU.add).then_inc(s_yc, 1)
                            dve.wait_ge(s_yc, n + 1)
                            nc.vector.tensor_scalar(yo[:, s, :], yo[:, s, :],
                                                    meta[:, s, bass.ds(pair * 2 + par, 1)], None,
                                                    ALU.mult).then_inc(s_yo, 1)


_INS = ['x', 'L0_conv_W_qkv', 'L0_conv_W_proj', 'L0_conv_W_gp', 'L0_ffn_c_fc_1', 'L0_ffn_c_fc_2', 'L0_ffn_c_proj_1',
        'L0_ffn_c_proj_2', 'L1_ffn_gate_w', 'L1_ffn_gate_b', 'L1_ffn_w1', 'L1_ffn_b1', 'L1_ffn_w2', 'L1_ffn_b2']


def kernel(**inputs):
    import numpy as _np
    import concourse.bacc as _bacc
    from concourse import mybir as _mybir
    from concourse.bass_utils import run_bass_kernel_spmd as _run

    nc = _bacc.Bacc("TRN2", target_bir_lowering=False, num_devices=1)
    arrays, args = {}, []
    for name in _INS:
        a = _np.ascontiguousarray(inputs[name])
        arrays[f"in_{name}_dram"] = a
        args.append(nc.dram_tensor(f"in_{name}_dram", a.shape, _mybir.dt.from_np(a.dtype), kind="ExternalInput").ap())
    args.append(nc.dram_tensor("out_0_dram", (B, HT, WD, C), F32, kind="ExternalOutput").ap())
    build(nc, *args)
    r = _run(nc, [arrays], core_ids=[0])
    return r.results[0]["out_0_dram"]
```

```python
from contextlib import ExitStack

import concourse.bass as bass
from concourse import mybir

F32 = mybir.dt.float32
F16 = mybir.dt.float16
I32 = mybir.dt.int32
U32 = mybir.dt.uint32
ACT = mybir.ActivationFunctionType
ALU = mybir.AluOpType
AX = mybir.AxisListType

P = 128
B, HT, WD, C = 4, 32, 32, 384
N = HT * WD
TOK = B * N
NT = N // P
CC = C // P
NH, HD = 12, 32
NG = 20
OHW = 68
FFN = 1536
FO = FFN // P
KI, KJ = 32, 12
NE = 4
W1, W2 = 5, 20
LW, RW = W2 // 2, W2 - W2 // 2 - 1
BIG = 30000.0
ACT_SET_EXP_LN = 6

SX = 2.0 ** 11
SW = 2.0 ** 10
SATT = 2.0
SZ = 2.0 ** 8
SC1 = 2.0 ** 8
QSCALE = -(HD ** -0.5)

RING = 6
N_T, N_QK, N_V = 2 * CC, 8, 4
N_XK, N_X = 4, 8
OFF_QK = N_T
OFF_G = OFF_QK + N_QK
OFF_V = OFF_G + 1
OFF_O = OFF_V + N_V
SEC1 = OFF_O + 1
OFF_PJ = SEC1
OFF_Z = OFF_PJ + NT
OFF_T3 = OFF_Z + 1
OFF_SC = OFF_T3 + N_T
NRING = OFF_SC + 1
HB = 3
HR = NH // HB
LAG = 4
FLT_MAX = 3.4028234663852886e38

NCST = 28
NW_LOADS = 10
NHI = 2 * N_T + N_QK
NA = 4
NVA = 36
NV = 288
SH = 2.0 ** 8
TT = 256
SEG = TOK + TT
MT = TOK // TT
ROW = C + NE + 1
WCH = CC
CHW = C * FFN // P // WCH
NPW = 2


def hi_count(n):
    if n < OFF_G:
        return n + 1
    return OFF_G + n - OFF_T3 + 1



class Chain:

    def __init__(self, eng, sem):
        self.eng, self.sem, self.base, self.n = eng, sem, 0, 0

    def mark(self, ins):
        ins.then_inc(self.sem, 1)
        self.n += 1
        return self.base + self.n

    def wait(self, value):
        self.eng.wait_ge(self.sem, value)

    def step(self, ins):
        self.wait(self.mark(ins))

    def enter(self, i, each):
        saved = (self.base, self.n, each)
        self.base, self.n = self.base + self.n + i * each, 0
        return saved

    def leave(self, saved, rounds):
        base, n, each = saved
        assert self.n == each, (self.n, each)
        self.base, self.n = base, n + rounds * each


def build(nc, x, W_qkv, W_proj, W_gp, c_fc_1, c_fc_2, c_proj_1, c_proj_2,
          gate_w, gate_b, w1, b1, w2, b2, out):
    x_tok = x.rearrange("b h w c -> (b h w) c")
    x_v = x_tok.rearrange("(b t p) c -> b p t c", p=P, t=NT)
    out_tok = out.rearrange("b h w c -> (b h w) c")

    with ExitStack() as ctx:
        layers = ExitStack()

        def sb(name, shape, dt, stack=None):
            return (stack or layers).enter_context(nc.sbuf_tensor(name, shape, dt))

        def sem(name):
            return ctx.enter_context(nc.semaphore(name))

        def dram(name, shape, dt):
            return nc.dram_tensor(name, shape, dt, kind="Internal").ap()

        qk_d = dram("qk_d", (2, NH, 3, HD, N), F16)
        oh_d = dram("oh_d", (3 * NG, N), F16)
        x3_d = dram("x3_d", (TOK + P, C), F32)
        att_d = dram("att_d", (NH, HD, N), F32)
        xg_d = dram("xg_d", (NE * SEG, ROW), F32)
        w16_d = dram("w16_d", (2, 2, NE, WCH, P, CHW), F16)

        ident16 = sb("ident16", [P, P], F16, ctx)
        desc = sb("desc", [P, NG], F32, ctx)
        b1T = sb("b1T", [P, NE * FO], F32, ctx)
        triu = sb("triu", [P, P], F32, ctx)
        ones = sb("ones", [P, P], F32, ctx)
        rout = sb("rout", [P, NT, ROW], F32, ctx)
        sc = sb("sc", [P, NT, NE], F32, ctx)
        prob = sb("prob", [P, NT, NE], F32, ctx)
        oh1 = sb("oh1", [P, NT, NE], F32, ctx)
        oh2 = sb("oh2", [P, NT, NE], F32, ctx)
        mask = sb("mask", [P, NT, NE], F32, ctx)
        pos = sb("pos", [P, NT, NE], F32, ctx)
        cum = [sb(f"cum{i}", [P, NT, NE], F32, ctx) for i in range(2)]
        red = sb("red", [P, NT], F32, ctx)
        slots = sb("slots", [P, NT, 2], I32, ctx)
        tok = sb("tok", [P, NT], F32, ctx)
        seg = sb("seg", [P, NE], F32, ctx)
        run = sb("run", [P, NE], F32, ctx)
        thr = sb("thr", [P, MT], F32, ctx)
        over = sb("over", [P, NE, MT], F32, ctx)
        tiles = sb("tiles", [P, NE], F32, ctx)
        tb = sb("tb", [P, NE + 1], F32, ctx)
        tbi = sb("tbi", [P, NE + 1], I32, ctx)
        cti = sb("cti", [P, NE], I32, ctx)
        runi = sb("runi", [P, NE], I32, ctx)
        padrow = sb("padrow", [P, ROW], F32, ctx)
        ident = sb("ident", [P, P], F32)
        band = sb("band", [P, P], F32)
        bandn = sb("bandn", [P, P], F32)
        cbox = [sb(f"cbox{i}", [P, P], F32) for i in range(3)]
        wqT = [sb(f"wqT{i}", [P, CC, 3 * C], F16) for i in range(2)]
        wpT = [sb(f"wpT{i}", [P, CC, C], F16) for i in range(2)]
        gpT = [sb(f"gpT{i}", [P, CC, NG], F16) for i in range(2)]
        gw16 = [sb(f"gw16_{i}", [P, CC, NE], F16) for i in range(2)]
        c1s = sb("c1s", [3 * KI, FFN], F16)
        cp1T = sb("cp1T", [P, FO, KI], F32)
        sel = sb("sel", [P, KI], F32)
        kw = sb("kw", [P, KI, KJ], F32)
        c2sum = sb("c2sum", [P, 1], F32)
        c2b = sb("c2b", [P, KJ], F32)
        cp2b = sb("cp2b", [P, KJ], F32)
        gbb = sb("gbb", [P, NE], F32)
        gwn = sb("gwn", [P, CC, NE], F32)
        xb = sb("xb", [P, NT, C], F32)
        xn = sb("xn", [P, NT, C], F32)
        at = sb("at", [P, NT, C], F32)
        xT = [sb(f"xT{i}", [P, CC, N], F16) for i in range(2)]
        stg = [sb(f"stg{i}", [P, 6, N], F16) for i in range(2)]
        va = sb("va", [P, NT, C], F32)
        qs = [sb(f"qs{i}", [P, N], F16) for i in range(HB)]
        ks = [sb(f"ks{i}", [P, N], F16) for i in range(HB)]
        E = sb("E", [P, NT, N], F32)
        oT = [sb(f"oT{i}", [P, N // 4], F32) for i in range(HB)]
        vp = sb("vp", [P, NT, HD], F32)
        ohn = sb("ohn", [P, NT, OHW], F16)
        ohT = sb("ohT", [OHW, N], F16)
        znat = sb("znat", [P, NT, 3 * KI], F16)
        zT = sb("zT", [3 * KI, N], F16)
        st6 = sb("st6", [P, NT, 6], F32)
        mv = sb("mv", [P, NT, 2], F32)
        ve = sb("ve", [P, NT], F32)
        lnv = sb("lnv", [P, NT], F32)
        y0 = sb("y0", [P, NT], F32)
        nt1 = sb("nt1", [P, NT], F32)
        rs = sb("rs", [P, NT], F32)
        gws = sb("gws", [P, NT, NG], F32)
        gwe = sb("gwe", [P, NT, NG], F32)
        gm = sb("gm", [P, NT], F32)
        zz = sb("zz", [P, NT, KI], F32)
        zs = sb("zs", [P, NT, KI], F32)
        mn = [sb(f"mn{i}", [P, NT], F32) for i in range(HB)]
        rsum = [sb(f"rsum{i}", [P, NT], F32) for i in range(HB)]
        lnr = [sb(f"lnr{i}", [P, NT], F32) for i in range(HB)]
        Lf = sb("Lf", [P, NT], F32)
        Ld = sb("Ld", [P, NT], F32)
        Lsp = sb("Lsp", [P, NT, 3], F16)
        csum = sb("csum", [P, NT], F32)
        cr = sb("cr", [P, NT], F32)
        wc = sb("wc", [P, CHW], F32)
        wch = [sb(f"wch{i}", [P, CHW], F16) for i in range(2)]

        layers.close()
        w1s = [[sb(f"w1s{i}{j}", [P, WCH, CHW], F16, ctx) for j in range(2)] for i in range(2)]
        w2s = [[sb(f"w2s{i}{j}", [P, WCH, CHW], F16, ctx) for j in range(2)] for i in range(2)]
        b2s = [sb(f"b2s{i}", [P, C], F32, ctx) for i in range(2)]
        xin32 = sb("xin", [P, 2, C], F32, ctx)
        meta = sb("meta", [P, 2, NE + 1], F32, ctx)
        xin = xin32[:, :, :].bitcast(F16)
        t16 = rout[:, :, :].bitcast(F16)
        gates = rout[:, :, C:C + NE]
        tT = sb("tT", [P, 2, CC, TT], F16, ctx)
        h32 = sb("h32", [P, FO, TT], F32, ctx)
        h16 = [sb(f"h16_{i}", [P, FO, TT], F16, ctx) for i in range(2)]
        yo = sb("yo", [P, 2, C], F32, ctx)

        ps = [ctx.enter_context(nc.psum_tensor(f"ps{i}", [P, 2, 512], F32)) for i in range(4)]

        def bank(i):
            return ps[i // 2][:, i % 2, :]

        def bank16(i):
            return bank(i).bitcast(F16)

        def first_pass(p, k):
            return ps[(p + 2 * k) % 3][:, :, :]

        def second_pass(p, t):
            return ps[(p + 1 + 2 * (t + LAG) + 1) % 3][:, :, :]

        attT = at[:, :, :].rearrange("p t c -> p (t c)").rearrange("p (c n) -> p c n", c=CC)
        uT = oT[0]
        Ef = E[:, :, :].rearrange("p t n -> p (t n)")
        wnat = Ef[:, 0:9 * C].rearrange("p (o c) -> p o c", o=9)
        pnat = Ef[:, 9 * C:12 * C].rearrange("p (o c) -> p o c", o=3)
        gnat = Ef[0:NG, 12 * C:13 * C]
        fnat = Ef[:, 13 * C:14 * C].rearrange("p (o i) -> p o i", o=FO)
        f16n = Ef[:, 14 * C:14 * C + FO * 48].bitcast(F16).rearrange("p (o i) -> p o i", o=FO)
        cpn = Ef[0:KI, 16 * C:20 * C]
        bnat = Ef[0:NE * FO, 20 * C:20 * C + P]
        sqT = [Ef[:, i * C:(i + 1) * C] for i in range(2)]
        dT = [Ef[:, (2 + i) * C:(3 + i) * C] for i in range(2)]
        num = [Ef[:, (4 + i) * C:(5 + i) * C] for i in range(2)]
        den = [Ef[:, (6 + i) * C:(7 + i) * C] for i in range(2)]
        tot = Ef[:, 8 * C:9 * C]
        hT = E

        prep_items = []
        for c in range(CC):
            for o0, o1 in ((0, 4), (4, 8), (8, 9)):
                prep_items.append(([w[:, c, o0 * P:o1 * P] for w in wqT], bank(len(prep_items) % RING)[:, 0:(o1 - o0) * P]))
        for c in range(CC):
            prep_items.append(([w[:, c, :] for w in wpT], bank(len(prep_items) % RING)[:, 0:C]))
        prep_items.append(([w[:, :, :].rearrange("p c g -> p (c g)") for w in gpT],
                           bank(len(prep_items) % RING)[:, 0:CC * NG]))

        s_wld = sem("s_wld")
        s_cst = sem("s_cst")
        s_pt = sem("s_pt")
        s_ph = sem("s_ph")
        s_pf = sem("s_pf")
        s_f16 = sem("s_f16")
        s_xb = sem("s_xb")
        s_xn = sem("s_xn")
        s_ve = sem("s_ve")
        s_y0 = sem("s_y0")
        s_pe = sem("s_pe")
        s_hi = sem("s_hi")
        s_fr = sem("s_fr")
        s_stg = sem("s_stg")
        s_oh = sem("s_oh")
        s_sto = sem("s_sto")
        s_xp = sem("s_xp")
        s_xh = sem("s_xh")
        s_xr = sem("s_xr")
        s_stg2 = sem("s_stg2")
        s_qm = [sem(f"s_qm{i}") for i in range(HB)]
        s_qk = [sem(f"s_qk{i}") for i in range(HB)]
        s_s1 = sem("s_s1")
        s_mx = sem("s_mx")
        s_e1 = sem("s_e1")
        s_ln = sem("s_ln")
        s_lf = sem("s_lf")
        s_lt = sem("s_lt")
        s_lr = sem("s_lr")
        s_s2 = sem("s_s2")
        s_e2 = sem("s_e2")
        s_vp = sem("s_vp")
        s_pv = sem("s_pv")
        s_ev = sem("s_ev")
        s_od = [sem(f"s_od{i}") for i in range(HB)]
        s_at = sem("s_at")
        s_at2 = sem("s_at2")
        s_ah = sem("s_ah")
        s_al = sem("s_al")
        s_ut = sem("s_ut")
        s_un = sem("s_un")
        s_kr = sem("s_kr")
        s_z = sem("s_z")
        s_h = sem("s_h")
        s_gl = sem("s_gl")
        s_u = sem("s_u")
        s_y2 = sem("s_y2")
        s_cv = sem("s_cv")
        s_sq = sem("s_sq")
        s_cb = sem("s_cb")
        s_cr = sem("s_cr")
        s_nc = sem("s_nc")
        s_rc = sem("s_rc")
        s_pp = sem("s_pp")
        s_zp = sem("s_zp")
        s_bx = sem("s_bx")
        s_th = sem("s_th")
        s_st = sem("s_st")
        s_tl = sem("s_tl")
        s_pv0 = sem("s_pv0")
        s_v = sem("s_v")
        s_a = sem("s_a")
        s_wc = sem("s_wc")
        s_wp = sem("s_wp")
        s_wl = sem("s_wl")
        s_pw = sem("s_pw")
        s_sw = sem("s_sw")
        s_pe2 = sem("s_pe2")
        s_aw = sem("s_aw")
        s_ws = sem("s_ws")
        s_ge = sem("s_ge")
        s_gs = sem("s_gs")
        s_gc = sem("s_gc")
        s_mk = sem("s_mk")
        s_rk = sem("s_rk")
        s_rt = sem("s_rt")
        s_sc = sem("s_sc")
        s_td = sem("s_td")
        s_pad = sem("s_pad")
        s_tb = sem("s_tb")
        s_mt = sem("s_mt")
        s_end = sem("s_end")
        s_ew2 = [sem("s_ew20"), sem("s_ew21")]
        s_ew = [sem("s_ew0"), sem("s_ew1")]
        s_xi = sem("s_xi")
        s_xt = sem("s_xt")
        s_xe = sem("s_xe")
        s_h1 = sem("s_h1")
        s_hg = sem("s_hg")
        s_ha = sem("s_ha")
        s_h2 = sem("s_h2")
        s_ys = sem("s_ys")
        s_yc = sem("s_yc")
        s_yo = sem("s_yo")
        s_yd = sem("s_yd")
        s_ya = sem("s_ya")

        NSTG = 3 * N_QK // 2
        NXN = NT + NT // 2 + 2

        block = ctx.enter_context(nc.Block())

        @block.sync
        def _(sp):
            sp.dma_start(wnat, W_qkv.rearrange("(o p) c -> p o c", p=P)).then_inc(s_wld, 16)
            sp.dma_start(pnat, W_proj.rearrange("(o p) c -> p o c", p=P)).then_inc(s_wld, 16)
            sp.dma_start(gnat, W_gp).then_inc(s_wld, 16)
            sp.dma_start(fnat, c_fc_1.rearrange("(o p) i -> p o i", p=P)).then_inc(s_wld, 16)
            sp.dma_start(cpn, c_proj_1).then_inc(s_wld, 16)
            sp.dma_start(gwn[:, :, :], gate_w.rearrange("(c p) e -> p c e", p=P)).then_inc(s_wld, 16)
            sp.dma_start(c2b[:, :], c_fc_2.to_broadcast([P, KJ])).then_inc(s_wld, 16)
            sp.dma_start(cp2b[:, :], c_proj_2.rearrange("j a -> a j").to_broadcast([P, KJ])).then_inc(s_wld, 16)
            sp.dma_start(gbb[:, :], gate_b.rearrange("(a e) -> a e", a=1).to_broadcast([P, NE])).then_inc(s_wld, 16)

            sp.dma_start(bnat, b1.rearrange("e (o p) -> (e o) p", p=P)).then_inc(s_wld, 16)

            def load_x(b):
                sp.dma_start(xb[:, :, :], x_v[b]).then_inc(s_xb, 16)

            def load_head(b, h, par):
                for dst, src in ((qs[par], qk_d[0, h]), (ks[par], qk_d[1, h])):
                    sp.dma_start(dst[0:3 * HD, :], src.rearrange("r d n -> (r d) n")).then_inc(s_qk[par], 16)

            def load_mask(par, mask):
                for dst, r in ((qs[par], 0), (ks[par], 1 + mask)):
                    sp.dma_start(dst[3 * HD + 3:3 * HD + 3 + NG, :], oh_d[r * NG:(r + 1) * NG, :]
                                 ).then_inc(s_qm[par], 16)

            for par in range(HB):
                sp.sem_inc(s_od[par], 16)
            with sp.Fori(0, B) as b:
                load_x(b)

                def stage(j, semaphore):
                    qk, h0 = j // 3, 4 * (j % 3)
                    for r, part in enumerate((0, 0, 1) if qk == 0 else (0, 1, 0)):
                        sp.dma_start(qk_d[qk, h0:h0 + 4, r], stg[part][:, j, :]).then_inc(semaphore, 16)

                for j in range(N_QK // 2):
                    sp.wait_ge(s_fr, b * NRING + (1 + OFF_QK + 2 * j + 2))
                    stage(j, s_stg)
                sp.wait_ge(s_stg, b * (16 * NSTG) + 16 * NSTG)
                for h in range(HB):
                    load_head(b, h, h)
                sp.wait_ge(s_fr, b * NRING + (1 + OFF_O + 1))
                sp.dma_start(oh_d, ohT[0:3 * NG, :]).then_inc(s_sto, 16)
                sp.wait_ge(s_sto, b * 16 + 16)
                for h in range(HB):
                    load_mask(h, 0)
                for j in range(N_XK // 2):
                    sp.wait_ge(s_xr, b * N_X + (2 * j + 2))
                    stage(N_QK // 2 + j, s_stg2)
                sp.wait_ge(s_stg2, b * (8 * 3 * N_XK) + 8 * 3 * N_XK)
                sp.sem_inc(s_sw, 1)

                def store_head(h, par):
                    sp.wait_ge(s_ev, b * NH + h + 1)
                    sp.dma_start(att_d[h].rearrange("d (j n) -> j d n", j=4), oT[par][:, :]).then_inc(s_od[par], 16)

                def next_head(h, par, mask):
                    sp.wait_ge(s_s2, b * (NH * NT) + (h - (HB - 1)) * NT)
                    sp.sem_inc(s_sw, 1)
                    load_head(b, h, par)
                    load_mask(par, mask)
                    store_head(h - HB, par)

                for par in range(HB):
                    next_head(HB + par, par, 0)
                with sp.Fori(2, HR) as i:
                    for par in range(HB):
                        next_head(i * HB + par, par, 1)
                att_c = att_d.rearrange("(c h) d n -> (h d) c n", c=CC)
                for par in range(HB):
                    sp.wait_ge(s_od[par], 16 + b * (16 * HR) + 16 * (HR - 1))
                sp.dma_start(attT[:, 0:CC - 1, :], att_c[:, 0:CC - 1, :]).then_inc(s_at, 16)
                for par in range(HB):
                    store_head(NH - HB + par, par)
                for par in range(HB):
                    sp.wait_ge(s_od[par], 16 + b * (16 * HR) + 16 * HR)
                sp.dma_start(attT[:, CC - 1, :], att_c[:, CC - 1, :]).then_inc(s_at2, 16)
                sp.wait_ge(s_bx, (b + 1) * NT)
                sp.dma_start(x3_d[0:TOK].rearrange("(b t p) c -> b p t c", p=P, t=NT)[b], xb[:, :, :]).then_inc(s_st, 16)
                sp.wait_ge(s_xn, b * NXN + NXN)
                sp.wait_ge(s_st, b * 16 + 16)
                sp.sem_inc(s_sw, 1)
            sp.wait_ge(s_tb, 1)
            for e in range(NE):
                row = sp.value_load(runi[0:1, e:e + 1], min_val=0, max_val=NE * SEG - TT)
                sp.dma_start(xg_d[bass.ds(row, TT)].rearrange("(s p) c -> p s c", p=P),
                             padrow[:, :].rearrange("p (a c) -> p a c", a=1).to_broadcast([P, TT // P, ROW])
                             ).then_inc(s_pad, 16)
            sp.wait_ge(s_pad, 16 * NE)
            sp.wait_ge(s_td, B + 1)
            xg_v = xg_d.rearrange("(m s p) c -> m p s c", s=2, p=P)

            def load_tile(m):
                sp.dma_start(xin32[:, :, :], xg_v[m, :, :, 0:C]).then_inc(s_xi, 16)

            with sp.Fori(0, NE) as e:
                first = sp.value_load(tbi[0:1, bass.ds(e, 1)], min_val=0, max_val=NE * MT)
                count = sp.value_load(cti[0:1, bass.ds(e, 1)], min_val=1, max_val=MT)
                with sp.Fori(0, count) as j:
                    i, m = first + j, e * (SEG // TT) + j
                    sp.wait_ge(s_xt, i + 1)
                    load_tile(m)
                    sp.wait_ge(s_yd, i * 2 + 2)
                    sp.dma_start(meta[:, :, :], xg_v[m, :, :, C:ROW]).then_inc(s_mt, 16)
            end = sp.value_load(tbi[0:1, NE:NE + 1], min_val=0, max_val=NE * MT)
            sp.wait_ge(s_xt, end + 1)
            sp.sem_inc(s_sw, 1)
            load_tile(0)
            sp.wait_ge(s_xi, end * 16 + 16)
            sp.sem_inc(s_sw, 1)
            sp.wait_ge(s_end, 1)
            sp.dma_start(out_tok, x3_d[0:TOK]).then_inc(s_st, 16)
            sp.wait_ge(s_st, B * 16 + 16)

        @block.gpsimd
        def _(pool):
            ch = Chain(pool, s_cst)
            ch.mark(pool.memset(ident[:, :], 0.0))
            ch.mark(pool.memset(ident16[:, :], 0.0))
            ch.step(pool.memset(band[:, :], 1.0))
            for m in (ident, ident16):
                ch.step(pool.affine_select(out=m[:, :], in_=m[:, :], compare_op=ALU.not_equal, fill=1.0, base=0,
                                           pattern=[[-1, P]], channel_multiplier=1))
            for base, step, cm in ((W1 // 2, -1, 1), (W1 // 2, 1, -1)):
                ch.step(pool.affine_select(out=band[:, :], in_=band[:, :], compare_op=ALU.is_ge, fill=0.0, base=base,
                                           pattern=[[step, P]], channel_multiplier=cm))
            bv = band[:, :].rearrange("p (a w) -> p a w", w=WD)
            for base, step, cm in ((0, -WD, 1), (WD - 1, WD, -1)):
                ch.step(pool.affine_select(out=bv, in_=bv, compare_op=ALU.is_ge, fill=0.0, base=base,
                                           pattern=[[step, P // WD], [0, WD]], channel_multiplier=cm))
            for m in cbox:
                ch.step(pool.memset(m[:, :], 1.0))
            for m, base, step in ((cbox[0], LW, -1), (cbox[0], RW, 1), (cbox[1], LW - P, -1), (cbox[2], RW - P, 1)):
                ch.step(pool.affine_select(out=m[:, :], in_=m[:, :], compare_op=ALU.is_ge, fill=0.0, base=base,
                                           pattern=[[step, P]], channel_multiplier=-step))
            ch.step(pool.iota(desc[:, :], pattern=[[-1, NG]], base=KI, channel_multiplier=0,
                              allow_small_or_imprecise_dtypes=True))
            for i in range(HB):
                ch.step(pool.memset(ks[i][3 * HD:3 * HD + 3, :], 1.0))
            ch.mark(pool.memset(ones[:, :], 1.0))
            ch.step(pool.memset(triu[:, :], 1.0))
            ch.step(pool.affine_select(out=triu[:, :], in_=triu[:, :], compare_op=ALU.is_ge, fill=0.0, base=-1,
                                       pattern=[[1, P]], channel_multiplier=-1))
            for dst, pattern, cm in ((tok, [[P, NT]], 1), (seg, [[SEG, NE]], 0), (thr, [[TT, MT]], 0)):
                ch.mark(pool.iota(dst[:, :], pattern=pattern, base=0, channel_multiplier=cm,
                                  allow_small_or_imprecise_dtypes=True))
            ch.step(pool.memset(padrow[:, :], 0.0))
            ch.step(pool.iota(padrow[:, :].bitcast(I32)[:, ROW - 1:ROW], pattern=[[0, 1]], base=TOK,
                              channel_multiplier=1))
            assert ch.n == NCST
            pool.dma_start(x3_d[TOK:TOK + P], padrow[:, 0:C]).then_inc(s_sc, 16)

            def wait_alone(semaphore, value, carrier=s_pw):
                pool.wait_ge(semaphore, value)
                pool.sem_inc(carrier, 1)

            pool.sem_inc(s_yd, 2)
            pool.sem_inc(s_td, 1)

            def weight_parts(b, ch):
                for k, src in enumerate((w1.rearrange("e (c p) f -> (e c) p f", p=P),
                                         w2.rearrange("e (g o p) d -> (e g) p o d", p=P, o=FO // WCH))):
                    with pool.Fori(0, WCH) as j:
                        m, done = b * WCH + j, b * (2 * WCH) + (j + k * WCH)
                        ch.base, ch.n = done * NPW, 0
                        pool.dma_start(wc[:, :] if k == 0 else wc[:, :].rearrange("p (o d) -> p o d", o=FO // WCH),
                                       src[m]).then_inc(s_wc, 16)
                        wait_alone(s_wc, done * 16 + 16)
                        wait_alone(s_wp, ch.mark(pool.tensor_scalar(wc[:, :], wc[:, :], SW, None, ALU.mult)))
                        wait_alone(s_wp, ch.mark(pool.tensor_copy(wch[0][:, :], wc[:, :])))
                        pool.tensor_tensor(wch[1][:, :], wc[:, :], wch[0][:, :], ALU.subtract).then_inc(s_wl, 1)
                        wait_alone(s_wl, done + 1)
                        for i in range(2):
                            pool.dma_start(w16_d[k, i].rearrange("e g p w -> (e g) p w")[m], wch[i][:, :]
                                           ).then_inc(s_ws, 16)
                        wait_alone(s_ws, done * 32 + 32)
                        assert ch.n == NPW

            def add_ratio(b, t, ch):
                n_, r_, x_ = num[t % 2], den[t % 2], xb[:, t, :]
                ch.base, ch.n = b * (2 * NT) + 2 * t, 0
                wait_alone(s_rc, b * NT + (t + 1))
                wait_alone(s_pp, ch.mark(pool.tensor_tensor(n_, n_, r_, ALU.mult)))
                wait_alone(s_pp, ch.mark(pool.tensor_scalar(n_, n_, FLT_MAX, None, ALU.min)))
                pool.tensor_tensor(x_, n_, x_, ALU.add).then_inc(s_bx, 1)

            def scatter(index, rows):
                pool.indirect_dma_start(out=xg_d, out_offset=bass.IndirectOffsetOnAxis(ap=index, axis=0), in_=rows,
                                        in_offset=None).then_inc(s_sc, 16)

            assert NE == B
            with pool.Fori(0, B) as b:
                weight_parts(b, Chain(pool, s_wp))
                for t in range(NT):
                    wait_alone(s_fr, b * NRING + (1 + OFF_PJ + t + 1))
                    pool.tensor_tensor(xn[:, t, :].rearrange("p (i j) -> p i j", j=KJ),
                                       xb[:, t, :].rearrange("p (i j) -> p i j", j=KJ),
                                       c2b[:, :].rearrange("p (a j) -> p a j", a=1).to_broadcast([P, KI, KJ]),
                                       ALU.mult).then_inc(s_zp, 1)
                for t in range(NT):
                    add_ratio(b, t, Chain(pool, s_pp))
                wait_alone(s_th, b + 1)
                pool.tensor_tensor(t16[:, :, C:2 * C], xn[:, :, :], t16[:, :, 0:C], ALU.subtract).then_inc(s_tl, 1)
                wait_alone(s_tl, b + 1)
                wait_alone(s_rt, b + 1)
                for t in range(NT):
                    for k in range(2):
                        scatter(slots[:, t, k:k + 1], rout[:, t, :])
                wait_alone(s_sc, b * (2 * NT * 16) + 16 + 2 * NT * 16)
                pool.sem_inc(s_td, 1)

            pool.wait_ge(s_tb, 1)
            total = pool.value_load(tbi[0:1, NE:NE + 1], min_val=0, max_val=NE * MT)
            with pool.Fori(0, total) as i:
                for s in range(2):
                    wait_alone(s_yo, i * 2 + (s + 1))
                    pool.indirect_dma_start(
                        out=x3_d, out_offset=bass.IndirectOffsetOnAxis(
                            ap=meta[:, :, :].bitcast(I32)[:, s, NE:NE + 1], axis=0),
                        in_=yo[:, s, :], in_offset=None, compute_op=ALU.add).then_inc(s_ya, 16)
                    wait_alone(s_ya, i * 32 + (s + 1) * 16, s_yd)
            pool.sem_inc(s_end, 1)

        @block.scalar
        def _(act):
            def table():
                act.add_instruction(mybir.InstLoadActFuncSet(
                    name=nc.get_next_instruction_name(), act_func_set_id=ACT_SET_EXP_LN, ins=[], outs=[]))

            table()
            for n, (dst, src) in enumerate(prep_items):
                act.wait_ge(s_pt, n + 1)
                nc.scalar.activation(dst[0], src, ACT.Copy, scale=SW).then_inc(s_ph, 1)
            act.wait_ge(s_wld, 16 * NW_LOADS)
            nc.scalar.activation(gw16[0][:, :, :], gwn[:, :, :], ACT.Copy, scale=SW).then_inc(s_ph, 1)

            chs = [0]
            with act.Fori(0, B) as b:
                ch = Chain(act, s_a)
                ch.base = b * NA

                def rsqrt_start(k):
                    act.wait_ge(s_ve, b * 4 + (k + 1))
                    ch.step(nc.scalar.activation(lnv[:, :], ve[:, :], ACT.Ln))
                    nc.scalar.activation(y0[:, :], lnv[:, :], ACT.Exp, scale=-0.5).then_inc(s_y0, 1)

                def hi_item(n, dst, src, scale):
                    act.wait_ge(s_pe, b * NRING + (n + 1))
                    nc.scalar.activation(dst, src, ACT.Copy, scale=scale).then_inc(s_hi, 1)

                rsqrt_start(0)
                for n in range(N_T):
                    hf, c = n // CC, n % CC
                    hi_item(n, xT[0][:, c, hf * 512:(hf + 1) * 512], bank(n % RING), 1.0)
                for n in range(N_QK):
                    j, hf = n // 2, n % 2
                    k = OFF_QK + n
                    hi_item(k, stg[0][:, j, hf * 512:(hf + 1) * 512], bank(k % RING),
                            (QSCALE if j < 3 else 1.0) / (SX * SW))

                def e1(h, p, k):
                    act.wait_ge(s_mx, b * (NH * NT) + h * NT + (k + 1))
                    scratch = first_pass(p, k).rearrange("p a n -> p (a n)")
                    nc.scalar.activation(scratch, scratch, ACT.Exp, bias=mn[p][:, k:k + 1], scale=-1.0,
                                         accum_out=rsum[p][:, k:k + 1]).then_inc(s_e1, 1)

                def e2(h, p, t, first=False):
                    act.wait_ge(s_s2, b * (NH * NT) + h * NT + (t + 1))
                    if not first:
                        act.wait_ge(s_pv, b * (NH * 4) + (h - 1) * 4 + (t // 2 + 1))
                    nc.scalar.activation(E[:, t, :], second_pass(p, t).rearrange("p a n -> p (a n)"), ACT.Exp,
                                         scale=-1.0, accum_out=csum[:, t:t + 1]).then_inc(s_e2, 1)

                def attention(r, p, first=True, second=True, third=True, head0=None):
                    p1, p2 = (p - 1) % HB, (p - 2) % HB
                    for k in range(NT):
                        if k == 0 and second:
                            act.wait_ge(s_e1, b * (NH * NT) + r * NT)
                            nc.scalar.activation(lnr[p1][:, :], rsum[p1][:, :], ACT.Ln).then_inc(s_ln, 1)
                        if not second and first and k in (2, 4, 6, 7):
                            d = (2, 4, 6, 7).index(k)
                            act.wait_ge(s_xp, b * N_X + (d + 1))
                            nc.scalar.activation(stg[0][:, (N_QK + d) // 2, d % 2 * 512:(d % 2 + 1) * 512],
                                                 bank(6 + d % 2), ACT.Copy, scale=1.0 / (SX * SW)).then_inc(s_xh, 1)
                        if first:
                            e1(r, p, k)
                        if k >= LAG and second:
                            e2(r - 1, p1, k - LAG, head0 == 1)
                        if k < LAG and third:
                            e2(r - 2, p2, k - LAG + NT, head0 == 2)

                attention(0, 0, second=False, third=False)
                attention(1, 1, third=False, head0=1)
                attention(2, 2, head0=2)
                with act.Fori(1, HR) as i:
                    for p in range(HB):
                        attention(i * HB + p, p)
                attention(NH, 0, first=False)
                attention(NH + 1, 1, first=False, second=False)

                act.wait_ge(s_at, b * 16 + 16)
                for c in range(CC):
                    if c == CC - 1:
                        act.wait_ge(s_at2, b * 16 + 16)
                    nc.scalar.activation(xT[0][:, c, :], attT[:, c, :], ACT.Copy, scale=SATT).then_inc(s_ah, 1)
                rsqrt_start(1)
                for o in range(FO):
                    act.wait_ge(s_h, b * FO + (o + 1))
                    if o >= 4:
                        act.wait_ge(s_u, b * FO + (o - 3))
                    nc.scalar.activation(hT[:, o % 4, :], ps[o % 2][:, :, :].rearrange("p a n -> p (a n)"), ACT.Gelu,
                                         scale=1.0 / (SZ * SC1)).then_inc(s_gl, 1)
                table()
                rsqrt_start(2)

                def squares(g):
                    act.wait_ge(s_xn, b * NXN + (NT + g + 1))
                    nc.scalar.activation(at[:, 2 * g:2 * g + 2, :], xn[:, 2 * g:2 * g + 2, :], ACT.Square).then_inc(s_y2, 1)

                def copy_num(t):
                    act.wait_ge(s_cb, b * NT + (t + 1))
                    if t >= 2:
                        act.wait_ge(s_bx, b * NT + (t - 1))
                    nc.scalar.activation(num[t % 2], ps[2][:, t % 2, 0:C], ACT.Copy).then_inc(s_nc, 1)

                squares(0)
                squares(1)
                for t in range(NT):
                    if t in (2, 4):
                        squares(t // 2 + 1)
                    act.wait_ge(s_cv, b * NT + (t + 1))
                    if t >= 2:
                        act.wait_ge(s_cb, b * NT + (t - 1))
                    nc.scalar.activation(sqT[t % 2][:, :], ps[0][:, t % 2, 0:C], ACT.Square)
                    nc.scalar.activation(dT[t % 2][:, :], ps[1][:, t % 2, 0:C], ACT.Copy).then_inc(s_sq, 1)
                    if t >= 1:
                        copy_num(t - 1)
                copy_num(NT - 1)
                rsqrt_start(3)
                for n in range(N_T):
                    hf, c = n // CC, n % CC
                    hi_item(OFF_T3 + n, xT[0][:, c, hf * 512:(hf + 1) * 512], bank(n % RING), 1.0)
                act.wait_ge(s_td, b + 1)
                nc.scalar.activation(t16[:, :, 0:C], xn[:, :, :], ACT.Copy).then_inc(s_th, 1)
                act.wait_ge(s_gs, b + 1)
                nc.scalar.activation(sc[:, :, :], sc[:, :, :], ACT.Exp).then_inc(s_ge, 1)
                assert ch.n == NA

            def load_first(e):
                for j in range(2):
                    act.dma_start(w1s[e % 2][j][:, :, :], w16_d[0, j, e].rearrange("g p w -> p g w")
                                  ).then_inc(s_ew[e % 2], 16)

            def load_second(e):
                for j in range(2):
                    act.dma_start(w2s[e % 2][j][:, :, :], w16_d[1, j, e].rearrange("g p w -> p g w")
                                  ).then_inc(s_ew2[e % 2], 16)
                act.dma_start(b2s[e % 2][:, :], b2[e].rearrange("(a c) -> a c", a=1).to_broadcast([P, C])
                              ).then_inc(s_ew2[e % 2], 16)

            act.wait_ge(s_tb, 1)
            act.wait_ge(s_st, B * 16)
            act.wait_ge(s_ws, 2 * NE * WCH * 32)
            load_first(0)
            for e in range(NE):
                first = act.value_load(tbi[0:1, e:e + 1], min_val=0, max_val=NE * MT)
                end = act.value_load(tbi[0:1, e + 1:e + 2], min_val=0, max_val=NE * MT)
                if e >= 1:
                    act.wait_ge(s_yo, first * 2)
                    act.sem_inc(s_aw, 1)
                else:
                    act.wait_ge(s_xi, 16)
                    load_second(0)
                if e + 1 < NE:
                    load_first(e + 1)
                    load_second(e + 1)
                with act.Fori(first, end) as i:
                    for q in range(FO // 2):
                        act.wait_ge(s_h1, i * (FO // 2) + (q + 1))
                        for o in (2 * q, 2 * q + 1):
                            last = nc.scalar.activation(h32[:, o, :], bank(q % 3)[:, (o % 2) * TT:(o % 2 + 1) * TT],
                                                        ACT.Gelu, bias=b1T[:, e * FO + o:e * FO + o + 1],
                                                        scale=1.0 / (SX * SW))
                        last.then_inc(s_hg, 1)

        @block.tensor
        def _(pe):
            pe.wait_ge(s_cst, NCST)
            pe.wait_ge(s_wld, 16 * NW_LOADS)
            n = 0
            for c in range(CC):
                for o0, o1 in ((0, 4), (4, 8), (8, 9)):
                    if n >= RING:
                        pe.wait_ge(s_pf, n - RING + 1)
                    for o in range(o0, o1):
                        last = nc.tensor.transpose(bank(n % RING)[:, (o - o0) * P:(o - o0 + 1) * P],
                                                   wnat[:, o, c * P:(c + 1) * P], ident[:, :])
                    last.then_inc(s_pt, 1)
                    n += 1
            for c in range(CC):
                pe.wait_ge(s_pf, n - RING + 1)
                for o in range(CC):
                    last = nc.tensor.transpose(bank(n % RING)[:, o * P:(o + 1) * P], pnat[:, o, c * P:(c + 1) * P],
                                               ident[:, :])
                last.then_inc(s_pt, 1)
                n += 1
            pe.wait_ge(s_pf, n - RING + 1)
            for c in range(CC):
                last = nc.tensor.transpose(bank(n % RING)[:, c * NG:(c + 1) * NG], gnat[:, c * P:(c + 1) * P],
                                           ident[0:NG, 0:NG])
            last.then_inc(s_pt, 1)
            n += 1
            assert n == len(prep_items)
            pe.wait_ge(s_pf, n - RING + 1)
            for o in range(FO):
                last = nc.tensor.transpose(bank(6)[:, o * KI:(o + 1) * KI], cpn[:, o * P:(o + 1) * P],
                                           ident[0:KI, 0:KI])
            nc.tensor.transpose(bank(7)[:, 0:NE * FO], bnat, ident[0:NE * FO, 0:NE * FO]).then_inc(s_pt, 1)
            pe.wait_ge(s_f16, 1)
            pe.wait_ge(s_pf, n)
            for o in range(FO):
                last = nc.tensor.transpose(bank16(o // 8)[0:3 * KI, (o % 8) * P:(o % 8 + 1) * P], f16n[:, o, :],
                                           ident16[:, :])
            last.then_inc(s_pt, 1)
            nc.tensor.matmul(bank(2)[:, 0:P], ones[:, :], band[:, :], start=True, stop=True).then_inc(s_pt, 1)
            pe.wait_ge(s_pf, n + 4)

            with pe.Fori(0, B) as b:
                def ring(k, s0):
                    pe.wait_ge(s_fr, b * NRING + (1 + max(s0, k - RING + 1)))
                    return (k - s0) % RING

                def products(dst, pairs):
                    todo = [(lh[i], rh[j]) for lh, rh in pairs for i, j in ((0, 0), (0, 1), (1, 0))]
                    for m, (lhsT, rhs) in enumerate(todo):
                        last = nc.tensor.matmul(dst, lhsT, rhs, start=(m == 0), stop=(m == len(todo) - 1))
                    return last

                def transposes(s0, k0, src, ready):
                    for n in range(N_T):
                        hf, c = n // CC, n % CC
                        if c == 0:
                            ready(hf)
                        at_bank = bank(ring(k0 + n, s0))
                        for tt in range(4):
                            last = nc.tensor.transpose(at_bank[:, tt * P:(tt + 1) * P],
                                                       src[:, 4 * hf + tt, c * P:(c + 1) * P], ident[:, :])
                        last.then_inc(s_pe, 1)

                transposes(0, 0, xn, lambda hf: pe.wait_ge(s_xn, b * NXN + 4 * (hf + 1)))
                def qk_products(dst, n):
                    j, hf = n // 2, n % 2
                    return products(dst, [([wqT[a][:, c, j * P:(j + 1) * P] for a in range(2)],
                                           [xT[a][:, c, hf * 512:(hf + 1) * 512] for a in range(2)])
                                          for c in range(CC)])

                for n in range(N_QK):
                    k = OFF_QK + n
                    pe.wait_ge(s_fr, b * NRING + (1 + (n % 2 + 1) * CC))
                    i = ring(k, 0)
                    qk_products(bank(i), n).then_inc(s_pe, 1)
                i = ring(OFF_G, 0)
                pe.wait_ge(s_fr, b * NRING + (1 + OFF_QK + 6))
                for t in range(NT):
                    last = products(bank(i)[:, t * 32:t * 32 + NG],
                                    [([stg[a][:, c, t * P:(t + 1) * P] for a in range(2)],
                                      [gpT[a][:, c, :] for a in range(2)]) for c in range(CC)])
                last.then_inc(s_pe, 1)

                def value_products(dst, t):
                    return products(dst, [([xT[a][:, c, t * P:(t + 1) * P] for a in range(2)],
                                           [wqT[a][:, c, 2 * C:3 * C] for a in range(2)]) for c in range(CC)])

                for t in range(N_V):
                    value_products(bank(ring(OFF_V + t, 0))[:, 0:C], t).then_inc(s_pe, 1)
                i = ring(OFF_O, 0)
                pe.wait_ge(s_oh, b + 1)
                for t in range(NT):
                    last = nc.tensor.transpose(bank16(i)[0:OHW, t * P:(t + 1) * P], ohn[:, t, :], ident16[:, :])
                last.then_inc(s_pe, 1)
                pe.wait_ge(s_fr, b * NRING + (1 + SEC1))

                pv = bank(6)
                lt = bank16(7)

                def quarters(lhsT, rhs, start, stop):
                    for j in range(4):
                        last = nc.tensor.matmul(pv[32 * j:32 * j + 32, 0:N // 4], lhsT,
                                                rhs[:, j * (N // 4):(j + 1) * (N // 4)], start=start, stop=stop)
                    return last

                def p1(h, p, k, before):
                    if k == 0:
                        pe.wait_ge(s_qk[p], b * (32 * HR) + before * 32 + 32)
                    for hf in range(2):
                        last = nc.tensor.matmul(first_pass(p, k)[:, hf, :], qs[p][0:3 * HD, k * P:(k + 1) * P],
                                                ks[p][0:3 * HD, hf * 512:(hf + 1) * 512], start=True, stop=True)
                    last.then_inc(s_s1, 1)

                def p2(h, p, t, before):
                    if t == 0:
                        pe.wait_ge(s_qm[p], b * (32 * HR) + before * 32 + 32)
                        pe.wait_ge(s_lr, b * NH + h + 1)
                    k2 = 3 * HD + 3 + NG
                    for hf in range(2):
                        last = nc.tensor.matmul(second_pass(p, t)[:, hf, :], ks[p][0:k2, t * P:(t + 1) * P],
                                                qs[p][0:k2, hf * 512:(hf + 1) * 512], start=True, stop=True)
                    last.then_inc(s_s2, 1)

                def lrows(h):
                    pe.wait_ge(s_lf, b * NH + h + 1)
                    for t in range(NT):
                        last = nc.tensor.transpose(lt[0:3, t * P:(t + 1) * P], Lsp[:, t, :], ident16[:, :])
                    last.then_inc(s_lt, 1)

                def pvs(h, u, head0=False):
                    pe.wait_ge(s_vp, b * (NH * 4) + h * 4 + (u + 1))
                    if u == 0 and not head0:
                        pe.wait_ge(s_ev, b * NH + h)
                    for t in (2 * u, 2 * u + 1):
                        last = quarters(vp[:, t, :], E[:, t, :], t == 0, t == NT - 1)
                    last.then_inc(s_pv, 1)

                def extra(d):
                    need = (0, 0, 1, 2, 3, 5, 6, 7)[d]
                    if need:
                        pe.wait_ge(s_xr, b * N_X + need)
                    if d < N_XK:
                        qk_products(bank(6 + d % 2), N_QK + d).then_inc(s_xp, 1)
                    else:
                        value_products(bank(6)[:, 0:C], N_V + d - N_XK).then_inc(s_xp, 1)

                def attention(r, p, before, first=True, second=True, third=True):
                    b1, b2 = (p - 1) % HB, (p - 2) % HB
                    for k in range(NT):
                        g1, g2 = b * (NH * NT) + r * NT + k, b * (NH * NT) + (r - 1) * NT + (k - LAG)
                        if first:
                            if not second or (not third and k <= LAG + 1):
                                if second or k >= 3:
                                    pe.wait_ge(s_e1, g1 - 2)
                            else:
                                pe.wait_ge(s_e2, g2 - 1)
                            p1(r, p, k, before)
                        if (second and k >= LAG) or (third and k < LAG):
                            if first or (second and k == 0):
                                pe.wait_ge(s_e1, g1)
                            if not first:
                                pe.wait_ge(s_e2, g2 - 2)
                            if k >= LAG:
                                p2(r - 1, b1, k - LAG, before if p > 0 else before - 1)
                            else:
                                p2(r - 2, b2, k - LAG + NT, 0)
                        if not second and first and k % 2 == 1:
                            extra(k // 2)
                        if second and not third and k in (0, 2, 4, 5):
                            extra(N_XK + (0, 2, 4, 5).index(k))
                        if third and k in (1, 3, 5):
                            pvs(r - 2, (k + 1) // 2)
                        if second and k == 2:
                            lrows(r - 1)
                        if second and k == 7:
                            if not third:
                                pe.wait_ge(s_xr, b * N_X + N_X)
                            pvs(r - 1, 0, head0=not third)

                attention(0, 0, 0, second=False, third=False)
                attention(1, 1, 0, third=False)
                attention(2, 2, 0)
                with pe.Fori(1, HR) as i:
                    for p in range(HB):
                        attention(i * HB + p, p, i)
                attention(NH, 0, HR, first=False)
                attention(NH + 1, 1, HR, first=False, second=False)

                pe.wait_ge(s_ev, b * NH + NH)
                pe.wait_ge(s_al, b * CC + CC)
                for t in range(NT):
                    i = ring(OFF_PJ + t, SEC1)
                    products(bank(i)[:, 0:C], [([xT[a][:, c, t * P:(t + 1) * P] for a in range(2)],
                                                [wpT[a][:, c, :] for a in range(2)])
                                               for c in range(CC)]).then_inc(s_pe, 1)
                i = ring(OFF_Z, SEC1)
                pe.wait_ge(s_z, b + 1)
                for t in range(NT):
                    last = nc.tensor.transpose(bank16(i)[0:3 * KI, t * P:(t + 1) * P], znat[:, t, :], ident16[:, :])
                last.then_inc(s_pe, 1)
                pe.wait_ge(s_fr, b * NRING + (1 + OFF_Z + 1))
                for o in range(FO + 1):
                    if o < FO:
                        if o >= 2:
                            pe.wait_ge(s_gl, b * FO + (o - 1))
                        for hf in range(2):
                            last = nc.tensor.matmul(ps[o % 2][:, hf, :], c1s[:, o * P:(o + 1) * P],
                                                    zT[:, hf * 512:(hf + 1) * 512], start=True, stop=True)
                        last.then_inc(s_h, 1)
                    if o >= 1:
                        pe.wait_ge(s_gl, b * FO + o)
                        quarters(cp1T[:, o - 1, :], hT[:, (o - 1) % 4, :], o == 1, o == FO).then_inc(s_u, 1)
                pe.wait_ge(s_ut, b + 1)
                for t in range(NT):
                    j, s = t // 2, t % 2
                    if t >= RING:
                        pe.wait_ge(s_kr, b * NT + (t - RING + 1))
                    nc.tensor.matmul(bank(t % RING)[:, 0:C], uT[j * KI:(j + 1) * KI, s * P:(s + 1) * P],
                                     kw[j * KI:(j + 1) * KI, :, :].rearrange("p i j -> p (i j)"),
                                     start=True, stop=True).then_inc(s_un, 1)
                for t in range(NT + 1):
                    if t < NT:
                        pe.wait_ge(s_y2, b * 4 + (t // 2 + 1))
                        if t >= 2:
                            pe.wait_ge(s_sq, b * NT + (t - 1))
                        for dst, src, m in ((ps[0], xn, band), (ps[1], at, bandn)):
                            for c in range(CC):
                                last = nc.tensor.matmul(dst[:, t % 2, c * P:(c + 1) * P], src[:, t, c * P:(c + 1) * P],
                                                        m[:, :], start=True, stop=True)
                        last.then_inc(s_cv, 1)
                    if t >= 1:
                        u = t - 1
                        pe.wait_ge(s_sq, b * NT + (u + 1))
                        if u >= 2:
                            pe.wait_ge(s_cr, b * NT + (u - 1))
                        for dst, src in ((ps[2], sqT[u % 2]), (ps[3], dT[u % 2])):
                            for c in range(CC):
                                parts = [(c + d, cbox[i]) for i, d in ((0, 0), (1, -1), (2, 1)) if 0 <= c + d < CC]
                                for i, (c2, m) in enumerate(parts):
                                    last = nc.tensor.matmul(dst[:, u % 2, c * P:(c + 1) * P],
                                                            src[:, c2 * P:(c2 + 1) * P], m[:, :],
                                                            start=(i == 0), stop=(i == len(parts) - 1))
                        last.then_inc(s_cb, 1)
                transposes(OFF_T3, OFF_T3, xn, lambda hf: pe.wait_ge(s_xn, b * NXN + (NT + NT // 2 + hf + 1)))
                i = ring(OFF_SC, OFF_T3)
                pe.wait_ge(s_fr, b * NRING + (1 + OFF_T3 + N_T))
                for t in range(NT):
                    last = products(bank(i)[:, t * NE:(t + 1) * NE],
                                    [([xT[a][:, c, t * P:(t + 1) * P] for a in range(2)],
                                      [gw16[a][:, c, :] for a in range(2)]) for c in range(CC)])
                last.then_inc(s_pe, 1)
                pe.wait_ge(s_mk, b + 1)
                for m, bk in ((triu, 6), (ones, 7)):
                    last = nc.tensor.matmul(bank(bk)[:, 0:NT * NE], m[:, :], mask[:, :, :].rearrange("p t e -> p (t e)"),
                                            start=True, stop=True)
                last.then_inc(s_rk, 1)

            pe.wait_ge(s_tb, 1)

            def transpose_tile(m):
                pe.wait_ge(s_xi, m * 16 + 16)
                for s in range(2):
                    for c in range(CC):
                        for th in range(2):
                            last = nc.tensor.transpose(bank16(6 + s)[:, c * TT + th * P:c * TT + (th + 1) * P],
                                                       xin[:, th, s * C + c * P:s * C + (c + 1) * P], ident16[:, :])
                last.then_inc(s_xt, 1)

            pe.sem_inc(s_xt, 1)
            transpose_tile(0)
            with pe.Fori(0, NE // 2) as pair:
                for par in range(2):
                    pe.wait_ge(s_ew[par], pair * 32 + 32)
                    pe.sem_inc(s_pe2, 1)
                    first = pe.value_load(tbi[0:1, bass.ds(pair * 2 + par, 1)], min_val=0, max_val=NE * MT)
                    end = pe.value_load(tbi[0:1, bass.ds(pair * 2 + (par + 1), 1)], min_val=0, max_val=NE * MT)
                    with pe.Fori(first, end) as i:
                        pe.wait_ge(s_xe, i * 2 + 2)
                        for q in range(FO // 2):
                            if q >= 3:
                                pe.wait_ge(s_hg, i * (FO // 2) + (q - 2))
                            for o in (2 * q, 2 * q + 1):
                                todo = [(a, c2, c) for c in range(CC) for a, c2 in ((0, 0), (1, 0), (0, 1))]
                                for m, (a, x_, c) in enumerate(todo):
                                    last = nc.tensor.matmul(bank(q % 3)[:, (o % 2) * TT:(o % 2 + 1) * TT],
                                                            w1s[par][a][:, c, o * P:(o + 1) * P], tT[:, x_, c, :],
                                                            start=(m == 0), stop=(m == len(todo) - 1))
                            last.then_inc(s_h1, 1)
                        transpose_tile(i + 1)
                        for s in range(2):
                            sl = slice(s * P, (s + 1) * P)
                            for o in range(FO):
                                if s == 0 and o == 0:
                                    pe.wait_ge(s_ew2[par], pair * 48 + 48)
                                    pe.sem_inc(s_pe2, 1)
                                if s == 0 and o % 2 == 0:
                                    pe.wait_ge(s_h2, i * (FO // 2) + (o // 2 + 1))
                                for m, (a, w_) in enumerate(((0, 0), (0, 1), (1, 0))):
                                    g, r = o // (FO // WCH), o % (FO // WCH)
                                    last = nc.tensor.matmul(bank(4 + s)[:, 0:C], h16[a][:, o, sl],
                                                            w2s[par][w_][:, g, r * C:(r + 1) * C],
                                                            start=(o == 0 and m == 0), stop=(o == FO - 1 and m == 2))
                            last.then_inc(s_ys, 1)

        @block.vector
        def _(dve):
            dve.sem_inc(s_fr, 1)
            ch = Chain(dve, s_pv0)
            dve.wait_ge(s_cst, NCST)
            nc.vector.memset(ohn[:, :, 3 * NG:OHW], 0.0)
            for n, (dst, src) in enumerate(prep_items):
                dve.wait_ge(s_ph, n + 1)
                nc.vector.scalar_tensor_tensor(out=dst[1], in0=src, scalar=SW, in1=dst[0], op0=ALU.mult,
                                               op1=ALU.subtract).then_inc(s_pf, 1)
                if n == 0:
                    ch.mark(nc.vector.tensor_scalar(f16n[:, :, 0:KI], fnat, SC1, None, ALU.mult))
                    ch.step(nc.vector.tensor_scalar(f16n[:, :, 2 * KI:3 * KI], fnat, SC1, None, ALU.mult))
                    nc.vector.scalar_tensor_tensor(out=f16n[:, :, KI:2 * KI], in0=fnat, scalar=SC1,
                                                   in1=f16n[:, :, 0:KI], op0=ALU.mult,
                                                   op1=ALU.subtract).then_inc(s_f16, 1)
            nc.vector.tensor_copy(run[:, :], seg[:, :])
            dve.wait_ge(s_wld, 16 * NW_LOADS)
            nc.vector.reduce_sum(c2sum[:, :], c2b[:, :], AX.X)
            ch.step(nc.vector.reduce_sum(sel[:, :], ident[:, :].rearrange("p (j i) -> p i j", i=KI), AX.X))
            nc.vector.tensor_tensor(kw[:, :, :], sel[:, :].rearrange("p (i a) -> p i a", a=1).to_broadcast([P, KI, KJ]),
                                    cp2b[:, :].rearrange("p (a j) -> p a j", a=1).to_broadcast([P, KI, KJ]), ALU.mult)
            np_ = len(prep_items)
            dve.wait_ge(s_ph, np_ + 1)
            nc.vector.scalar_tensor_tensor(out=gw16[1][:, :, :], in0=gwn[:, :, :], scalar=SW, in1=gw16[0][:, :, :],
                                           op0=ALU.mult, op1=ALU.subtract).then_inc(s_pf, 1)
            dve.wait_ge(s_pt, np_ + 1)
            nc.vector.tensor_copy(cp1T[:, :, :].rearrange("p o i -> p (o i)"), bank(6)[:, 0:C])
            nc.vector.tensor_copy(b1T[:, :], bank(7)[:, 0:NE * FO]).then_inc(s_pf, 1)
            dve.wait_ge(s_pt, np_ + 2)
            nc.vector.tensor_copy(c1s[:, 0:1024], bank16(0)[0:3 * KI, :])
            nc.vector.tensor_copy(c1s[:, 1024:FFN], bank16(1)[0:3 * KI, 0:512]).then_inc(s_pf, 1)
            dve.wait_ge(s_pt, np_ + 3)
            nc.vector.tensor_tensor(bandn[:, :], bank(2)[:, 0:P], band[:, :], ALU.mult).then_inc(s_pf, 1)

            with dve.Fori(0, B) as b:
                ch = Chain(dve, s_v)
                ch.base = b * NV

                def stats(t):
                    return ch.mark(nc.vector.bn_stats(st6[:, t, :], xb[:, t, :]))

                def layer_stats(k, eps, scale, done=False):
                    if not done:
                        for t in range(NT):
                            stats(t)
                    m = ch.base + ch.n
                    ch.wait(m)
                    nc.vector.memset(nt1[:, :], 0.0)
                    for t in range(NT):
                        m = ch.mark(nc.vector.bn_aggr(mv[:, t, :], st6[:, t, :]))
                    ch.wait(m)
                    nc.vector.tensor_scalar(ve[:, :], mv[:, :, 1], eps, None, ALU.add).then_inc(s_ve, 1)
                    dve.wait_ge(s_y0, b * 4 + (k + 1))
                    ch.step(nc.vector.tensor_tensor(nt1[:, :], y0[:, :], y0[:, :], ALU.mult))
                    ch.step(nc.vector.tensor_tensor(nt1[:, :], nt1[:, :], ve[:, :], ALU.mult))
                    ch.step(nc.vector.tensor_scalar(nt1[:, :], nt1[:, :], -0.5 * scale, 1.5 * scale, ALU.mult, ALU.add))
                    ch.step(nc.vector.tensor_tensor(rs[:, :], nt1[:, :], y0[:, :], ALU.mult))

                def normalise(t):
                    return nc.vector.tensor_scalar(xn[:, t, :], xb[:, t, :], mv[:, t, 0:1], rs[:, t:t + 1],
                                                   ALU.subtract, ALU.mult)

                def lo_item(n, dst, src, hi, scale):
                    dve.wait_ge(s_hi, b * NHI + hi_count(n))
                    nc.vector.scalar_tensor_tensor(out=dst, in0=src, scalar=scale, in1=hi, op0=ALU.mult,
                                                   op1=ALU.subtract).then_inc(s_fr, 1)

                def lo_transposed(k0, scale):
                    for n in range(N_T):
                        hf, c = n // CC, n % CC
                        lo_item(k0 + n, xT[1][:, c, hf * 512:(hf + 1) * 512], bank(n % RING),
                                xT[0][:, c, hf * 512:(hf + 1) * 512], scale)

                dve.wait_ge(s_xb, b * 16 + 16)
                layer_stats(0, 1e-6, SX)
                for t in range(NT):
                    normalise(t).then_inc(s_xn, 1)
                lo_transposed(0, 1.0)
                for n in range(N_QK):
                    j, hf = n // 2, n % 2
                    k = OFF_QK + n
                    sl = slice(hf * 512, (hf + 1) * 512)
                    lo_item(k, stg[1][:, j, sl], bank(k % RING), stg[0][:, j, sl], (QSCALE if j < 3 else 1.0) / (SX * SW))
                dve.wait_ge(s_pe, b * NRING + (OFF_G + 1))
                g3 = bank(OFF_G % RING)[:, 0:NT * 32].rearrange("p (t g) -> p t g", g=32)[:, :, 0:NG]
                cp = nc.vector.tensor_copy(gws[:, :, :], g3)
                cp.then_inc(s_fr, 1)
                dve.wait_ge(s_fr, b * NRING + (1 + OFF_G + 1))
                gb = gm[:, :].rearrange("p (t a) -> p t a", a=1).to_broadcast([P, NT, NG])
                db = desc[:, :].rearrange("p (a g) -> p a g", a=1).to_broadcast([P, NT, NG])
                ch.step(nc.vector.tensor_reduce(gm[:, :], gws[:, :, :], axis=AX.X, op=ALU.min))
                ch.step(nc.vector.tensor_tensor(gwe[:, :, :], gws[:, :, :], gb, ALU.is_equal))
                ch.step(nc.vector.tensor_tensor(gwe[:, :, :], gwe[:, :, :], db, ALU.mult))
                ch.step(nc.vector.tensor_reduce(gm[:, :], gwe[:, :, :], axis=AX.X, op=ALU.max))
                ch.step(nc.vector.tensor_tensor(gws[:, :, :], gwe[:, :, :], gb, ALU.is_equal))
                ch.mark(nc.vector.tensor_scalar(ohn[:, :, 0:NG], gws[:, :, :], BIG, None, ALU.mult))
                ch.mark(nc.vector.tensor_scalar(ohn[:, :, NG:2 * NG], gws[:, :, :], -1.0, 1.0, ALU.mult, ALU.add))
                nc.vector.tensor_copy(ohn[:, :, 2 * NG:3 * NG], gws[:, :, :]).then_inc(s_oh, 1)

                def values_out(t, src):
                    return nc.vector.tensor_scalar(va[:, t, :], src, 1.0 / (SX * SW), None, ALU.mult)

                for t in range(N_V):
                    k = OFF_V + t
                    dve.wait_ge(s_pe, b * NRING + (k + 1))
                    values_out(t, bank(k % RING)[:, 0:C]).then_inc(s_fr, 1)
                dve.wait_ge(s_pe, b * NRING + (OFF_O + 1))
                nc.vector.tensor_copy(ohT[:, :], bank16(OFF_O % RING)[0:OHW, :]).then_inc(s_fr, 1)

                def mx(h, par, k):
                    dve.wait_ge(s_s1, b * (NH * NT) + h * NT + (k + 1))
                    nc.vector.tensor_reduce(mn[par][:, k:k + 1], first_pass(par, k).rearrange("p a n -> p (a n)"),
                                            axis=AX.X, op=ALU.min).then_inc(s_mx, 1)

                def values(h, u):
                    sl = slice(2 * u, 2 * u + 2)
                    dve.wait_ge(s_e2, b * (NH * NT) + h * NT + (2 * u + 2))
                    ch.step(nc.vector.tensor_scalar(cr[:, sl], csum[:, sl], 1e-8, None, ALU.add))
                    ch.step(nc.vector.reciprocal(cr[:, sl], cr[:, sl]))
                    nc.vector.tensor_tensor(vp[:, sl, :], va[:, sl, bass.ds(h * HD, HD)],
                                            cr[:, sl].rearrange("p (t a) -> p t a", a=1).to_broadcast([P, 2, HD]),
                                            ALU.mult).then_inc(s_vp, 1)

                def lparts(h, par):
                    dve.wait_ge(s_ln, b * NH + h + 1)
                    ch.step(nc.vector.tensor_tensor(Lf[:, :], lnr[par][:, :], mn[par][:, :], ALU.subtract))
                    ch.step(nc.vector.tensor_copy(Lsp[:, :, 0], Lf[:, :]))
                    ch.step(nc.vector.tensor_tensor(Ld[:, :], Lf[:, :], Lsp[:, :, 0], ALU.subtract))
                    ch.step(nc.vector.tensor_copy(Lsp[:, :, 1], Ld[:, :]))
                    nc.vector.tensor_tensor(Lsp[:, :, 2], Ld[:, :], Lsp[:, :, 1], ALU.subtract).then_inc(s_lf, 1)

                def lcopy(h, par):
                    dve.wait_ge(s_lt, b * NH + h + 1)
                    nc.vector.tensor_copy(qs[par][3 * HD:3 * HD + 3, :], bank16(7)[0:3, :]).then_inc(s_lr, 1)

                def evict(h, par, before):
                    dve.wait_ge(s_pv, b * (NH * 4) + h * 4 + 4)
                    dve.wait_ge(s_od[par], 16 + b * (16 * HR) + before * 16)
                    nc.vector.tensor_copy(oT[par][:, :], bank(6)[:, 0:N // 4]).then_inc(s_ev, 1)

                def attention(r, p, before, first=True, second=True, third=True):
                    b1, b2 = (p - 1) % HB, (p - 2) % HB
                    for k in range(NT):
                        if first:
                            mx(r, p, k)
                        for d in {3: (0,), 5: (1,), 7: (2, 3)}.get(k, ()) if first and not second else ():
                            j, sl = (N_QK + d) // 2, slice(d % 2 * 512, (d % 2 + 1) * 512)
                            dve.wait_ge(s_xh, b * N_XK + (d + 1))
                            nc.vector.scalar_tensor_tensor(
                                out=stg[1][:, j, sl], in0=bank(6 + d % 2), scalar=1.0 / (SX * SW),
                                in1=stg[0][:, j, sl], op0=ALU.mult, op1=ALU.subtract).then_inc(s_xr, 1)
                        if second and not third and first and k in (1, 3, 5, 6):
                            d = N_XK + (1, 3, 5, 6).index(k)
                            dve.wait_ge(s_xp, b * N_X + (d + 1))
                            values_out(N_V + d - N_XK, bank(6)[:, 0:C]).then_inc(s_xr, 1)
                        if third and k in (0, 2, 4):
                            values(r - 2, k // 2 + 1)
                        if second and k == 1:
                            lparts(r - 1, b1)
                        if second and k == 3:
                            lcopy(r - 1, b1)
                        if third and k == 6:
                            evict(r - 2, b2, before)
                        if second and k == 6:
                            values(r - 1, 0)

                attention(0, 0, 0, second=False, third=False)
                attention(1, 1, 0, third=False)
                attention(2, 2, 0)
                with dve.Fori(1, HR) as i:
                    saved = ch.enter(i - 1, NVA)
                    for p in range(HB):
                        attention(i * HB + p, p, i - 1 if p < 2 else i)
                ch.leave(saved, HR - 1)
                attention(NH, 0, HR - 1, first=False)
                attention(NH + 1, 1, HR - 1, first=False, second=False)

                for c in range(CC):
                    dve.wait_ge(s_ah, b * CC + (c + 1))
                    nc.vector.scalar_tensor_tensor(out=xT[1][:, c, :], in0=attT[:, c, :], scalar=SATT,
                                                   in1=xT[0][:, c, :], op0=ALU.mult, op1=ALU.subtract).then_inc(s_al, 1)
                def sum_products(t):
                    dve.wait_ge(s_zp, b * NT + (t + 1))
                    ch.mark(nc.vector.reduce_sum(zz[:, t, :], xn[:, t, :].rearrange("p (i j) -> p i j", j=KJ), AX.X))

                for t in range(NT):
                    k = OFF_PJ + t
                    dve.wait_ge(s_pe, b * NRING + (k + 1))
                    nc.vector.scalar_tensor_tensor(out=xb[:, t, :], in0=bank((k - SEC1) % RING)[:, 0:C],
                                                   scalar=1.0 / (SATT * SW), in1=xb[:, t, :], op0=ALU.mult,
                                                   op1=ALU.add).then_inc(s_fr, 1)
                    dve.wait_ge(s_fr, b * NRING + (1 + k + 1))
                    stats(t)
                    if t >= 1:
                        sum_products(t - 1)
                sum_products(NT - 1)
                layer_stats(1, 1e-5, SZ, done=True)
                ch.step(nc.vector.tensor_scalar(gm[:, :], mv[:, :, 0], c2sum[:, 0:1], None, ALU.mult))

                def per_token(v):
                    return v[:, :].rearrange("p (t a) -> p t a", a=1).to_broadcast([P, NT, KI])

                ch.step(nc.vector.tensor_tensor(zz[:, :, :], zz[:, :, :], per_token(gm), ALU.subtract))
                ch.step(nc.vector.tensor_tensor(zs[:, :, :], zz[:, :, :], per_token(rs), ALU.mult))
                ch.mark(nc.vector.tensor_copy(znat[:, :, KI:2 * KI], zs[:, :, :]))
                ch.step(nc.vector.tensor_copy(znat[:, :, 0:KI], zs[:, :, :]))
                nc.vector.tensor_tensor(znat[:, :, 2 * KI:3 * KI], zs[:, :, :], znat[:, :, 0:KI], ALU.subtract
                                        ).then_inc(s_z, 1)
                dve.wait_ge(s_pe, b * NRING + (OFF_Z + 1))
                nc.vector.tensor_copy(zT[:, :], bank16((OFF_Z - SEC1) % RING)[0:3 * KI, :]).then_inc(s_fr, 1)
                dve.wait_ge(s_u, b * FO + FO)
                nc.vector.tensor_copy(uT[:, :], bank(6)[:, 0:N // 4]).then_inc(s_ut, 1)
                for t in range(NT):
                    dve.wait_ge(s_un, b * NT + (t + 1))
                    nc.vector.tensor_tensor(xb[:, t, :], bank(t % RING)[:, 0:C], xb[:, t, :], ALU.add).then_inc(s_kr, 1)
                    dve.wait_ge(s_kr, b * NT + (t + 1))
                    stats(t)
                layer_stats(2, 1e-6, 1.0, done=True)
                for t in range(0, NT, 2):
                    normalise(t)
                    normalise(t + 1).then_inc(s_xn, 1)
                for t in range(NT):
                    n_, d_ = num[t % 2], den[t % 2]
                    ds = ps[3][:, t % 2, 0:C]
                    dve.wait_ge(s_nc, b * NT + (t + 1))
                    ch.step(nc.vector.tensor_tensor(tot, n_, ds, ALU.add))
                    nc.vector.scalar_tensor_tensor(out=n_, in0=tot, scalar=0.0, in1=n_, op0=ALU.is_equal, op1=ALU.add)
                    if t >= 2:
                        dve.wait_ge(s_bx, b * NT + (t - 1))
                    nc.vector.scalar_tensor_tensor(out=d_, in0=tot, scalar=0.0, in1=ds, op0=ALU.is_equal,
                                                   op1=ALU.add).then_inc(s_cr, 1)
                    dve.wait_ge(s_cr, b * NT + (t + 1))
                    nc.vector.reciprocal(d_, d_).then_inc(s_rc, 1)
                    if t >= 1:
                        dve.wait_ge(s_bx, b * NT + t)
                        stats(t - 1)
                dve.wait_ge(s_bx, b * NT + NT)
                stats(NT - 1)
                layer_stats(3, 1e-5, SX, done=True)
                for t in range(NT):
                    last = normalise(t)
                    if t % 4 == 3:
                        last.then_inc(s_xn, 1)
                lo_transposed(OFF_T3, 1.0)
                dve.wait_ge(s_pe, b * NRING + NRING)
                nc.vector.scalar_tensor_tensor(
                    out=sc[:, :, :], in0=bank((OFF_SC - OFF_T3) % RING)[:, 0:NT * NE].rearrange("p (t e) -> p t e", e=NE),
                    scalar=1.0 / (SX * SW), in1=gbb[:, :].rearrange("p (a e) -> p a e", a=1).to_broadcast([P, NT, NE]),
                    op0=ALU.mult, op1=ALU.add).then_inc(s_fr, 1)
                dve.wait_ge(s_fr, b * NRING + (1 + NRING))

                def rows(v):
                    return v[:, :].rearrange("p (t a) -> p t a", a=1).to_broadcast([P, NT, NE])

                def all_rows(v):
                    return v.rearrange("p (a e) -> p a e", a=1).to_broadcast([P, NT, NE])

                ch.step(nc.vector.tensor_reduce(red[:, :], sc[:, :, :], axis=AX.X, op=ALU.max))
                nc.vector.tensor_tensor(sc[:, :, :], sc[:, :, :], rows(red), ALU.subtract).then_inc(s_gs, 1)
                dve.wait_ge(s_ge, b + 1)
                ch.step(nc.vector.reduce_sum(red[:, :], sc[:, :, :], AX.X))
                ch.step(nc.vector.reciprocal(red[:, :], red[:, :]))
                ch.step(nc.vector.tensor_tensor(prob[:, :, :], sc[:, :, :], rows(red), ALU.mult))
                src = prob
                for k, oh in enumerate((oh1, oh2)):
                    ch.step(nc.vector.tensor_reduce(red[:, :], src[:, :, :], axis=AX.X, op=ALU.max))
                    ch.step(nc.vector.tensor_tensor(oh[:, :, :], src[:, :, :], rows(red), ALU.is_equal))
                    ch.step(nc.vector.tensor_tensor(oh[:, :, :], oh[:, :, :], all_rows(desc[:, 0:NE]), ALU.mult))
                    ch.step(nc.vector.tensor_reduce(red[:, :], oh[:, :, :], axis=AX.X, op=ALU.max))
                    ch.step(nc.vector.tensor_tensor(oh[:, :, :], oh[:, :, :], rows(red), ALU.is_equal))
                    if k == 0:
                        ch.step(nc.vector.scalar_tensor_tensor(out=sc[:, :, :], in0=oh1[:, :, :], scalar=-2.0,
                                                               in1=prob[:, :, :], op0=ALU.mult, op1=ALU.add))
                        src = sc
                nc.vector.tensor_tensor(mask[:, :, :], oh1[:, :, :], oh2[:, :, :], ALU.add).then_inc(s_mk, 1)
                dve.wait_ge(s_mk, b + 1)
                ch.step(nc.vector.tensor_tensor(prob[:, :, :], prob[:, :, :], mask[:, :, :], ALU.mult))
                ch.step(nc.vector.reduce_sum(red[:, :], prob[:, :, :], AX.X))
                ch.step(nc.vector.tensor_scalar(red[:, :], red[:, :], 1e-9, None, ALU.add))
                ch.step(nc.vector.reciprocal(red[:, :], red[:, :]))
                nc.vector.tensor_tensor(gates, prob[:, :, :], rows(red), ALU.mult)
                nc.vector.tensor_copy(rout[:, :, :].bitcast(I32)[:, :, ROW - 1], tok[:, :])
                dve.wait_ge(s_rk, b + 1)
                ch.mark(nc.vector.tensor_scalar(tok[:, :], tok[:, :], float(N), None, ALU.add))
                before, total = [bank(i)[:, 0:NT * NE].rearrange("p (t e) -> p t e", e=NE) for i in (6, 7)]
                ch.step(nc.vector.tensor_copy(cum[0][:, :, :], total))
                ch.step(nc.vector.tensor_tensor(pos[:, :, :], before, cum[0][:, :, :], ALU.subtract))
                old, new = cum
                for d in (1, 2, 4):
                    ch.mark(nc.vector.tensor_tensor(new[:, d:, :], old[:, d:, :], old[:, 0:NT - d, :], ALU.add))
                    ch.step(nc.vector.tensor_copy(new[:, 0:d, :], old[:, 0:d, :]))
                    old, new = new, old
                ch.step(nc.vector.tensor_tensor(pos[:, :, :], pos[:, :, :], old[:, :, :], ALU.add))
                ch.step(nc.vector.tensor_tensor(pos[:, :, :], pos[:, :, :], all_rows(run[:, :]), ALU.add))
                ch.step(nc.vector.tensor_tensor(run[:, :], run[:, :], old[:, NT - 1, :], ALU.add))
                for oh in (oh1, oh2):
                    ch.step(nc.vector.tensor_tensor(oh[:, :, :], oh[:, :, :], pos[:, :, :], ALU.mult))
                ch.step(nc.vector.reduce_sum(red[:, :], oh1[:, :, :], AX.X))
                ch.step(nc.vector.tensor_copy(slots[:, :, 0], red[:, :]))
                ch.step(nc.vector.reduce_sum(red[:, :], oh2[:, :, :], AX.X))
                dve.wait_ge(s_tl, b + 1)
                nc.vector.tensor_copy(slots[:, :, 1], red[:, :]).then_inc(s_rt, 1)
                assert ch.n == NV, ch.n

            ch = Chain(dve, s_gc)
            ch.step(nc.vector.tensor_tensor(tiles[:, :], run[:, :], seg[:, :], ALU.subtract))
            ch.step(nc.vector.tensor_tensor(
                over[:, :, :], tiles[:, :].rearrange("p (e a) -> p e a", a=1).to_broadcast([P, NE, MT]),
                thr[:, :].rearrange("p (a j) -> p a j", a=1).to_broadcast([P, NE, MT]), ALU.is_gt))
            ch.step(nc.vector.reduce_sum(tiles[:, :], over[:, :, :], AX.X))
            ch.step(nc.vector.tensor_scalar(tiles[:, :], tiles[:, :], 1.0, None, ALU.max))
            ch.step(nc.vector.memset(tb[:, :], 0.0))
            for e in range(NE):
                ch.step(nc.vector.tensor_tensor(tb[:, e + 1:e + 2], tb[:, e:e + 1], tiles[:, e:e + 1], ALU.add))
            nc.vector.tensor_copy(runi[:, :], run[:, :])
            nc.vector.tensor_copy(cti[:, :], tiles[:, :])
            nc.vector.tensor_copy(tbi[:, :], tb[:, :]).then_inc(s_tb, 1)

            def read_tile(m):
                dve.wait_ge(s_xt, m + 2)
                for s in range(2):
                    nc.vector.tensor_copy(tT[:, s, :, :].rearrange("p c n -> p (c n)"),
                                          bank16(6 + s)[:, 0:CC * TT]).then_inc(s_xe, 1)

            dve.wait_ge(s_tb, 1)
            read_tile(0)
            with dve.Fori(0, NE // 2) as pair:
                for par in range(2):
                    first = dve.value_load(tbi[0:1, bass.ds(pair * 2 + par, 1)], min_val=0, max_val=NE * MT)
                    end = dve.value_load(tbi[0:1, bass.ds(pair * 2 + (par + 1), 1)], min_val=0, max_val=NE * MT)
                    with dve.Fori(first, end) as i:
                        for q in range(FO // 2):
                            dve.wait_ge(s_hg, i * (FO // 2) + (q + 1))
                            hs = slice(2 * q, 2 * q + 2)
                            nc.vector.tensor_scalar(h16[0][:, hs, :], h32[:, hs, :], SH, None, ALU.mult).then_inc(s_ha, 1)
                            dve.wait_ge(s_ha, i * (FO // 2) + (q + 1))
                            nc.vector.scalar_tensor_tensor(out=h16[1][:, hs, :], in0=h32[:, hs, :], scalar=SH,
                                                           in1=h16[0][:, hs, :], op0=ALU.mult, op1=ALU.subtract
                                                           ).then_inc(s_h2, 1)
                        read_tile(i + 1)
                        dve.wait_ge(s_mt, i * 16 + 16)
                        for s in range(2):
                            n = i * 2 + s
                            dve.wait_ge(s_ys, n + 1)
                            dve.wait_ge(s_yd, n + 1)
                            nc.vector.scalar_tensor_tensor(out=yo[:, s, :], in0=bank(4 + s)[:, 0:C],
                                                           scalar=1.0 / (SH * SW), in1=b2s[par][:, :],
                                                           op0=ALU.mult, op1=ALU.add).then_inc(s_yc, 1)
                            dve.wait_ge(s_yc, n + 1)
                            nc.vector.tensor_scalar(yo[:, s, :], yo[:, s, :],
                                                    meta[:, s, bass.ds(pair * 2 + par, 1)], None,
                                                    ALU.mult).then_inc(s_yo, 1)


_INS = ['x', 'L0_conv_W_qkv', 'L0_conv_W_proj', 'L0_conv_W_gp', 'L0_ffn_c_fc_1', 'L0_ffn_c_fc_2', 'L0_ffn_c_proj_1',
        'L0_ffn_c_proj_2', 'L1_ffn_gate_w', 'L1_ffn_gate_b', 'L1_ffn_w1', 'L1_ffn_b1', 'L1_ffn_w2', 'L1_ffn_b2']


def kernel(**inputs):
    import numpy as _np
    import concourse.bacc as _bacc
    from concourse import mybir as _mybir
    from concourse.bass_utils import run_bass_kernel_spmd as _run

    nc = _bacc.Bacc("TRN2", target_bir_lowering=False, num_devices=1)
    arrays, args = {}, []
    for name in _INS:
        a = _np.ascontiguousarray(inputs[name])
        arrays[f"in_{name}_dram"] = a
        args.append(nc.dram_tensor(f"in_{name}_dram", a.shape, _mybir.dt.from_np(a.dtype), kind="ExternalInput").ap())
    args.append(nc.dram_tensor("out_0_dram", (B, HT, WD, C), F32, kind="ExternalOutput").ap())
    build(nc, *args)
    r = _run(nc, [arrays], core_ids=[0])
    return r.results[0]["out_0_dram"]
```
